# Optimizing a Trainium2 kernel written in Bass

```python
import numpy as np
import jax
import jax.numpy as jnp

def _softmax(x, axis=-1):
    return jax.nn.softmax(x, axis=axis)

def _gelu(x):
    return jax.nn.gelu(x, approximate=True)

def _silu(x):
    return jax.nn.silu(x)

def _sigmoid(x):
    return jax.nn.sigmoid(x)

def _layernorm(x, axis=-1, eps=1e-05):
    m = jnp.mean(x, axis=axis, keepdims=True)
    v = jnp.var(x, axis=axis, keepdims=True)
    return (x - m) / jnp.sqrt(v + eps)

def _scatter_add(tgt, idx, src, axis=0):
    return tgt.at[idx].add(src)

def _segment_sum(src, seg, n):
    return jax.ops.segment_sum(src, seg, n)
kernel_name = 'mk_recurrent_d2_jaxref_r8_86a2d3'

def setup_inputs(seed: int=0):
    np.random.seed(seed)
    _w = jnp.asarray

    def _L0_attn_setup():
        import jax, jax.numpy as jnp
        import numpy as np
        NL, H, N, B, L = (4, 128, 32, 8, 128)

        def _layernorm_channels(z, w, b):
            mu = jnp.mean(z, axis=1, keepdims=True)
            var = jnp.mean((z - mu) ** 2, axis=1, keepdims=True)
            zn = (z - mu) * jax.lax.rsqrt(var + 1e-05)
            return zn * w[None, :, None] + b[None, :, None]

        def _s4d_layer(z, log_dt, A_re_log, A_im, C_re, C_im, D_skip, W, bvec):
            Bz, Hh, Lz = z.shape
            dt = jnp.exp(log_dt)
            A = -jnp.exp(A_re_log) + 1j * A_im
            dtA = A * dt[:, None]
            C = (C_re + 1j * C_im) * (jnp.expm1(dtA) / A)
            l = jnp.arange(Lz, dtype=jnp.float32)
            K = 2.0 * jnp.einsum('hn,hnl->hl', C, jnp.exp(dtA[:, :, None] * l)).real
            kf = jnp.fft.rfft(K, n=2 * Lz)
            uf = jnp.fft.rfft(z, n=2 * Lz)
            y = jnp.fft.irfft(uf * kf, n=2 * Lz)[..., :Lz]
            y = y + z * D_skip[:, None]
            y = jax.nn.gelu(y)
            out = jnp.einsum('oh,bhl->bol', W, y) + bvec[None, :, None]
            return out[:, :Hh] * jax.nn.sigmoid(out[:, Hh:])
        key = jax.random.key(seed)
        ks = jax.random.split(key, 10)
        x = jax.random.normal(ks[0], (B, L, H), dtype=jnp.float32)
        ln_w = jnp.ones((NL, H), jnp.float32)
        ln_b = jnp.zeros((NL, H), jnp.float32)
        log_dt = (jax.random.uniform(ks[1], (NL, H)) * (np.log(0.1) - np.log(0.001)) + np.log(0.001)).astype(jnp.float32)
        A_re_log = jnp.full((NL, H, N), np.log(0.5), jnp.float32)
        A_im = jnp.broadcast_to(np.pi * jnp.arange(N, dtype=jnp.float32), (NL, H, N))
        C_re = jax.random.normal(ks[2], (NL, H, N), jnp.float32) * 0.5 ** 0.5
        C_im = jax.random.normal(ks[3], (NL, H, N), jnp.float32) * 0.5 ** 0.5
        D_skip = jax.random.normal(ks[4], (NL, H), jnp.float32)
        W_out = jax.random.normal(ks[5], (NL, 2 * H, H), jnp.float32) * (1.0 / np.sqrt(H))
        b_out = jnp.zeros((NL, 2 * H), jnp.float32)
        return {'x': x, 'ln_w': ln_w, 'ln_b': ln_b, 'log_dt': log_dt, 'A_re_log': A_re_log, 'A_im': A_im, 'C_re': C_re, 'C_im': C_im, 'D_skip': D_skip, 'W_out': W_out, 'b_out': b_out}
    _L0_attn_in = _L0_attn_setup()

    def _L0_ffn_setup():
        import jax, jax.numpy as jnp
        import numpy as np
        FP8_MAX = 448.0
        key = jax.random.key(seed)
        k_x, k_w, k_b = jax.random.split(key, 3)
        B, S, IN, OUT = (4, 1024, 128, 128)
        x = jax.random.normal(k_x, (B, S, IN), dtype=jnp.float32)
        w_fp32 = jax.random.normal(k_w, (OUT, IN), dtype=jnp.float32)
        weight_fp8 = w_fp32.astype(jnp.float8_e4m3fn).astype(jnp.float32)
        bias = jax.random.normal(k_b, (OUT,), dtype=jnp.float32)
        input_scale = jnp.ones((1,), dtype=jnp.float32)
        weight_scale = jnp.ones((1,), dtype=jnp.float32)
        return {'x': x, 'weight_fp8': weight_fp8, 'bias': bias, 'input_scale': input_scale, 'weight_scale': weight_scale}
    _L0_ffn_in = _L0_ffn_setup()

    def _L1_attn_setup():
        import jax, jax.numpy as jnp
        import numpy as np
        import math
        CTX_LEN = 96
        N_EMBD = 128

        def _depthwise_causal_conv(z, w, T, C):
            return jax.lax.conv_general_dilated(z, w, window_strides=(1,), padding=[(T - 1, 0)], feature_group_count=C, dimension_numbers=('NCH', 'OIH', 'NCH'))
        key = jax.random.key(seed)
        ks = jax.random.split(key, 8)
        B, T, C = (8, CTX_LEN, N_EMBD)
        x = jax.random.normal(ks[0], (B, T, C), dtype=jnp.float32)
        time_decay = jax.random.normal(ks[1], (C, 1), dtype=jnp.float32) * 0.1
        time_first = jnp.full((C, 1), math.log(0.3), dtype=jnp.float32)
        time_mix = jax.random.uniform(ks[2], (1, 1, C), dtype=jnp.float32)
        s = 0.02
        Wk = jax.random.normal(ks[3], (C, C), dtype=jnp.float32) * s
        Wv = jax.random.normal(ks[4], (C, C), dtype=jnp.float32) * s
        Wr = jax.random.normal(ks[5], (C, C), dtype=jnp.float32) * s
        Wo = jax.random.normal(ks[6], (C, C), dtype=jnp.float32) * s
        return {'x': x, 'time_decay': time_decay, 'time_first': time_first, 'time_mix': time_mix, 'Wk': Wk, 'Wv': Wv, 'Wr': Wr, 'Wo': Wo}
    _L1_attn_in = _L1_attn_setup()

    def _L1_ffn_setup():
        import jax, jax.numpy as jnp
        import numpy as np
        B, S, H, F, E = (1, 256, 128, 256, 8)

        def _swiglu(x, wg, wu, wd):
            return jax.nn.silu(x @ wg.T) * (x @ wu.T) @ wd.T
        key = jax.random.key(seed)
        ks = jax.random.split(key, 8)
        sc = 1.0 / np.sqrt(H)
        scf = 1.0 / np.sqrt(F)
        return {'hidden_states': jax.random.normal(ks[0], (B, S, H), jnp.float32), 'gate_w': jax.random.normal(ks[1], (E, H), jnp.float32) * sc, 'shared_gate': jax.random.normal(ks[2], (F, H), jnp.float32) * sc, 'shared_up': jax.random.normal(ks[3], (F, H), jnp.float32) * sc, 'shared_down': jax.random.normal(ks[4], (H, F), jnp.float32) * scf, 'r_gate': jax.random.normal(ks[5], (E, F, H), jnp.float32) * sc, 'r_up': jax.random.normal(ks[6], (E, F, H), jnp.float32) * sc, 'r_down': jax.random.normal(ks[7], (E, H, F), jnp.float32) * scf}
    _L1_ffn_in = _L1_ffn_setup()
    _d = {'L0_attn_x': _L0_attn_in['x'], 'L0_attn_ln_w': _L0_attn_in['ln_w'], 'L0_attn_ln_b': _L0_attn_in['ln_b'], 'L0_attn_log_dt': _L0_attn_in['log_dt'], 'L0_attn_A_re_log': _L0_attn_in['A_re_log'], 'L0_attn_A_im': _L0_attn_in['A_im'], 'L0_attn_C_re': _L0_attn_in['C_re'], 'L0_attn_C_im': _L0_attn_in['C_im'], 'L0_attn_D_skip': _L0_attn_in['D_skip'], 'L0_attn_W_out': _L0_attn_in['W_out'], 'L0_attn_b_out': _L0_attn_in['b_out'], 'L0_ffn_weight_fp8': _L0_ffn_in['weight_fp8'], 'L0_ffn_bias': _L0_ffn_in['bias'], 'L0_ffn_input_scale': _L0_ffn_in['input_scale'], 'L0_ffn_weight_scale': _L0_ffn_in['weight_scale'], 'L1_attn_time_decay': _L1_attn_in['time_decay'], 'L1_attn_time_first': _L1_attn_in['time_first'], 'L1_attn_time_mix': _L1_attn_in['time_mix'], 'L1_attn_Wk': _L1_attn_in['Wk'], 'L1_attn_Wv': _L1_attn_in['Wv'], 'L1_attn_Wr': _L1_attn_in['Wr'], 'L1_attn_Wo': _L1_attn_in['Wo'], 'L1_ffn_gate_w': _L1_ffn_in['gate_w'], 'L1_ffn_shared_gate': _L1_ffn_in['shared_gate'], 'L1_ffn_shared_up': _L1_ffn_in['shared_up'], 'L1_ffn_shared_down': _L1_ffn_in['shared_down'], 'L1_ffn_r_gate': _L1_ffn_in['r_gate'], 'L1_ffn_r_up': _L1_ffn_in['r_up'], 'L1_ffn_r_down': _L1_ffn_in['r_down']}
    _x0 = _d['L0_attn_x']
    _d['L0_attn_x'] = jax.random.normal(jax.random.fold_in(jax.random.key(seed), 1), (8, 512, 128), dtype=_x0.dtype)
    del _x0
    return _d

def reference(L0_attn_x, L0_attn_ln_w, L0_attn_ln_b, L0_attn_log_dt, L0_attn_A_re_log, L0_attn_A_im, L0_attn_C_re, L0_attn_C_im, L0_attn_D_skip, L0_attn_W_out, L0_attn_b_out, L0_ffn_weight_fp8, L0_ffn_bias, L0_ffn_input_scale, L0_ffn_weight_scale, L1_attn_time_decay, L1_attn_time_first, L1_attn_time_mix, L1_attn_Wk, L1_attn_Wv, L1_attn_Wr, L1_attn_Wo, L1_ffn_gate_w, L1_ffn_shared_gate, L1_ffn_shared_up, L1_ffn_shared_down, L1_ffn_r_gate, L1_ffn_r_up, L1_ffn_r_down):

    def _L0_attn_ref(x, ln_w, ln_b, log_dt, A_re_log, A_im, C_re, C_im, D_skip, W_out, b_out):
        import jax, jax.numpy as jnp
        import numpy as np
        NL, H, N, B, L = (4, 128, 32, 8, 128)

        def _layernorm_channels(z, w, b):
            mu = jnp.mean(z, axis=1, keepdims=True)
            var = jnp.mean((z - mu) ** 2, axis=1, keepdims=True)
            zn = (z - mu) * jax.lax.rsqrt(var + 1e-05)
            return zn * w[None, :, None] + b[None, :, None]

        def _s4d_layer(z, log_dt, A_re_log, A_im, C_re, C_im, D_skip, W, bvec):
            Bz, Hh, Lz = z.shape
            dt = jnp.exp(log_dt)
            A = -jnp.exp(A_re_log) + 1j * A_im
            dtA = A * dt[:, None]
            C = (C_re + 1j * C_im) * (jnp.expm1(dtA) / A)
            l = jnp.arange(Lz, dtype=jnp.float32)
            K = 2.0 * jnp.einsum('hn,hnl->hl', C, jnp.exp(dtA[:, :, None] * l)).real
            kf = jnp.fft.rfft(K, n=2 * Lz)
            uf = jnp.fft.rfft(z, n=2 * Lz)
            y = jnp.fft.irfft(uf * kf, n=2 * Lz)[..., :Lz]
            y = y + z * D_skip[:, None]
            y = jax.nn.gelu(y)
            out = jnp.einsum('oh,bhl->bol', W, y) + bvec[None, :, None]
            return out[:, :Hh] * jax.nn.sigmoid(out[:, Hh:])
        h = jnp.transpose(x, (0, 2, 1))
        for i in range(NL):
            z = _layernorm_channels(h, ln_w[i], ln_b[i])
            z = _s4d_layer(z, log_dt[i], A_re_log[i], A_im[i], C_re[i], C_im[i], D_skip[i], W_out[i], b_out[i])
            h = z + h
        return jnp.transpose(h, (0, 2, 1))

    def _L0_ffn_ref(x, weight_fp8, bias, input_scale, weight_scale):
        import jax, jax.numpy as jnp
        import numpy as np
        FP8_MAX = 448.0
        x_q = jnp.clip(x / input_scale, -FP8_MAX, FP8_MAX)
        x_dq = x_q.astype(jnp.float8_e4m3fn).astype(x.dtype) * input_scale
        w_dq = weight_fp8 * weight_scale
        out = jnp.einsum('bsi,oi->bso', x_dq, w_dq) + bias
        return out

    def _L1_attn_ref(x, time_decay, time_first, time_mix, Wk, Wv, Wr, Wo):
        import jax, jax.numpy as jnp
        import numpy as np
        import math
        CTX_LEN = 96
        N_EMBD = 128

        def _depthwise_causal_conv(z, w, T, C):
            return jax.lax.conv_general_dilated(z, w, window_strides=(1,), padding=[(T - 1, 0)], feature_group_count=C, dimension_numbers=('NCH', 'OIH', 'NCH'))
        B, T, C = x.shape
        xs = jnp.pad(x, ((0, 0), (1, 0), (0, 0)))[:, :-1]
        xm = x * time_mix + xs * (1.0 - time_mix)
        k = jnp.einsum('btc,dc->bdt', xm, Wk)
        v = jnp.einsum('btc,dc->bdt', xm, Wv)
        r = jnp.einsum('btc,dc->btd', xm, Wr)
        k = jnp.exp(jnp.minimum(k, 60.0))
        kv = k * v
        time_curve = (jnp.arange(T - 1, dtype=jnp.float32) - (T - 2))[None, :]
        time_w = jnp.concatenate([jnp.exp(time_decay) * time_curve, time_first], axis=-1)
        w = jnp.exp(time_w)[:, None, :]
        wkv = _depthwise_causal_conv(kv, w, T, C)
        wk = _depthwise_causal_conv(k, w, T, C) + 1e-09
        rwkv = jax.nn.sigmoid(r) * jnp.swapaxes(wkv / wk, 1, 2)
        return jnp.einsum('btc,dc->btd', rwkv, Wo)

    def _L1_ffn_ref(hidden_states, gate_w, shared_gate, shared_up, shared_down, r_gate, r_up, r_down):
        import jax, jax.numpy as jnp
        import numpy as np
        B, S, H, F, E = (1, 256, 128, 256, 8)

        def _swiglu(x, wg, wu, wd):
            return jax.nn.silu(x @ wg.T) * (x @ wu.T) @ wd.T
        b, s, h = hidden_states.shape
        x = hidden_states.reshape(-1, h)
        shared_out = _swiglu(x, shared_gate, shared_up, shared_down)
        logits = x @ gate_w.T
        top_id = jnp.argmax(logits, axis=-1)
        score = jax.nn.sigmoid(jnp.max(logits, axis=-1))
        xs = x * score[:, None]

        def body(acc, ws):
            wg, wu, wd, e = ws
            xe = jnp.where((top_id == e)[:, None], xs, 0.0)
            return (acc + _swiglu(xe, wg, wu, wd), None)
        acc0 = jnp.zeros_like(x)
        routed_out, _ = jax.lax.scan(body, acc0, (r_gate, r_up, r_down, jnp.arange(E)))
        return (shared_out + routed_out).reshape(b, s, h)
    x = L0_attn_x
    xn = _layernorm(x, axis=-1)
    s = _L0_attn_ref(xn, L0_attn_ln_w, L0_attn_ln_b, L0_attn_log_dt, L0_attn_A_re_log, L0_attn_A_im, L0_attn_C_re, L0_attn_C_im, L0_attn_D_skip, L0_attn_W_out, L0_attn_b_out)
    g = _silu(_L0_ffn_ref(xn, L0_ffn_weight_fp8, L0_ffn_bias, L0_ffn_input_scale, L0_ffn_weight_scale))
    x = x + s * g
    xn = _layernorm(x, axis=-1)
    s = _L1_attn_ref(xn, L1_attn_time_decay, L1_attn_time_first, L1_attn_time_mix, L1_attn_Wk, L1_attn_Wv, L1_attn_Wr, L1_attn_Wo)
    g = _silu(_L1_ffn_ref(xn, L1_ffn_gate_w, L1_ffn_shared_gate, L1_ffn_shared_up, L1_ffn_shared_down, L1_ffn_r_gate, L1_ffn_r_up, L1_ffn_r_down))
    x = x + s * g
    return x

_drawn_inputs = setup_inputs


def setup_inputs(seed=0):
    import zlib

    import numpy as np

    out = dict(_drawn_inputs(seed))
    spreads = {'L0_attn_ln_w': (1.0, 0.2),
     'L0_attn_ln_b': (0.0, 0.1),
     'L0_attn_A_re_log': (-0.6931471824645996, 0.2),
     'L0_attn_b_out': (0.0, 0.1),
     'L1_attn_time_first': (-1.2039728164672852, 0.6)}
    factors = {'L1_attn_time_decay': 8.0,
     'L1_attn_time_mix': 8.0,
     'L1_attn_Wk': 8.0,
     'L1_attn_Wv': 8.0,
     'L1_attn_Wr': 8.0,
     'L1_attn_Wo': 8.0,
     'L1_ffn_gate_w': 8.0,
     'L1_ffn_shared_gate': 8.0,
     'L1_ffn_shared_up': 8.0,
     'L1_ffn_shared_down': 8.0,
     'L1_ffn_r_gate': 8.0,
     'L1_ffn_r_up': 8.0,
     'L1_ffn_r_down': 8.0}
    for name, (base, spread) in spreads.items():
        noise = np.random.default_rng([zlib.crc32(name.encode()), seed]).standard_normal(out[name].shape)
        drawn = base * np.exp(spread * noise) if base else spread * noise
        out[name] = jnp.asarray(drawn.astype(out[name].dtype))
    for name, factor in factors.items():
        out[name] = (out[name] * factor).astype(out[name].dtype)
    return out
```

```python
from contextlib import ExitStack

import numpy as np

import concourse.bass as bass
from concourse import mybir

P = 128
ARENA = 30528
B, T, H = 8, 512, 128
C = T // P
NL, NM = 4, 32
NSMALL, NBIG = 32, 16
NPOW = NSMALL + NBIG
QH = 16
NQ = H // QH
NK = 3
E, F = 8, 256
NT = 40
FMAX8 = 448.0
EPS = 1e-5
TWO_PI = 6.283185
ROUND = 12582912.0
CW = 4 * NK * P + T + P

ALU = mybir.AluOpType
ACT = mybir.ActivationFunctionType
AX = mybir.AxisListType.X
F32, BF16, I32, U32 = mybir.dt.float32, mybir.dt.bfloat16, mybir.dt.int32, mybir.dt.uint32


def ds(i, n=1):
    return bass.ds(i, n)


def build(nc, d):
    with ExitStack() as ctx:
        def sb(name, shape, dt=F32):
            return ctx.enter_context(nc.sbuf_tensor(name, shape, dt))

        def pb(name, shape):
            return ctx.enter_context(nc.psum_tensor(name, shape, F32))

        def sem(name):
            return ctx.enter_context(nc.semaphore(name))

        const = sb("const", [P, CW])
        ident = sb("ident", [P, P])
        spectra = sb("spectra", [P, NL, C, NK, H])
        ln_bias_response = sb("ln_bias_response", [P, NL, T])
        w_glu = sb("w_glu", [P, NL, 2 * H])
        b_glu = sb("b_glu", [3, NL, 4 * H], BF16)
        b_ffn = sb("b_ffn", [3, 4 * H], BF16)
        ones3 = sb("ones3", [3, P], BF16)
        w8 = sb("w8", [P, H])
        w_attn = sb("w_attn", [P, 4, H])
        w_gate = sb("w_gate", [P, E])
        w_sgu = sb("w_sgu", [P, 2, F])
        w_sd = sb("w_sd", [P, 2, H])
        routed = sb("routed", [P, E * (2 * F + 2 * H)])
        cols = sb("cols", [P, 16])
        arena = sb("arena", [P, ARENA])

        fwd = [const[:, k * P:(k + 1) * P] for k in range(3)]
        ker = const[:, 3 * P:6 * P].rearrange("p (k f) -> p k f", k=NK)
        ker2 = const[:, 6 * P:9 * P].rearrange("p (k f) -> p k f", k=NK)
        inv = const[:, 9 * P:12 * P].rearrange("p (k t) -> p k t", k=NK)
        tri = const[:, 12 * P:12 * P + T]
        strict = const[:, 12 * P + T:12 * P + T + P]

        class Carve:
            def __init__(self, at):
                self.at = at

            def __call__(self, *shape):
                n = int(np.prod(shape))
                v = arena[:, self.at:self.at + n]
                self.at += n
                assert self.at <= ARENA
                if len(shape) == 1:
                    return v
                names = [chr(97 + i) for i in range(len(shape))]
                return v.rearrange(f"p ({' '.join(names)}) -> p {' '.join(names)}",
                                   **dict(zip(names, shape)))

        cut = Carve(0)
        decay = cut(H, NPOW)
        turns = cut(2, QH, NPOW)
        part = cut(2, QH, NPOW)
        apart = cut(2, QH, NPOW)
        sines = cut(2, QH, NPOW)
        cosines = cut(2, QH, NPOW)
        pow_re = cut(2, QH, NPOW)
        pow_im = cut(2, QH, NPOW)
        vt = cut(4, QH, NBIG)
        v_re = cut(2, QH, NBIG)
        v_im = cut(2, QH, NBIG)
        vbd_re = cut(2, QH, NL, NBIG)
        vbd_im = cut(2, QH, NL, NBIG)
        iota = cut(NPOW)
        small = cut(22, H)
        raw = cut(4, H)
        kgen_end = cut.at
        taps = cut(NL, C, H)
        taps_w = cut(NL, C, H)
        ln_w_rows = sb("ln_w_rows", [P, NL, H])
        d_row = ln_bias_response[0:1, 0, :]
        b_glu_raw = routed[0:3, B * T:B * T + NL * 4 * H]

        cut = Carve(0)
        x_in = routed[:, 0:B * T].rearrange("p (b c h) -> p b c h", b=B, c=C)
        x_again = cut(B, C, H)
        h = cut(B, C, H)
        g0 = cut(B, C, H)
        zn = cut(2, C, H)
        acc = cut(2, NK, C * H)
        tmp = cut(NK * H * 6)
        y = cut(2, T)
        th = cut(2, C, H)
        prod = cut(2, C, H)
        q8 = cut(T)
        q8s = cut(T)
        q8r = cut(2, T)
        q8T = cut(2, T)
        th8 = th
        b_ffn_raw = zn[0:3, 0, :, :].rearrange("p c h -> p (c h)")
        bsp = prod[0:3, :, :, :].rearrange("p u c h -> p u (c h)")
        bsp16 = acc[0:3, 0, 0:3, :].bitcast(BF16)
        idle = sb("idle", [P, 4])
        assert cut.at <= kgen_end
        tmps, at = [None], 0
        for dist in range(1, C):
            n = (C - dist) * H
            tmps.append(tmp[:, at:at + NK * n].rearrange("p (k n) -> p k n", k=NK))
            at += NK * n
        stats = sb("stats", [P, 2, C, 6])
        rs = sb("rs", [P, 2, 8, C])
        pconst = sb("pconst", [P, 6, C])

        x1 = x_again
        sa = g0
        fo = h
        xs = spectra[:, :, :, :, :].rearrange("p a b c d -> p (a b c d)")[:, 0:B * T]\
            .rearrange("p (b c h) -> p b c h", b=B, c=C)
        l8_flat = spectra[:, :, :, :, :].rearrange("p a b c d -> p (a b c d)")[:, B * T:B * T + B * C * E]
        l8 = l8_flat.rearrange("p (b c e) -> p b c e", b=B, c=C)
        cut = Carve(3 * B * T)
        sg = cut(T)
        xn1 = cut(2, C, H)
        xT = cut(2, T)
        xm = cut(T)
        kmin = cut(T)
        ek = cut(T)
        kv = cut(T)
        s_num = cut(T + 1)
        s_den = cut(T + 1)
        num = cut(T)
        den = cut(T)
        rw = cut(2, T)
        tr = cut(T)
        tg = cut(T)
        sl = cut(T)
        hs = cut(2, 2, T)
        rt = cut(6, B * C * E)
        cut = Carve(cut.at)
        sil = cut(2, F)
        h_r = cut(2, F)
        xt_r = cut(2, P)
        hT_r = cut(2, 2 * P)
        xtok = cut(2, P)
        ytok = cut(2, P)
        cut3 = Carve(3 * B * T)
        gat = cut3(2, C, H)
        tot = cut3(2, C, H)
        oh16 = sb("oh16", [P, B * C * E], BF16)
        strict16 = sb("strict16", [P, P], BF16)
        ones16 = sb("ones16", [P, P], BF16)
        etab = sb("etab", [P, 6, E])
        mx = sb("mx", [P, B, C])
        emin = sb("emin", [P, B * C])
        sc = sb("sc", [P, 2, 2, C])
        slot_f = sb("slot_f", [P, B * C])
        slot = sb("slot", [P, B * C], U32)
        tile_f = rt[:, 5, :].rearrange("p (t e) -> p t e", e=E)
        tile_n = sb("tile_n", [P, NT])
        tile_e = sb("tile_e", [P, NT], I32)
        iota_e = sb("iota_e", [P, E])
        iota_t = sb("iota_t", [P, NT])
        ones_e = sb("ones_e", [P, E])
        run_mask = sb("run_mask", [P, E, B * C])
        zero_tile = sb("zero_tile", [P, H])
        dcol = sb("dcol", [P, 4])

        zbank = pb("zbank", [P, NK, T])
        glbank = pb("glbank", [P, 2, T])
        ybank = [pb("ybank0", [P, T]), pb("ybank1", [P, T])]
        xbank = pb("xbank", [P, T])

        x_sorted = nc.dram_tensor("x_sorted", [NT * P, H], F32).ap()
        y_sorted = nc.dram_tensor("y_sorted", [NT * P, H], F32).ap()

        modes_in = sem("modes_in")
        const_in = sem("const_in")
        rows_in = sem("rows_in")
        wts_in = sem("wts_in")
        x_in_s = sem("x_in_s")
        exps_ready = sem("exps_ready")
        iota_ready = sem("iota_ready")
        dve_chain = sem("dve_chain")
        pool_chain = sem("pool_chain")
        decay_ready = sem("decay_ready")
        decay_exp = sem("decay_exp")
        small_sin = sem("small_sin")
        coef_ready = sem("coef_ready")
        turns_ready = sem("turns_ready")
        part_ready = sem("part_ready")
        sines_ready = sem("sines_ready")
        pow_ready = sem("pow_ready")
        v_ready = sem("v_ready")
        vbd_re_ready = sem("vbd_re_ready")
        vbd_im_ready = sem("vbd_im_ready")
        taps_psum = sem("taps_psum")
        taps_ready = sem("taps_ready")
        tapsw_ready = sem("tapsw_ready")
        spec_psum = sem("spec_psum")
        spec_ready = sem("spec_ready")
        resp_psum = sem("resp_psum")
        resp_ready = sem("resp_ready")
        kgen_idle = sem("kgen_idle")
        xstats = sem("xstats")
        xrstd = sem("xrstd")
        x_norm = sem("x_norm")
        q8_ready = sem("q8_ready")
        q8_turned = sem("q8_turned")
        q8T_ready = sem("q8T_ready")
        ffn_psum = sem("ffn_psum")
        ffn_tanh = sem("ffn_tanh")
        g0_ready = sem("g0_ready")
        lstats = sem("lstats")
        lrstd = sem("lrstd")
        zn_ready = sem("zn_ready")
        z_ready = sem("z_ready")
        conv_step = sem("conv_step")
        y_psum = sem("y_psum")
        y_ready = sem("y_ready")
        glu_psum = sem("glu_psum")
        glu_tanh = sem("glu_tanh")
        glu_ready = sem("glu_ready")
        h_ready = sem("h_ready")
        zero_ready = sem("zero_ready")
        zeros_out = sem("zeros_out")
        routed_in = sem("routed_in")
        x_again_in = sem("x_again_in")
        out_s = sem("out_s")
        small_w = sem("small_w")
        x1_step = sem("x1_step")
        nstats = sem("nstats")
        nrstd = sem("nrstd")
        xn1_ready = sem("xn1_ready")
        xn1_turned = sem("xn1_turned")
        xT_ready = sem("xT_ready")
        xm_step = sem("xm_step")
        kvr_psum = sem("kvr_psum")
        kmin_ready = sem("kmin_ready")
        ek_ready = sem("ek_ready")
        tr_ready = sem("tr_ready")
        logit_psum = sem("logit_psum")
        logit_step = sem("logit_step")
        mx_tanh = sem("mx_tanh")
        sc_ready = sem("sc_ready")
        xs_ready = sem("xs_ready")
        gu_psum = sem("gu_psum")
        tg_ready = sem("tg_ready")
        ffn_step = sem("ffn_step")
        wkv_step = sem("wkv_step")
        rw_ready = sem("rw_ready")
        attn_psum = sem("attn_psum")
        sa_ready = sem("sa_ready")
        down_psum = sem("down_psum")
        fo_ready = sem("fo_ready")
        w_half = sem("w_half")
        route_step = sem("route_step")
        oh_ready = sem("oh_ready")
        rank_psum = sem("rank_psum")
        slot_ready = sem("slot_ready")
        pool_consts = sem("pool_consts")
        scattered = sem("scattered")
        tiles_in = [sem(f"tiles_in_{u}") for u in range(2)]
        tile_turned = sem("tile_turned")
        tile_copied = sem("tile_copied")
        gur_psum = sem("gur_psum")
        sil_ready = sem("sil_ready")
        hr_ready = sem("hr_ready")
        hr_turned = sem("hr_turned")
        hT_ready = sem("hT_ready")
        y_r_psum = sem("y_r_psum")
        ytok_ready = sem("ytok_ready")
        stored = [sem(f"stored_{u}") for u in range(2)]
        gathered = [sem(f"gathered_{u}") for u in range(2)]
        tot_ready = sem("tot_ready")
        tot_silu = sem("tot_silu")
        final_step = sem("final_step")
        dcols = sem("dcols")

        RSTD = 11
        WKV = 8
        CONV = 7

        block = ctx.enter_context(nc.Block())

        def vbd_copies(eng, e, q, v, vbd, done):
            u = q % 2
            eng.wait_ge(v_ready, 2 * (q + 1))
            if q >= 2:
                eng.wait_ge(taps_psum, q - 1)
            for l in range(NL):
                rows = slice(NM * l, NM * (l + 1))
                if e is nc.scalar:
                    e.copy(vbd[rows, u, :, l, :], v[rows, u, :, :]).then_inc(done, 1)
                else:
                    e.tensor_scalar(vbd[:, u, :, l, :], v[:, u, :, :], cols[:, 11 + l:12 + l], None,
                                    ALU.mult).then_inc(done, 1)

        par = {}

        def k_par(k):
            return par["u"]

        def run_steps(eng, step, rstd0=None):
            if rstd0:
                for n in range(2):
                    rstd0(n)
            for k in range(4):
                par["u"] = k % 2
                step(k, k < 2, False)
            with eng.Fori(2, NL * B // 2 - 1) as i:
                for u in range(2):
                    par["u"] = u
                    step(2 * i + u, False, False)
            for k in range(NL * B - 2, NL * B + 2):
                par["u"] = k % 2
                step(k, False, True)

        def run_batches(eng, batch):
            batch(0, 0, True, False)
            batch(1, 1, True, True)
            with eng.Fori(1, B // 2 - 1) as i:
                for u in range(2):
                    batch(2 * i + u, u, True, True)
            batch(B - 2, 0, True, True)
            batch(B - 1, 1, False, True)

        def run_tiles(eng, step):
            for k in range(6):
                step(k, k % 2)
            with eng.Fori(3, NT // 2) as i:
                for u in range(2):
                    step(2 * i + u, u)
            for k in range(NT, NT + 4):
                step(k, k % 2)

        def live(k, back):
            return not isinstance(k, int) or 0 <= k - back < NT

        def at_least(n, v):
            return not isinstance(n, int) or n >= v

        @block.sync
        def _(sp):
            sp.dma_start(raw, d["modes"]).then_inc(modes_in, 16)
            for l in range(NL):
                sp.dma_start(small[NM * l:NM * (l + 1), 0, :],
                             d["log_dt"][l:l + 1, :].partition_broadcast(NM)).then_inc(modes_in, 16)
            sp.dma_start(const[:, :], d["const"]).then_inc(const_in, 16)
            sp.dma_start(ident[:, :], d["ident"]).then_inc(const_in, 16)
            sp.dma_start(ln_w_rows[:, :, :], d["ln_w"].partition_broadcast(P)).then_inc(rows_in, 16)
            sp.dma_start(d_row, d["d_skip"]).then_inc(rows_in, 16)
            sp.dma_start(cols[:, :], d["cols"]).then_inc(rows_in, 16)
            sp.dma_start(x_in, d["x"]).then_inc(x_in_s, 16)
            sp.dma_start(w_glu[:, :, :], d["w_glu"]).then_inc(wts_in, 16)
            sp.dma_start(b_glu_raw, d["b_glu"].partition_broadcast(3)).then_inc(wts_in, 16)
            sp.dma_start(w8[:, :], d["w8"]).then_inc(wts_in, 16)
            sp.dma_start(w_attn[:, :, :], d["w_attn"]).then_inc(wts_in, 16)
            sp.dma_start(w_gate[:, :], d["w_gate"]).then_inc(wts_in, 16)
            sp.dma_start(w_sgu[:, :, :], d["w_sgu"]).then_inc(wts_in, 16)
            sp.dma_start(w_sd[:, :, :], d["w_sd"]).then_inc(wts_in, 16)
            sp.wait_ge(kgen_idle, 1)
            sp.dma_start(b_ffn_raw, d["b_ffn"].partition_broadcast(3)).then_inc(rows_in, 16)
            sp.dma_start(x_again, d["x"]).then_inc(x_again_in, 16)
            sp.wait_ge(pool_consts, 6)
            sp.dma_start(x_sorted.rearrange("(t p) h -> p t h", p=P),
                         zero_tile[:, :].unsqueeze(1).broadcast_to([P, NT, H])).then_inc(zeros_out, 16)
            sp.wait_ge(g0_ready, B)
            sp.dma_start(routed[:, :], d["w_routed"]).then_inc(routed_in, 16)
            sp.wait_ge(scattered, 16 * B * C)

            def load(i, u, past):
                if past:
                    sp.wait_ge(tile_turned, i - 1)
                sp.dma_start(xtok[:, u, :], x_sorted[ds(i * P, P), :]).then_inc(tiles_in[u], 16)
            for u in range(2):
                load(u, u, False)
            with sp.Fori(1, NT // 2) as i:
                for u in range(2):
                    load(2 * i + u, u, True)
            for b in range(B):
                sp.wait_ge(final_step, 3 * (b + 1))
                sp.dma_start(d["out"][:, b, :, :], x1[:, b, :, :]).then_inc(out_s, 16)
            sp.wait_ge(out_s, 16 * B)

        @block.gpsimd
        def _(pool):
            pool.iota(iota[:, 0:NSMALL], pattern=[[1, NSMALL]], base=0, channel_multiplier=0,
                      allow_small_or_imprecise_dtypes=True).then_inc(iota_ready, 1)
            pool.iota(iota[:, NSMALL:NPOW], pattern=[[1, NBIG]], base=0, channel_multiplier=0,
                      allow_small_or_imprecise_dtypes=True).then_inc(iota_ready, 1)
            for m, value in enumerate((-0.5, H / 4, H * EPS, H ** 0.5, -0.5 * H ** 0.5, 0.5)):
                pool.memset(pconst[:, m, :], value).then_inc(iota_ready, 1)
            pool.memset(vbd_re, 0.0).then_inc(iota_ready, 1)
            pool.memset(zero_tile[:, :], 0.0).then_inc(pool_consts, 1)
            pool.iota(iota_e[:, :], pattern=[[1, E]], base=0, channel_multiplier=0,
                      allow_small_or_imprecise_dtypes=True).then_inc(pool_consts, 1)
            pool.iota(iota_t[:, :], pattern=[[1, NT]], base=0, channel_multiplier=0,
                      allow_small_or_imprecise_dtypes=True).then_inc(pool_consts, 1)
            pool.memset(ones_e[:, :], 1.0).then_inc(pool_consts, 1)
            pool.memset(run_mask[:, :, 1:], 1.0).then_inc(pool_consts, 1)
            pool.memset(run_mask[:, :, 0:1], 0.0).then_inc(pool_consts, 1)
            pool.memset(ones3[:, :], 1.0).then_inc(iota_ready, 1)
            pool.wait_ge(iota_ready, 10)
            pool.wait_ge(decay_ready, 1)
            for j, (lo, n) in enumerate(((0, NSMALL), (NSMALL, NBIG))):
                rate = small[:, 1 + j, :]
                pool.tensor_tensor(decay[:, :, lo:lo + n],
                                   rate.unsqueeze(2).broadcast_to([P, H, n]),
                                   iota[:, lo:lo + n].unsqueeze(1).broadcast_to([P, H, n]),
                                   ALU.mult).then_inc(pool_chain, 1)
            pool.wait_ge(rows_in, 48)
            for q in range(NQ):
                u = q % 2
                if q >= 2:
                    pool.wait_ge(part_ready, 2 * (q - 1))
                for j, (lo, n) in enumerate(((0, NSMALL), (NSMALL, NBIG))):
                    rate = small[:, 3 + j, QH * q:QH * (q + 1)]
                    pool.tensor_tensor(turns[:, u, :, lo:lo + n],
                                       rate.unsqueeze(2).broadcast_to([P, QH, n]),
                                       iota[:, lo:lo + n].unsqueeze(1).broadcast_to([P, QH, n]),
                                       ALU.mult).then_inc(turns_ready, 1)
                if q >= 1:
                    vbd_copies(pool, nc.gpsimd, q - 1, v_im, vbd_im, vbd_im_ready)
            vbd_copies(pool, nc.gpsimd, NQ - 1, v_im, vbd_im, vbd_im_ready)

            def rstd(stat, done, n, u):
                even, odd = stats[:, u, :, 1], stats[:, u, :, 4]
                even2, odd2 = stats[:, u, :, 2], stats[:, u, :, 5]
                r = [rs[:, u, m, :] for m in range(8)]
                w = RSTD * n
                pool.wait_ge(stat, C * (n + 1))
                pool.tensor_tensor(r[2], even, odd, ALU.add).then_inc(done, 1)
                pool.tensor_tensor(r[3], even, odd, ALU.subtract).then_inc(done, 1)
                pool.tensor_tensor(r[4], even2, odd2, ALU.add).then_inc(done, 1)
                pool.wait_ge(done, w + 3)
                pool.tensor_tensor(r[5], r[3], r[3], ALU.mult).then_inc(done, 1)
                pool.wait_ge(done, w + 4)
                pool.tensor_tensor(r[6], r[5], pconst[:, 1, :], ALU.mult).then_inc(done, 1)
                pool.wait_ge(done, w + 5)
                pool.tensor_tensor(r[7], r[6], r[4], ALU.add).then_inc(done, 1)
                pool.wait_ge(done, w + 6)
                pool.tensor_tensor(r[3], r[7], pconst[:, 2, :], ALU.add).then_inc(done, 1)
                pool.wait_ge(done, w + 7)
                pool.tensor_tensor(r[4], r[3], pconst[:, 0, :], ALU.pow).then_inc(done, 1)
                pool.wait_ge(done, w + 8)
                pool.tensor_tensor(r[5], r[4], r[2], ALU.mult).then_inc(done, 1)
                pool.tensor_tensor(r[0], r[4], pconst[:, 3, :], ALU.mult).then_inc(done, 1)
                pool.wait_ge(done, w + 9)
                pool.tensor_tensor(r[1], r[5], pconst[:, 4, :], ALU.mult).then_inc(done, 1)

            with pool.Fori(0, B // 2) as i:
                for u in range(2):
                    rstd(xstats, xrstd, 2 * i + u, u)

            def step(k, first, last):
                if not last:
                    rstd(lstats, lrstd, k + 2, k_par(k))
                if not first:
                    n = k - 2
                    pool.wait_ge(glu_ready, n + 1)
                    hb = h[:, ds(n % B), :, :].squeeze(1) if not isinstance(n, int) else h[:, n % B, :, :]
                    pool.tensor_tensor(hb, hb, prod[:, k_par(k), :, :], ALU.add).then_inc(h_ready, 1)
            run_steps(pool, step, rstd0=lambda n: rstd(lstats, lrstd, n, n % 2))

            rstd(nstats, nrstd, 0, 0)

            def second(n, u, more, past):
                pool.wait_ge(mx_tanh, n + 1)
                pool.tensor_tensor(sc[:, u, 1, :], sc[:, u, 0, :], pconst[:, 5, :], ALU.mult).then_inc(sc_ready, 1)
                pool.wait_ge(sc_ready, 2 * n + 1)
                pool.tensor_tensor(sc[:, u, 1, :], sc[:, u, 1, :], pconst[:, 5, :], ALU.add).then_inc(sc_ready, 1)
                pool.wait_ge(sc_ready, 2 * n + 2)
                pool.tensor_tensor(xs[:, ds(n), :, :].squeeze(1), xn1[:, u, :, :],
                                   sc[:, u, 1, :].unsqueeze(2).broadcast_to([P, C, H]), ALU.mult).then_inc(xs_ready, 1)
                if more:
                    rstd(nstats, nrstd, n + 1, 1 - u)
            run_batches(pool, second)
            pool.wait_ge(slot_ready, 1)
            pool.wait_ge(xs_ready, B)
            pool.wait_ge(zeros_out, 16)
            for b in range(B):
                for c in range(C):
                    j = b * C + c
                    pool.indirect_dma_start(x_sorted, bass.IndirectOffsetOnAxis(ap=slot[:, j:j + 1], axis=0),
                                            xs[:, b, c, :], None).then_inc(scattered, 16)
            for u in range(2):
                pool.wait_ge(stored[u], 16 * NT // 2)
            for b in range(B):
                if b >= 2:
                    pool.wait_ge(tot_ready, b - 1)
                for c in range(C):
                    j = b * C + c
                    pool.indirect_dma_start(gat[:, b % 2, c, :], None, y_sorted,
                                            bass.IndirectOffsetOnAxis(ap=slot[:, j:j + 1], axis=0))\
                        .then_inc(gathered[b % 2], 16)

        @block.scalar
        def _(act):
            act.wait_ge(modes_in, 80)
            act.activation(small[:, 5, :], raw[:, 0, :], ACT.Exp).then_inc(exps_ready, 1)
            act.activation(small[:, 6, :], small[:, 0, :], ACT.Exp).then_inc(exps_ready, 1)
            act.wait_ge(rows_in, 48)
            act.activation(dcol[:, 0:1], cols[:, 5:6], ACT.Exp).then_inc(dcols, 1)
            act.activation(dcol[:, 2:3], cols[:, 6:7], ACT.Exp).then_inc(dcols, 1)
            act.wait_ge(dcols, 1)
            act.activation(dcol[:, 1:2], dcol[:, 0:1], ACT.Exp, scale=-1.0).then_inc(dcols, 1)
            act.wait_ge(decay_ready, 1)
            act.activation(small[:, 7, :], small[:, 1, :], ACT.Exp, scale=-1.0).then_inc(exps_ready, 1)
            act.activation(small[:, 8, :], small[:, 1, :], ACT.Tanh, scale=-0.5).then_inc(exps_ready, 1)
            act.wait_ge(pool_chain, 2)
            act.activation(decay, decay, ACT.Exp, scale=-1.0).then_inc(decay_exp, 1)
            act.activation(small[:, 9, :], small[:, 3, :], ACT.Sin, scale=TWO_PI).then_inc(small_sin, 1)
            act.activation(small[:, 10, :], small[:, 3, :], ACT.Sin, scale=TWO_PI / 2).then_inc(small_sin, 1)

            def evacuate_taps(q):
                u = q % 2
                bank = (zbank if u == 0 else glbank)[0:NSMALL, 0:2, :]\
                    .rearrange("p a (h l d j) -> p (l d) (a h) j", l=NL, d=C, j=C, h=QH // 2)
                act.wait_ge(taps_psum, q + 1)
                for j in range(C):
                    out = taps[NSMALL * j:NSMALL * (j + 1), :, :, QH * q:QH * (q + 1)]\
                        .rearrange("p l d h -> p (l d) h")
                    nc.scalar.copy(out, bank[:, :, :, j]).then_inc(taps_ready, 1)

            act.wait_ge(rows_in, 48)
            for q in range(NQ):
                u = q % 2
                act.wait_ge(part_ready, 2 * (q + 1))
                if q >= 2:
                    act.wait_ge(pow_ready, 2 * (q - 1))
                act.activation(sines[:, u, :, :], part[:, u, :, :], ACT.Sin, scale=TWO_PI).then_inc(sines_ready, 1)
                act.activation(cosines[:, u, :, :], apart[:, u, :, :], ACT.Sin, scale=-TWO_PI,
                               bias=cols[:, 8:9]).then_inc(sines_ready, 1)
                if q >= 1:
                    vbd_copies(act, nc.scalar, q - 1, v_re, vbd_re, vbd_re_ready)
                if q >= 2:
                    evacuate_taps(q - 2)
            vbd_copies(act, nc.scalar, NQ - 1, v_re, vbd_re, vbd_re_ready)
            evacuate_taps(NQ - 2)
            evacuate_taps(NQ - 1)
            for l in range(NL):
                act.wait_ge(spec_psum, l + 1)
                nc.scalar.copy(spectra[:, l, :, :, :].rearrange("p d k h -> p k d h"),
                               zbank[:, :, :].rearrange("p k (d h) -> p k d h", d=C)).then_inc(spec_ready, 1)
                act.wait_ge(resp_psum, l + 1)
                act.activation(ln_bias_response[:, l, :], ybank[1][:, :], ACT.Identity,
                               scale=cols[:, l:l + 1]).then_inc(resp_ready, 1)

            def normalize(out, src, u, done):
                for c in range(C):
                    act.activation(out[:, c, :], src[:, c, :], ACT.Identity, scale=rs[:, u, 0, c:c + 1],
                                   bias=rs[:, u, 1, c:c + 1]).then_inc(done[c == C - 1], 1)

            def x_part(n, u):
                act.wait_ge(xrstd, RSTD * (n + 1))
                normalize(h[:, ds(n), :, :].squeeze(1), x_in[:, ds(n), :, :].squeeze(1), u, (x_norm, h_ready))
                act.wait_ge(q8_turned, n + 1)
                nc.scalar.copy(q8T[:, u, :], ybank[0][:, :]).then_inc(q8T_ready, 1)
                act.wait_ge(ffn_psum, n + 1)
                act.activation(th8[:, u, :, :], xbank[:, :].rearrange("p (c h) -> p c h", c=C), ACT.Tanh,
                               scale=0.5).then_inc(ffn_tanh, 1)
            act.wait_ge(kgen_idle, 1)
            with act.Fori(0, B // 2) as i:
                for u in range(2):
                    x_part(2 * i + u, u)

            def make_zn(n, u):
                act.wait_ge(lrstd, RSTD * (n + 1))
                if not isinstance(n, int) or n >= 2:
                    act.wait_ge(z_ready, n - 1)
                hb = h[:, ds(n % B), :, :].squeeze(1) if not isinstance(n, int) else h[:, n % B, :, :]
                normalize(zn[:, u, :, :], hb, u, (zn_ready, zn_ready))

            make_zn(0, 0)

            def step(k, first, last):
                u = k_par(k)
                if not last or k + 1 < NL * B:
                    make_zn(k + 1, 1 - u)
                if not (isinstance(k, int) and (k < 1 or k > NL * B)):
                    n = k - 1
                    act.wait_ge(y_psum, n + 1)
                    if not (isinstance(n, int) and n < 2):
                        act.wait_ge(glu_psum, n - 1)
                    act.activation(y[:, 1 - u, :], ybank[1 - u][:, :], ACT.Gelu_apprx_tanh).then_inc(y_ready, 1)
                if not first:
                    n = k - 2
                    act.wait_ge(glu_psum, n + 1)
                    if not (isinstance(n, int) and n < 2):
                        act.wait_ge(glu_ready, n - 1)
                    act.activation(th[:, u, :, :],
                                   glbank[:, :, :].rearrange("p a (c o) -> p (a c) o", c=2)[:, :, H:2 * H],
                                   ACT.Tanh, scale=0.5).then_inc(glu_tanh, 1)
            run_steps(act, step)

            def norm_and_turn(n, u, past2):
                act.wait_ge(nrstd, RSTD * (n + 1))
                if past2:
                    act.wait_ge(xs_ready, n - 1)
                normalize(xn1[:, u, :, :], x1[:, ds(n), :, :].squeeze(1), u, (xn1_ready, xn1_ready))
                act.wait_ge(xn1_turned, n + 1)
                nc.scalar.copy(xT[:, u, :], ybank[0][:, :]).then_inc(xT_ready, 1)
            norm_and_turn(0, 0, False)

            def second(n, u, more, past):
                act.wait_ge(kmin_ready, n + 1)
                if past:
                    act.wait_ge(wkv_step, WKV * n)
                act.activation(ek, kmin, ACT.Exp).then_inc(ek_ready, 1)
                if past:
                    act.wait_ge(rw_ready, n)
                act.activation(tr, zbank[:, 2, :], ACT.Tanh, scale=0.5).then_inc(tr_ready, 1)
                act.wait_ge(logit_step, 2 * (n + 1))
                act.activation(sc[:, u, 0, :], mx[:, ds(n), :].squeeze(1), ACT.Tanh, scale=0.5).then_inc(mx_tanh, 1)
                for f in range(2):
                    act.wait_ge(gu_psum, 2 * n + f + 1)
                    if past or f:
                        act.wait_ge(ffn_step, 2 * (2 * n + f))
                    act.activation(tg, glbank[:, 0, :], ACT.Tanh, scale=0.5).then_inc(tg_ready, 1)
                if more:
                    norm_and_turn(n + 1, 1 - u, past)
                act.wait_ge(down_psum, n + 1)
                nc.scalar.copy(fo[:, ds(n), :, :].squeeze(1), xbank[:, :].rearrange("p (c h) -> p c h", c=C))\
                    .then_inc(fo_ready, 1)
                act.wait_ge(attn_psum, n + 1)
                nc.scalar.copy(sa[:, ds(n), :, :].squeeze(1), ybank[1][:, :].rearrange("p (c h) -> p c h", c=C))\
                    .then_inc(sa_ready, 1)
            run_batches(act, second)

            def step(k, u):
                if live(k, 1):
                    n = k - 1
                    act.wait_ge(gur_psum, n + 1)
                    if at_least(n, 2):
                        act.wait_ge(hr_ready, n - 1)
                    act.activation(sil[:, 1 - u, :], glbank[:, 1 - u, 0:F], ACT.Silu).then_inc(sil_ready, 1)
                if live(k, 3):
                    n = k - 3
                    act.wait_ge(y_r_psum, n + 1)
                    if at_least(n, 2):
                        act.wait_ge(stored[1 - u], 16 * (n // 2))
                    nc.scalar.copy(ytok[:, 1 - u, :], (xbank[:, 0:P] if u else zbank[:, 2, 0:P])).then_inc(ytok_ready, 1)
                if live(k, 4):
                    n = k - 4
                    act.wait_ge(ytok_ready, n + 1)
                    act.dma_start(y_sorted[ds(n * P, P), :], ytok[:, u, :]).then_inc(stored[u], 16)
            run_tiles(act, step)
            for b in range(B):
                act.wait_ge(tot_ready, b + 1)
                act.activation(tot[:, b % 2, :, :], tot[:, b % 2, :, :], ACT.Silu).then_inc(tot_silu, 1)

        @block.tensor
        def _(pe):
            pe.wait_ge(const_in, 32)
            for q in range(NQ):
                u = q % 2
                bank = (zbank if u == 0 else glbank)[0:NSMALL, 0:2, :]\
                    .rearrange("p a (h n) -> p (a h) n", n=NL * NBIG)
                pe.wait_ge(pow_ready, 2 * (q + 1))
                pe.wait_ge(vbd_re_ready, NL * (q + 1))
                pe.wait_ge(vbd_im_ready, NL * (q + 1))
                if q >= 2:
                    pe.wait_ge(taps_ready, C * (q - 1))
                for c in range(QH):
                    pe.matmul(bank[:, c, :], pow_re[:, u, c, 0:NSMALL], vbd_re[:, u, c, :, :],
                              start=True, stop=False)
                    mm = pe.matmul(bank[:, c, :], pow_im[:, u, c, 0:NSMALL], vbd_im[:, u, c, :, :],
                                   start=False, stop=True)
                mm.then_inc(taps_psum, 1)
            for l in range(NL):
                pe.wait_ge(tapsw_ready, l + 1)
                if l >= 1:
                    pe.wait_ge(spec_ready, l)
                for k in range(NK):
                    pe.matmul(zbank[:, k, :], ker[:, k, :], taps_w[:, l, :, :], start=True, stop=False)
                    mm = pe.matmul(zbank[:, k, H:T], ker2[:, k, :], taps_w[:, l, 0:C - 1, :],
                                   start=False, stop=True)
                mm.then_inc(spec_psum, 1)
                if l >= 1:
                    pe.wait_ge(resp_ready, l)
                for c in range(C):
                    mm = pe.matmul(ybank[1][:, c * P:T], taps[:, l, c, :], tri[:, 0:T - c * P],
                                   start=(c == 0), stop=(c == C - 1))
                mm.then_inc(resp_psum, 1)

            pe.wait_ge(wts_in, 7 * 16)
            pe.wait_ge(small_w, 2 + NL + 1)

            def x_part(n, u, past):
                pe.wait_ge(q8_ready, 6 * (n + 1))
                if past:
                    pe.wait_ge(q8T_ready, n)
                for c in range(C):
                    mm = pe.transpose(ybank[0][:, c * P:(c + 1) * P], q8r[:, u, c * P:(c + 1) * P], ident[:, :])
                mm.then_inc(q8_turned, 1)
                pe.wait_ge(q8T_ready, n + 1)
                if past:
                    pe.wait_ge(g0_ready, n)
                pe.matmul(xbank[:, :], ones3[:, :], b_ffn[:, :], start=True, stop=False)
                for c in range(C):
                    mm = pe.matmul(xbank[:, c * H:(c + 1) * H], q8T[:, u, c * P:(c + 1) * P], w8[:, :],
                                   start=False, stop=(c == C - 1))
                mm.then_inc(ffn_psum, 1)
            for u in range(2):
                x_part(u, u, u > 0)
            with pe.Fori(1, B // 2) as i:
                for u in range(2):
                    x_part(2 * i + u, u, True)

            def step(k, first, last):
                u = k_par(k)
                if not (isinstance(k, int) and k >= NL * B):
                    pe.wait_ge(zn_ready, C * (k + 1))
                    if not (isinstance(k, int) and k < 1):
                        pe.wait_ge(conv_step, CONV * k - 3)
                    for m in range(NK):
                        mm = pe.matmul(zbank[:, m, :], fwd[m], zn[:, u, :, :], start=True, stop=True)
                    mm.then_inc(z_ready, 1)
                if not (isinstance(k, int) and (k < 1 or k > NL * B)):
                    n = k - 1
                    pe.wait_ge(conv_step, CONV * (n + 1))
                    if not (isinstance(n, int) and n < 2):
                        pe.wait_ge(y_ready, n - 1)
                    resp = ln_bias_response[:, ds(n // B), :].squeeze(1) if not isinstance(n, int) \
                        else ln_bias_response[:, n // B, :]
                    pe.matmul(ybank[1 - u][:, :], ident[:, :], resp, start=True, stop=False)
                    for c in range(C):
                        for m in range(NK):
                            mm = pe.matmul(ybank[1 - u][:, c * P:(c + 1) * P], acc[:, 1 - u, m, c * H:(c + 1) * H],
                                           inv[:, m, :], start=False, stop=(c == C - 1 and m == NK - 1))
                    mm.then_inc(y_psum, 1)
                if not first:
                    n = k - 2
                    pe.wait_ge(y_ready, n + 1)
                    if not (isinstance(n, int) and n < 1):
                        pe.wait_ge(glu_ready, n)
                    dyn = not isinstance(n, int)
                    wg = w_glu[:, ds(n // B), :].squeeze(1) if dyn else w_glu[:, n // B, :]
                    bg = b_glu[:, ds(n // B), :].squeeze(1) if dyn else b_glu[:, n // B, :]
                    for a in range(2):
                        pe.matmul(glbank[:, a, :], ones3[:, :], bg, start=True, stop=False)
                        for c in range(2):
                            mm = pe.matmul(glbank[:, a, c * 2 * H:(c + 1) * 2 * H],
                                           y[:, u, (2 * a + c) * P:(2 * a + c + 1) * P], wg,
                                           start=False, stop=(c == 1))
                    mm.then_inc(glu_psum, 1)
            run_steps(pe, step)

            def turn(n, u, past):
                pe.wait_ge(xn1_ready, C * (n + 1))
                if past:
                    pe.wait_ge(logit_step, 2 * n)
                for c in range(C):
                    mm = pe.transpose(ybank[0][:, c * P:(c + 1) * P], xn1[:, u, c, :], ident[:, :])
                mm.then_inc(xn1_turned, 1)
            turn(0, 0, False)
            pe.wait_ge(w_half, 2)

            def second(n, u, more, past):
                pe.wait_ge(xm_step, 2 * (n + 1))
                if past:
                    pe.wait_ge(wkv_step, WKV * n)
                    pe.wait_ge(tr_ready, n)
                for m in range(3):
                    mm = pe.matmul(zbank[:, m, :], w_attn[:, m, :], xm, start=True, stop=True)
                mm.then_inc(kvr_psum, 1)
                pe.wait_ge(xT_ready, n + 1)
                for c in range(C):
                    mm = pe.matmul(ybank[0][:, c * E:(c + 1) * E], xT[:, u, c * P:(c + 1) * P], w_gate[:, :],
                                   start=True, stop=True)
                mm.then_inc(logit_psum, 1)
                for f in range(2):
                    if past or f:
                        pe.wait_ge(ffn_step, 2 * (2 * n + f))
                    for m in range(2):
                        mm = pe.matmul(glbank[:, m, :], w_sgu[:, m, f * P:(f + 1) * P], xT[:, u, :],
                                       start=True, stop=True)
                    mm.then_inc(gu_psum, 1)
                if more:
                    turn(n + 1, 1 - u, True)
                pe.wait_ge(ffn_step, 2 * (2 * n + 2))
                if past:
                    pe.wait_ge(fo_ready, n)
                for c in range(C):
                    for f in range(2):
                        mm = pe.matmul(xbank[:, c * H:(c + 1) * H], hs[:, u, f, c * P:(c + 1) * P], w_sd[:, f, :],
                                       start=(f == 0), stop=(f == 1))
                mm.then_inc(down_psum, 1)
                pe.wait_ge(rw_ready, n + 1)
                if past:
                    pe.wait_ge(sa_ready, n)
                for c in range(C):
                    mm = pe.matmul(ybank[1][:, c * H:(c + 1) * H], rw[:, u, c * P:(c + 1) * P], w_attn[:, 3, :],
                                   start=True, stop=True)
                mm.then_inc(attn_psum, 1)
            run_batches(pe, second)

            pe.wait_ge(oh_ready, 3)
            pe.wait_ge(xT_ready, B)
            pe.matmul(ybank[0][:, 0:B * C * E], strict16[:, :], oh16[:, :], start=True, stop=True)
            pe.matmul(ybank[0][:, B * C * E:2 * B * C * E], ones16[:, :], oh16[:, :],
                      start=True, stop=True).then_inc(rank_psum, 1)

            pe.wait_ge(slot_ready, 2)
            pe.wait_ge(routed_in, 16)
            pe.wait_ge(fo_ready, B)
            pe.wait_ge(sa_ready, B)

            def step(k, u):
                if live(k, 0):
                    pe.wait_ge(tiles_in[u], 16 * (k // 2 + 1))
                    if at_least(k, 2):
                        pe.wait_ge(tile_copied, k - 1)
                    pe.transpose(zbank[:, u, 0:P], xtok[:, u, :], ident[:, :]).then_inc(tile_turned, 1)
                if live(k, 1):
                    n = k - 1
                    e = pe.value_load(tile_e[0:1, ds(n)], min_val=0, max_val=E - 1)
                    pe.wait_ge(tile_copied, n + 1)
                    if at_least(n, 2):
                        pe.wait_ge(hr_ready, n - 1)
                    pe.matmul(glbank[:, 1 - u, :], xt_r[:, 1 - u, :], routed[:, ds(e * (2 * F), 2 * F)],
                              start=True, stop=True).then_inc(gur_psum, 1)
                if live(k, 2):
                    n = k - 2
                    pe.wait_ge(hr_ready, n + 1)
                    if at_least(n, 2):
                        pe.wait_ge(hT_ready, n - 1)
                    for f in range(2):
                        mm = pe.transpose(ybank[u][:, f * P:(f + 1) * P], h_r[:, u, f * P:(f + 1) * P], ident[:, :])
                    mm.then_inc(hr_turned, 1)
                if live(k, 3):
                    n = k - 3
                    e = pe.value_load(tile_e[0:1, ds(n)], min_val=0, max_val=E - 1)
                    pe.wait_ge(hT_ready, n + 1)
                    if at_least(n, 2):
                        pe.wait_ge(ytok_ready, n - 1)
                    out = xbank[:, 0:P] if u else zbank[:, 2, 0:P]
                    for f in range(2):
                        mm = pe.matmul(out, hT_r[:, 1 - u, f * P:(f + 1) * P],
                                       routed[:, ds(e * (2 * H) + E * 2 * F + f * H, H)], start=(f == 0), stop=(f == 1))
                    mm.then_inc(y_r_psum, 1)
            run_tiles(pe, step)

        @block.vector
        def _(dve):
            links = [0]

            def link(ins):
                links[0] += 1
                ins.then_inc(dve_chain, 1)
                dve.wait_ge(dve_chain, links[0])

            def tt(o, a, b, op):
                link(dve.tensor_tensor(o, a, b, op))

            def ts(o, a, s1, s2, op0, op1=None):
                link(dve.tensor_scalar(o, a, s1, s2, op0) if op1 is None
                     else dve.tensor_scalar(o, a, s1, s2, op0, op1))

            def stt(o, a, s, b, op0, op1):
                link(dve.scalar_tensor_tensor(out=o, in0=a, scalar=s, in1=b, op0=op0, op1=op1))

            S = [small[:, i, :] for i in range(22)]
            alpha, dt, ea, tha, s1, s2 = S[5], S[6], S[7], S[8], S[9], S[10]
            beta, c_re, c_im = raw[:, 1, :], raw[:, 2, :], raw[:, 3, :]
            dve.wait_ge(exps_ready, 2)
            tt(S[1], alpha, dt, ALU.mult)
            tt(S[11], beta, dt, ALU.mult)
            ts(S[11], S[11], float(1 / (2 * np.pi)), None, ALU.mult)
            ts(S[12], S[11], ROUND, -ROUND, ALU.add, ALU.add)
            tt(S[3], S[11], S[12], ALU.subtract)
            ts(S[11], S[3], float(NSMALL), None, ALU.mult)
            ts(S[12], S[11], ROUND, -ROUND, ALU.add, ALU.add)
            tt(S[4], S[11], S[12], ALU.subtract)
            dve.tensor_scalar(S[2], S[1], float(NSMALL), None, ALU.mult).then_inc(decay_ready, 1)
            dve.wait_ge(exps_ready, 4)
            dve.wait_ge(small_sin, 2)
            stt(S[13], ea, 1.0, tha, ALU.add, ALU.mult)
            tt(S[14], s2, s2, ALU.mult)
            ts(S[15], S[14], -2.0, 1.0, ALU.mult, ALU.add)
            tt(S[13], S[13], S[15], ALU.mult)
            stt(S[13], S[14], -2.0, S[13], ALU.mult, ALU.add)
            tt(S[14], ea, s1, ALU.mult)
            tt(S[15], alpha, alpha, ALU.mult)
            tt(S[16], beta, beta, ALU.mult)
            tt(S[15], S[15], S[16], ALU.add)
            link(dve.reciprocal(S[15], S[15]))
            tt(S[16], S[14], beta, ALU.mult)
            tt(S[17], S[13], alpha, ALU.mult)
            tt(S[16], S[16], S[17], ALU.subtract)
            tt(S[16], S[16], S[15], ALU.mult)
            tt(S[17], S[13], beta, ALU.mult)
            tt(S[18], S[14], alpha, ALU.mult)
            tt(S[17], S[17], S[18], ALU.add)
            tt(S[17], S[17], S[15], ALU.mult)
            tt(S[18], c_re, S[16], ALU.mult)
            tt(S[19], c_im, S[17], ALU.mult)
            tt(S[18], S[18], S[19], ALU.add)
            tt(S[19], c_im, S[16], ALU.mult)
            tt(S[20], c_re, S[17], ALU.mult)
            tt(S[19], S[19], S[20], ALU.subtract)
            cr, ci, ncr, nci = S[13], S[14], S[15], S[16]
            ts(cr, S[18], 2.0, None, ALU.mult)
            ts(ncr, S[18], -2.0, None, ALU.mult)
            ts(ci, S[19], 2.0, None, ALU.mult)
            ts(nci, S[19], -2.0, None, ALU.mult)
            dve.wait_ge(decay_exp, 1)

            for q in range(NQ):
                u = q % 2
                dve.wait_ge(turns_ready, 2 * (q + 1))
                if q >= 2:
                    dve.wait_ge(sines_ready, 2 * (q - 1))
                ts(apart[:, u, :, :], turns[:, u, :, :], ROUND, -ROUND, ALU.add, ALU.add)
                dve.tensor_tensor(part[:, u, :, :], turns[:, u, :, :], apart[:, u, :, :], ALU.subtract).then_inc(part_ready, 1)
                dve.wait_ge(part_ready, 2 * q + 1)
                dve.tensor_scalar(apart[:, u, :, :].bitcast(I32), part[:, u, :, :].bitcast(I32), 0x7FFFFFFF, None,
                                  ALU.bitwise_and).then_inc(part_ready, 1)
                dve.wait_ge(sines_ready, 2 * (q + 1))
                if q >= 2:
                    dve.wait_ge(taps_psum, q - 1)
                dq = decay[:, QH * q:QH * (q + 1), :]
                dve.tensor_tensor(pow_re[:, u, :, :], dq, cosines[:, u, :, :], ALU.mult).then_inc(pow_ready, 1)
                dve.tensor_tensor(pow_im[:, u, :, :], dq, sines[:, u, :, :], ALU.mult).then_inc(pow_ready, 1)
                dve.wait_ge(pow_ready, 2 * (q + 1))

                def coef(x):
                    return x[:, QH * q:QH * (q + 1)].unsqueeze(2).broadcast_to([P, QH, NBIG])
                big_re, big_im = pow_re[:, u, :, NSMALL:NPOW], pow_im[:, u, :, NSMALL:NPOW]
                tt(vt[:, 0, :, :], big_re, coef(cr), ALU.mult)
                tt(vt[:, 1, :, :], big_im, coef(ci), ALU.mult)
                tt(vt[:, 2, :, :], big_re, coef(nci), ALU.mult)
                tt(vt[:, 3, :, :], big_im, coef(ncr), ALU.mult)
                if q >= 2:
                    dve.wait_ge(vbd_re_ready, NL * (q - 1))
                    dve.wait_ge(vbd_im_ready, NL * (q - 1))
                dve.tensor_tensor(v_re[:, u, :, :], vt[:, 0, :, :], vt[:, 1, :, :], ALU.subtract).then_inc(v_ready, 1)
                dve.tensor_tensor(v_im[:, u, :, :], vt[:, 2, :, :], vt[:, 3, :, :], ALU.add).then_inc(v_ready, 1)
            dve.wait_ge(rows_in, 48)
            dve.wait_ge(taps_ready, C * NQ)
            tt(taps[0:1, :, 0, :], taps[0:1, :, 0, :], d_row.rearrange("p (l h) -> p l h", l=NL), ALU.add)
            for l in range(NL):
                dve.tensor_tensor(taps_w[:, l, :, :], taps[:, l, :, :],
                                  ln_w_rows[:, l, :].unsqueeze(1).broadcast_to([P, C, H]),
                                  ALU.mult).then_inc(tapsw_ready, 1)
            dve.wait_ge(spec_ready, NL)
            dve.wait_ge(resp_ready, NL)
            dve.memset(idle[:, 0:1], 0.0).then_inc(kgen_idle, 1)
            dve.wait_ge(wts_in, 7 * 16)
            bg = b_glu_raw.rearrange("p (l a o) -> p (l a) o", l=NL, a=2)
            dve.tensor_scalar(w_glu[:, :, 0:H], w_glu[:, :, 0:H], 0.5, None, ALU.mult).then_inc(small_w, 1)
            ts(bg[:, :, 0:H], bg[:, :, 0:H], 0.5, None, ALU.mult)
            dve.tensor_scalar(w8[:, :], w8[:, :], cols[:, 10:11], cols[:, 9:10], ALU.mult, ALU.mult).then_inc(small_w, 1)
            link(dve.reciprocal(idle[:, 2:3], cols[:, 9:10]))

            def in_three(out, src):
                w = [bsp[:, i, :] for i in range(2)]
                w16 = [bsp16[:, i, 0:4 * H] for i in range(3)]
                link(dve.tensor_copy(w16[0], src))
                tt(w[0], src, w16[0], ALU.subtract)
                link(dve.tensor_copy(w16[1], w[0]))
                tt(w[1], w[0], w16[1], ALU.subtract)
                link(dve.tensor_copy(w16[2], w[1]))
                ts(w[0], w16[0], ident[0:3, 0:1], None, ALU.mult)
                stt(w[1], w16[1], ident[0:3, 1:2], w[0], ALU.mult, ALU.add)
                dve.scalar_tensor_tensor(out=out, in0=w16[2], scalar=ident[0:3, 2:3], in1=w[1],
                                         op0=ALU.mult, op1=ALU.add).then_inc(small_w, 1)
                dve.wait_ge(small_w, 3 + weights[0])
                weights[0] += 1
            weights = [0]
            for l in range(NL):
                in_three(b_glu[:, l, :], b_glu_raw[:, l * 4 * H:(l + 1) * 4 * H])
            dve.wait_ge(rows_in, 64)
            in_three(b_ffn[:, :], b_ffn_raw)

            def norm_stats(src, u, done):
                for c in range(C):
                    dve.bn_stats(stats[:, u, c, :], src[:, c, :]).then_inc(done, 1)

            def quantize(n, u):
                w = 6 * n
                dve.wait_ge(x_norm, (C - 1) * (n + 1))
                dve.wait_ge(h_ready, n + 1)
                xn = h[:, ds(n), :, :].squeeze(1).rearrange("p c h -> p (c h)")
                dve.tensor_scalar(q8, xn, idle[:, 2:3], FMAX8, ALU.mult, ALU.min).then_inc(q8_ready, 1)
                dve.wait_ge(q8_ready, w + 1)
                dve.tensor_scalar(q8, q8, -FMAX8, None, ALU.max).then_inc(q8_ready, 1)
                dve.wait_ge(q8_ready, w + 2)
                dve.tensor_scalar(q8s.bitcast(I32), q8.bitcast(I32), 0x7F800000, None,
                                  ALU.bitwise_and).then_inc(q8_ready, 1)
                dve.wait_ge(q8_ready, w + 3)
                dve.tensor_scalar(q8s, q8s, 2.0 ** -6, 1.5 * 2.0 ** 20, ALU.max, ALU.mult).then_inc(q8_ready, 1)
                dve.wait_ge(q8_ready, w + 4)
                dve.tensor_tensor(q8, q8, q8s, ALU.add).then_inc(q8_ready, 1)
                dve.wait_ge(q8_ready, w + 5)
                dve.tensor_tensor(q8r[:, u, :], q8, q8s, ALU.subtract).then_inc(q8_ready, 1)

            def gate0(n, u):
                dve.wait_ge(ffn_tanh, n + 1)
                dve.scalar_tensor_tensor(out=g0[:, ds(n), :, :].squeeze(1), in0=th8[:, u, :, :], scalar=1.0,
                                         in1=xbank[:, :].rearrange("p (c h) -> p c h", c=C),
                                         op0=ALU.add, op1=ALU.mult).then_inc(g0_ready, 1)
            dve.wait_ge(x_in_s, 16)
            with dve.Fori(0, B // 2) as i:
                for u in range(2):
                    n = 2 * i + u
                    norm_stats(x_in[:, ds(n), :, :].squeeze(1), u, xstats)
                    quantize(n, u)
                    gate0(n, u)

            def layer_stats(n, u):
                if not isinstance(n, int) or n >= 2:
                    dve.wait_ge(zn_ready, C * (n - 1))
                dve.wait_ge(h_ready, n + 1)
                hb = h[:, ds(n % B), :, :].squeeze(1) if not isinstance(n, int) else h[:, n % B, :, :]
                norm_stats(hb, u, lstats)

            layer_stats(0, 0)
            layer_stats(1, 1)

            def step(k, first, last):
                u = k_par(k)
                dyn = not isinstance(k, int)
                if dyn or k < NL * B:
                    w = CONV * k
                    dve.wait_ge(z_ready, k + 1)
                    if dyn or k >= 2:
                        dve.wait_ge(y_psum, k - 1)
                    if dyn or k >= 1:
                        dve.wait_ge(conv_step, w)
                    for dist in range(C):
                        n = C - dist
                        sp_d = spectra[:, ds(k // B), dist, :, :].squeeze(1) if dyn else spectra[:, k // B, dist, :, :]
                        dst = acc[:, u, :, :] if dist == 0 else tmps[dist]
                        dve.tensor_tensor(dst.rearrange("p k (c h) -> p k c h", c=n),
                                          zbank[:, :, 0:n * H].rearrange("p k (c h) -> p k c h", c=n),
                                          sp_d.unsqueeze(2).broadcast_to([P, NK, n, H]),
                                          ALU.mult).then_inc(conv_step, 1)
                    for dist in range(1, C):
                        dve.wait_ge(conv_step, w + C + dist - 1)
                        a = acc[:, u, :, dist * H:]
                        dve.tensor_tensor(a, a, tmps[dist], ALU.add).then_inc(conv_step, 1)
                if not first:
                    n = k - 2
                    dve.wait_ge(glu_tanh, n + 1)
                    if not (isinstance(n, int) and n < 2):
                        dve.wait_ge(h_ready, B + n - 1)
                    dve.scalar_tensor_tensor(
                        out=prod[:, u, :, :], in0=th[:, u, :, :], scalar=1.0,
                        in1=glbank[:, :, :].rearrange("p a (c o) -> p (a c) o", c=2)[:, :, 0:H],
                        op0=ALU.add, op1=ALU.mult).then_inc(glu_ready, 1)
                if not last:
                    layer_stats(k + 2, u)
            run_steps(dve, step)

            dve.tensor_scalar(w_attn[:, 3, :], w_attn[:, 3, :], 0.5, None, ALU.mult).then_inc(w_half, 1)
            dve.tensor_scalar(w_sd[:, :, :], w_sd[:, :, :], 0.5, None, ALU.mult).then_inc(w_half, 1)
            ts(dcol[:, 3:4], cols[:, 4:5], -1.0, 1.0, ALU.mult, ALU.add)
            dve.wait_ge(h_ready, B + NL * B)
            dve.wait_ge(x_again_in, 16)
            dve.wait_ge(dcols, 3)
            link(dve.memset(s_num[:, 0:1], 0.0))
            link(dve.memset(s_den[:, 0:1], 0.0))

            def first_residual(n, u):
                if at_least(n, 1):
                    dve.wait_ge(x1_step, 2 * n)
                dve.tensor_tensor(sg.rearrange("p (c h) -> p c h", c=C), h[:, ds(n), :, :].squeeze(1),
                                  g0[:, ds(n), :, :].squeeze(1), ALU.mult).then_inc(x1_step, 1)
                dve.wait_ge(x1_step, 2 * n + 1)
                xb = x1[:, ds(n), :, :].squeeze(1)
                dve.scalar_tensor_tensor(out=xb, in0=sg.rearrange("p (c h) -> p c h", c=C), scalar=0.5, in1=xb,
                                         op0=ALU.mult, op1=ALU.add).then_inc(x1_step, 1)
                return xb
            x1_first = first_residual(0, 0)
            dve.wait_ge(x1_step, 2)
            norm_stats(x1_first, 0, nstats)

            def second(n, u, more, past):
                dve.wait_ge(xT_ready, n + 1)
                if past:
                    dve.wait_ge(kvr_psum, n)
                dve.tensor_scalar(xm, xT[:, u, :], cols[:, 4:5], None, ALU.mult).then_inc(xm_step, 1)
                dve.wait_ge(xm_step, 2 * n + 1)
                dve.scalar_tensor_tensor(out=xm[:, 1:T], in0=xT[:, u, 0:T - 1], scalar=dcol[:, 3:4],
                                         in1=xm[:, 1:T], op0=ALU.mult, op1=ALU.add).then_inc(xm_step, 1)
                dve.wait_ge(kvr_psum, n + 1)
                if past:
                    dve.wait_ge(ek_ready, n)
                dve.tensor_scalar(kmin, zbank[:, 0, :], 60.0, None, ALU.min).then_inc(kmin_ready, 1)
                dve.wait_ge(logit_psum, n + 1)
                l8n = l8[:, ds(n), :, :].squeeze(1)
                dve.tensor_copy(l8n, ybank[0][:, 0:C * E].rearrange("p (c e) -> p c e", c=C)).then_inc(logit_step, 1)
                dve.wait_ge(logit_step, 2 * n + 1)
                dve.tensor_reduce(mx[:, ds(n), :].squeeze(1), l8n, AX, ALU.max).then_inc(logit_step, 1)

                def shared(f):
                    dve.wait_ge(tg_ready, 2 * n + f + 1)
                    dve.scalar_tensor_tensor(out=sl, in0=tg, scalar=1.0, in1=glbank[:, 0, :], op0=ALU.add,
                                             op1=ALU.mult).then_inc(ffn_step, 1)
                    dve.wait_ge(ffn_step, 2 * (2 * n + f) + 1)
                    dve.tensor_tensor(hs[:, u, f, :], sl, glbank[:, 1, :], ALU.mult).then_inc(ffn_step, 1)
                shared(0)
                w = WKV * n
                dve.wait_ge(ek_ready, n + 1)
                dve.tensor_tensor(kv, ek, zbank[:, 1, :], ALU.mult).then_inc(wkv_step, 1)
                step_decay = dcol[:, 1:2].broadcast_to([P, T])
                dve.tensor_tensor_scan(s_den[:, 1:T + 1], step_decay, ek, 0.0, ALU.mult, ALU.add).then_inc(wkv_step, 1)
                dve.wait_ge(wkv_step, w + 1)
                dve.tensor_tensor_scan(s_num[:, 1:T + 1], step_decay, kv, 0.0, ALU.mult, ALU.add).then_inc(wkv_step, 1)
                dve.wait_ge(wkv_step, w + 2)
                dve.scalar_tensor_tensor(out=den, in0=ek, scalar=dcol[:, 2:3], in1=s_den[:, 0:T], op0=ALU.mult,
                                         op1=ALU.add).then_inc(wkv_step, 1)
                dve.wait_ge(wkv_step, w + 3)
                dve.scalar_tensor_tensor(out=num, in0=kv, scalar=dcol[:, 2:3], in1=s_num[:, 0:T], op0=ALU.mult,
                                         op1=ALU.add).then_inc(wkv_step, 1)
                dve.wait_ge(wkv_step, w + 4)
                dve.tensor_scalar(den, den, 1e-9, None, ALU.add).then_inc(wkv_step, 1)
                dve.wait_ge(wkv_step, w + 6)
                dve.reciprocal(den, den).then_inc(wkv_step, 1)
                dve.wait_ge(wkv_step, w + 7)
                dve.tensor_tensor(num, num, den, ALU.mult).then_inc(wkv_step, 1)
                dve.wait_ge(wkv_step, w + 8)
                dve.wait_ge(tr_ready, n + 1)
                dve.scalar_tensor_tensor(out=rw[:, u, :], in0=tr, scalar=1.0, in1=num, op0=ALU.add,
                                         op1=ALU.mult).then_inc(rw_ready, 1)
                if more:
                    x1_next = first_residual(n + 1, 1 - u)
                shared(1)
                if more:
                    norm_stats(x1_next, 1 - u, nstats)
            run_batches(dve, second)

            NJ = B * C

            def je(x):
                return x.rearrange("p (j e) -> p j e", e=E)

            def ej(x):
                return x.rearrange("p (e j) -> p e j", e=E)
            l8j = je(l8_flat)
            mxj = mx[:, :, :].rearrange("p b c -> p (b c)").unsqueeze(2).broadcast_to([P, NJ, E])
            dve.wait_ge(logit_step, 2 * B)
            dve.wait_ge(pool_consts, 6)
            tt(je(rt[:, 0, :]), l8j, mxj, ALU.is_ge)
            stt(je(rt[:, 1, :]), je(rt[:, 0, :]), -float(E), iota_e[:, :].unsqueeze(1).broadcast_to([P, NJ, E]),
                ALU.mult, ALU.add)
            link(dve.tensor_reduce(emin[:, :], je(rt[:, 1, :]), AX, ALU.min))
            oh = rt[:, 0, :]
            tt(je(oh), je(rt[:, 1, :]), emin[:, :].unsqueeze(2).broadcast_to([P, NJ, E]), ALU.is_equal)
            dve.tensor_copy(oh16[:, :], oh).then_inc(oh_ready, 1)
            dve.tensor_copy(strict16[:, :], strict).then_inc(oh_ready, 1)
            dve.memset(ones16[:, :], 1.0).then_inc(oh_ready, 1)
            dve.wait_ge(rank_psum, 1)
            total, until = rt[:, 1, :], rt[:, 2, :]
            link(dve.tensor_copy(ej(total), je(ybank[0][:, NJ * E:2 * NJ * E]).rearrange("p j e -> p e j")))
            link(dve.tensor_tensor_scan(until, run_mask[:, :, :].rearrange("p e j -> p (e j)"), total, 0.0,
                                        ALU.mult, ALU.add))
            tiles, ends, start = etab[:, 0, :], etab[:, 1, :], etab[:, 2, :]
            ts(tiles, ej(until)[:, :, NJ - 1], 1.0 / P, 127.0 / P - 0.498, ALU.mult, ALU.add)
            ts(tiles, tiles, ROUND, -ROUND, ALU.add, ALU.add)
            link(dve.tensor_tensor_scan(ends, ones_e[:, :], tiles, 0.0, ALU.mult, ALU.add))
            tt(start, ends, tiles, ALU.subtract)
            ts(start, start, float(P), None, ALU.mult)
            before = rt[:, 3, :]
            tt(before, until, total, ALU.subtract)
            tt(ej(before), ej(before), start.unsqueeze(2).broadcast_to([P, E, NJ]), ALU.add)
            tt(je(total), ej(before).rearrange("p e j -> p j e"), je(ybank[0][:, 0:NJ * E]), ALU.add)
            tt(je(total), je(total), je(oh), ALU.mult)
            link(dve.tensor_reduce(slot_f[:, :], je(total), AX, ALU.add))
            dve.tensor_copy(slot[:, :], slot_f[:, :]).then_inc(slot_ready, 1)
            for lo, hi in ((0, NT // 2), (NT // 2, NT)):
                tf = tile_f[:, 0:hi - lo, :]
                tt(tf, iota_t[:, lo:hi].unsqueeze(2).broadcast_to([P, hi - lo, E]),
                   ends.unsqueeze(1).broadcast_to([P, hi - lo, E]), ALU.is_ge)
                link(dve.tensor_reduce(tile_n[:, lo:hi], tf, AX, ALU.add))
            ts(tile_n[:, :], tile_n[:, :], float(E - 1), None, ALU.min)
            dve.tensor_copy(tile_e[:, :], tile_n[:, :]).then_inc(slot_ready, 1)

            def step(k, u):
                if live(k, 0):
                    dve.wait_ge(tile_turned, k + 1)
                    if at_least(k, 2):
                        dve.wait_ge(gur_psum, k - 1)
                    dve.tensor_copy(xt_r[:, u, :], zbank[:, u, 0:P]).then_inc(tile_copied, 1)
                if live(k, 1):
                    n = k - 1
                    dve.wait_ge(sil_ready, n + 1)
                    if at_least(n, 2):
                        dve.wait_ge(hr_turned, n - 1)
                    dve.tensor_tensor(h_r[:, 1 - u, :], sil[:, 1 - u, :], glbank[:, 1 - u, F:2 * F],
                                      ALU.mult).then_inc(hr_ready, 1)
                if live(k, 2):
                    n = k - 2
                    dve.wait_ge(hr_turned, n + 1)
                    if at_least(n, 2):
                        dve.wait_ge(y_r_psum, n - 1)
                    dve.tensor_copy(hT_r[:, u, :], ybank[u][:, 0:2 * P]).then_inc(hT_ready, 1)
            run_tiles(dve, step)

            for b in range(B):
                dve.wait_ge(gathered[b % 2], 16 * C * (b // 2 + 1))
                dve.tensor_tensor(tot[:, b % 2, :, :], gat[:, b % 2, :, :], fo[:, b, :, :], ALU.add).then_inc(tot_ready, 1)
                dve.wait_ge(tot_silu, b + 1)
                t = tot[:, b % 2, :, :]
                dve.tensor_tensor(t, t, sa[:, b, :, :], ALU.mult).then_inc(final_step, 1)
                dve.wait_ge(final_step, 3 * b + 1)
                dve.tensor_tensor(x1[:, b, :, :], x1[:, b, :, :], t, ALU.add).then_inc(final_step, 2)



def constants():
    t = np.arange(P)[:, None]
    w = 2 * np.pi * (np.arange(P)[None, :] + 0.5) / (2 * P)

    def comps(a, b, kinds):
        return [kinds[0](a, b), kinds[1](a, b), kinds[2](a, b)]
    out = []
    a, b = np.cos(w * t), -np.sin(w * t)
    out += [a + b, a, b]
    out += [a, b - a, a + b]
    a, b = np.cos(w * (t - P)), -np.sin(w * (t - P))
    out += [a, b - a, a + b]
    c, s = np.cos(w * t).T / P, np.sin(w * t).T / P
    out += [c - s, -s, -c]
    tri = np.ones((P, T))
    tri[:, :P] = np.arange(P)[None, :] >= t
    return np.concatenate(out + [tri, (np.arange(P)[None, :] > t)], axis=1).astype(np.float32)


def laid_out(x):
    f = np.ascontiguousarray

    def modes(name):
        return x[name].transpose(0, 2, 1).reshape(NL * NM, H)
    col = lambda a: np.broadcast_to(a.reshape(-1, 1), (P, 1))
    half_pi = np.full((P, 1), np.pi / 2, np.float32)
    zero = np.zeros((P, 1), np.float32)
    return {
        "modes": f(np.stack([modes("L0_attn_A_re_log"), modes("L0_attn_A_im"), modes("L0_attn_C_re"),
                             modes("L0_attn_C_im")], axis=1)),
        "log_dt": f(x["L0_attn_log_dt"]),
        "const": constants(),
        "ident": np.eye(P, dtype=np.float32),
        "ln_w": f(x["L0_attn_ln_w"]),
        "d_skip": f(x["L0_attn_D_skip"].reshape(1, NL * H)),
        "cols": f(np.concatenate([x["L0_attn_ln_b"].T, x["L1_attn_time_mix"].reshape(P, 1),
                                  x["L1_attn_time_decay"], x["L1_attn_time_first"], zero, half_pi,
                                  col(x["L0_ffn_input_scale"]), col(x["L0_ffn_weight_scale"])]
                                 + [np.kron(np.eye(NL), np.ones((NM, 1))).astype(np.float32), zero], axis=1)),
        "x": f(x["L0_attn_x"].reshape(B, C, P, H).transpose(2, 0, 1, 3)),
        "w_glu": f(x["L0_attn_W_out"].transpose(2, 0, 1)),
        "b_glu": f(np.repeat(x["L0_attn_b_out"][:, None, :], 2, axis=1).reshape(NL * 4 * H)),
        "w8": f(x["L0_ffn_weight_fp8"].T),
        "b_ffn": f(np.tile(x["L0_ffn_bias"], 4)),
        "w_attn": f(np.stack([x[f"L1_attn_W{c}"].T for c in "kvro"], axis=1)),
        "w_gate": f(x["L1_ffn_gate_w"].T),
        "w_sgu": f(np.stack([x["L1_ffn_shared_gate"].T, x["L1_ffn_shared_up"].T], axis=1)),
        "w_sd": f(x["L1_ffn_shared_down"].T.reshape(2, P, H).transpose(1, 0, 2)),
        "w_routed": f(np.concatenate([
            np.stack([x["L1_ffn_r_gate"], x["L1_ffn_r_up"]], 1).transpose(3, 0, 1, 2).reshape(P, -1),
            x["L1_ffn_r_down"].transpose(0, 2, 1).reshape(E, 2, P, H).transpose(2, 0, 1, 3).reshape(P, -1)],
            axis=1)),
    }


def kernel(**inputs):
    import concourse.bacc as bacc
    from concourse.bass_utils import run_bass_kernel_spmd

    nc = bacc.Bacc("TRN2", target_bir_lowering=False, num_devices=1)
    arrays = laid_out({k: np.asarray(v) for k, v in inputs.items()})
    d = {k: nc.dram_tensor(f"in_{k}", a.shape, F32, kind="ExternalInput").ap() for k, a in arrays.items()}
    d["out"] = nc.dram_tensor("out", (P, B, C, H), F32, kind="ExternalOutput").ap()
    build(nc, d)
    r = run_bass_kernel_spmd(nc, [{f"in_{k}": a for k, a in arrays.items()}], core_ids=[0])
    return np.ascontiguousarray(r.results[0]["out"].transpose(1, 2, 0, 3)).reshape(B, T, H)
```

```python
from contextlib import ExitStack

import numpy as np

import concourse.bass as bass
from concourse import mybir

P = 128
ARENA = 30656
B, T, H = 8, 512, 128
C = T // P
NL, NM = 4, 32
NSMALL, NBIG = 32, 16
NPOW = NSMALL + NBIG
QH = 16
NQ = H // QH
NK = 3
E, F = 8, 256
NT = 40
FMAX8 = 448.0
EPS = 1e-5
TWO_PI = 6.283185
LN2_HI = 0.693145751953125
LN2_LO = float(np.log(2) - 0.693145751953125)
ROUND = 12582912.0
CW = 4 * NK * P + T + P

ALU = mybir.AluOpType
ACT = mybir.ActivationFunctionType
AX = mybir.AxisListType.X
F32, BF16, I32, U32 = mybir.dt.float32, mybir.dt.bfloat16, mybir.dt.int32, mybir.dt.uint32


def ds(i, n=1):
    return bass.ds(i, n)


def build(nc, d):
    with ExitStack() as ctx:
        def sb(name, shape, dt=F32):
            return ctx.enter_context(nc.sbuf_tensor(name, shape, dt))

        def pb(name, shape):
            return ctx.enter_context(nc.psum_tensor(name, shape, F32))

        def sem(name):
            return ctx.enter_context(nc.semaphore(name))

        const = sb("const", [P, CW])
        ident = sb("ident", [P, P])
        spectra = sb("spectra", [P, NL, C, NK, H])
        ln_bias_response = sb("ln_bias_response", [P, NL, T])
        w_glu = sb("w_glu", [P, NL, 2 * H])
        biases = sb("biases", [3, NL * 2 * H + H], BF16)
        b_glu = biases[:, 0:NL * 2 * H].rearrange("p (l o) -> p l o", l=NL)
        b_ffn = biases[:, NL * 2 * H:]
        ones3 = sb("ones3", [3, P], BF16)
        w8 = sb("w8", [P, H])
        w_attn = sb("w_attn", [P, 4, H])
        w_gate = sb("w_gate", [P, E])
        w_sgu = sb("w_sgu", [P, 2, F])
        w_sd = sb("w_sd", [P, 2, H])
        routed = sb("routed", [P, E * (2 * F + 2 * H)])
        cols = sb("cols", [P, 16])
        arena = sb("arena", [P, ARENA])

        fwd = [const[:, k * P:(k + 1) * P] for k in range(3)]
        ker = const[:, 3 * P:6 * P].rearrange("p (k f) -> p k f", k=NK)
        ker2 = const[:, 6 * P:9 * P].rearrange("p (k f) -> p k f", k=NK)
        inv = const[:, 9 * P:12 * P].rearrange("p (k t) -> p k t", k=NK)
        tri = const[:, 12 * P:12 * P + T]
        strict = const[:, 12 * P + T:12 * P + T + P]

        class Carve:
            def __init__(self, at):
                self.at = at

            def __call__(self, *shape):
                n = int(np.prod(shape))
                v = arena[:, self.at:self.at + n]
                self.at += n
                assert self.at <= ARENA
                if len(shape) == 1:
                    return v
                names = [chr(97 + i) for i in range(len(shape))]
                return v.rearrange(f"p ({' '.join(names)}) -> p {' '.join(names)}",
                                   **dict(zip(names, shape)))

        cut = Carve(0)
        decay = cut(H, NPOW)
        turns = cut(2, QH, NPOW)
        part = cut(2, QH, NPOW)
        apart = cut(2, QH, NPOW)
        sines = cut(2, QH, NPOW)
        cosines = cut(2, QH, NPOW)
        pow_re = cut(2, QH, NPOW)
        pow_im = cut(2, QH, NPOW)
        vt = cut(4, QH, NBIG)
        v_re = cut(2, QH, NBIG)
        v_im = cut(2, QH, NBIG)
        vbd_re = cut(2, QH, NL, NBIG)
        vbd_im = cut(2, QH, NL, NBIG)
        iota = cut(NPOW)
        small = cut(22, H)
        raw = cut(5, H)
        kgen_end = cut.at
        taps = cut(NL, C, H)
        taps_w = cut(NL, C, H)
        ln_w_rows = sb("ln_w_rows", [P, NL, H])
        d_row = ln_bias_response[0:1, 0, :]
        NBIAS = NL * 2 * H + H
        biases_raw = routed[0:3, B * T:B * T + NBIAS]
        spectra_flat = spectra[:, :, :, :, :].rearrange("p a b c d -> p (a b c d)")
        bsp = spectra_flat[0:3, 0:2 * NBIAS].rearrange("p (u n) -> p u n", u=2)
        bsp16 = spectra_flat[0:3, 2 * NBIAS:4 * NBIAS].bitcast(BF16).rearrange("p (u n) -> p u n", u=4)

        cut = Carve(0)
        x_in = routed[:, 0:B * T].rearrange("p (b c h) -> p b c h", b=B, c=C)
        x_again = cut(B, C, H)
        h = cut(B, C, H)
        g0 = cut(B, C, H)
        zn = cut(2, C, H)
        acc = cut(2, NK, C * H)
        tmp = cut(NK * H * 6)
        y = cut(2, T)
        th = cut(2, C, H)
        prod = cut(2, C, H)
        q8_at = cut.at
        q8 = cut(T)
        q8s = cut(T)
        q8r = cut(2, T)
        q8T = cut(2, T)
        th8 = th
        idle = sb("idle", [P, 4])
        assert cut.at <= kgen_end
        tmps, at = [None], 0
        for dist in range(1, C):
            n = (C - dist) * H
            tmps.append(tmp[:, at:at + NK * n].rearrange("p (k n) -> p k n", k=NK))
            at += NK * n
        stats = sb("stats", [P, 2, C, 6])
        rs = sb("rs", [P, 2, 8, C])
        pconst = sb("pconst", [P, 6, C])

        x1 = x_again
        sa = g0
        fo = h
        xs = spectra[:, :, :, :, :].rearrange("p a b c d -> p (a b c d)")[:, 0:B * T]\
            .rearrange("p (b c h) -> p b c h", b=B, c=C)
        l8_flat = spectra[:, :, :, :, :].rearrange("p a b c d -> p (a b c d)")[:, B * T:B * T + B * C * E]
        l8 = l8_flat.rearrange("p (b c e) -> p b c e", b=B, c=C)
        cut = Carve(q8_at)
        sg = cut(T)
        xn1 = cut(2, C, H)
        xT = cut(2, T)
        xm = cut(T)
        moe_at = cut.at
        cut = Carve(3 * B * T)
        kmin = cut(T)
        ek = cut(T)
        kv = cut(T)
        s_num = cut(T + 1)
        s_den = cut(T + 1)
        num = cut(T)
        den = cut(T)
        ratio = cut(T)
        rw = cut(2, T)
        tr = cut(T)
        tg = cut(T)
        sl = cut(T)
        hs = cut(2, 2, T)
        assert cut.at <= q8_at
        rt = Carve(3 * B * T)(6, B * C * E)
        cut = Carve(moe_at)
        sil = cut(2, F)
        h_r = cut(2, F)
        xt_r = cut(2, P)
        hT_r = cut(2, 2 * P)
        xtok = cut(2, P)
        ytok = cut(2, P)
        cut3 = Carve(3 * B * T)
        gat = cut3(2, C, H)
        tot = cut3(2, C, H)
        oh16 = sb("oh16", [P, B * C * E], BF16)
        strict16 = sb("strict16", [P, P], BF16)
        ones16 = sb("ones16", [P, P], BF16)
        etab = sb("etab", [P, 6, E])
        mx = sb("mx", [P, B, C])
        emin = sb("emin", [P, B * C])
        sc = sb("sc", [P, 2, 2, C])
        slot_f = sb("slot_f", [P, B * C])
        slot = sb("slot", [P, B * C], U32)
        tile_f = rt[:, 5, :].rearrange("p (t e) -> p t e", e=E)
        tile_n = sb("tile_n", [P, NT])
        tile_e = sb("tile_e", [P, NT], I32)
        iota_e = sb("iota_e", [P, E])
        iota_t = sb("iota_t", [P, NT])
        ones_e = sb("ones_e", [P, E])
        run_mask = sb("run_mask", [P, E, B * C])
        zero_tile = sb("zero_tile", [P, H])
        dcol = sb("dcol", [P, 4])

        zbank = pb("zbank", [P, NK, T])
        glbank = pb("glbank", [P, 2, T])
        ybank = [pb("ybank0", [P, T]), pb("ybank1", [P, T])]
        xbank = pb("xbank", [P, T])

        x_sorted = nc.dram_tensor("x_sorted", [NT * P, H], F32).ap()
        y_sorted = nc.dram_tensor("y_sorted", [NT * P, H], F32).ap()

        modes_in = sem("modes_in")
        const_in = sem("const_in")
        rows_in = sem("rows_in")
        wts_in = sem("wts_in")
        x_in_s = sem("x_in_s")
        exps_ready = sem("exps_ready")
        iota_ready = sem("iota_ready")
        dve_chain = sem("dve_chain")
        pool_chain = sem("pool_chain")
        decay_ready = sem("decay_ready")
        decay_exp = sem("decay_exp")
        small_sin = sem("small_sin")
        coef_ready = sem("coef_ready")
        turns_ready = sem("turns_ready")
        part_ready = sem("part_ready")
        sines_ready = sem("sines_ready")
        pow_ready = sem("pow_ready")
        v_ready = sem("v_ready")
        vbd_re_ready = sem("vbd_re_ready")
        vbd_im_ready = sem("vbd_im_ready")
        taps_psum = sem("taps_psum")
        taps_ready = sem("taps_ready")
        tapsw_ready = sem("tapsw_ready")
        spec_psum = sem("spec_psum")
        spec_ready = sem("spec_ready")
        resp_psum = sem("resp_psum")
        resp_ready = sem("resp_ready")
        kgen_idle = sem("kgen_idle")
        xstats = sem("xstats")
        xrstd = sem("xrstd")
        x_norm = sem("x_norm")
        q8_ready = sem("q8_ready")
        q8_turned = sem("q8_turned")
        q8T_ready = sem("q8T_ready")
        ffn_psum = sem("ffn_psum")
        ffn_tanh = sem("ffn_tanh")
        g0_ready = sem("g0_ready")
        lstats = sem("lstats")
        lrstd = sem("lrstd")
        zn_ready = sem("zn_ready")
        z_ready = sem("z_ready")
        conv_step = sem("conv_step")
        y_psum = sem("y_psum")
        y_ready = sem("y_ready")
        glu_psum = sem("glu_psum")
        glu_tanh = sem("glu_tanh")
        glu_ready = sem("glu_ready")
        h_ready = sem("h_ready")
        zero_ready = sem("zero_ready")
        zeros_out = sem("zeros_out")
        routed_in = sem("routed_in")
        x_again_in = sem("x_again_in")
        out_s = sem("out_s")
        small_w = sem("small_w")
        x1_step = sem("x1_step")
        nstats = sem("nstats")
        nrstd = sem("nrstd")
        xn1_ready = sem("xn1_ready")
        xn1_turned = sem("xn1_turned")
        xT_ready = sem("xT_ready")
        xm_step = sem("xm_step")
        kvr_psum = sem("kvr_psum")
        kmin_ready = sem("kmin_ready")
        ek_ready = sem("ek_ready")
        tr_ready = sem("tr_ready")
        logit_psum = sem("logit_psum")
        logit_step = sem("logit_step")
        mx_tanh = sem("mx_tanh")
        sc_ready = sem("sc_ready")
        xs_ready = sem("xs_ready")
        gu_psum = sem("gu_psum")
        tg_ready = sem("tg_ready")
        ffn_step = sem("ffn_step")
        wkv_step = sem("wkv_step")
        ratio_ready = sem("ratio_ready")
        rw_ready = sem("rw_ready")
        attn_psum = sem("attn_psum")
        sa_ready = sem("sa_ready")
        down_psum = sem("down_psum")
        fo_ready = sem("fo_ready")
        w_half = sem("w_half")
        route_step = sem("route_step")
        oh_ready = sem("oh_ready")
        rank_psum = sem("rank_psum")
        slot_ready = sem("slot_ready")
        pool_consts = sem("pool_consts")
        scattered = sem("scattered")
        tiles_in = [sem(f"tiles_in_{u}") for u in range(2)]
        tile_turned = sem("tile_turned")
        tile_copied = sem("tile_copied")
        gur_psum = sem("gur_psum")
        sil_ready = sem("sil_ready")
        hr_ready = sem("hr_ready")
        hr_turned = sem("hr_turned")
        hT_ready = sem("hT_ready")
        y_r_psum = sem("y_r_psum")
        ytok_ready = sem("ytok_ready")
        stored = [sem(f"stored_{u}") for u in range(2)]
        gathered = [sem(f"gathered_{u}") for u in range(2)]
        tot_ready = sem("tot_ready")
        tot_silu = sem("tot_silu")
        final_step = sem("final_step")
        dcols = sem("dcols")

        RSTD = 11
        WKV = 7
        CONV = 7

        block = ctx.enter_context(nc.Block())

        def vbd_copies(eng, e, q, v, vbd, done):
            u = q % 2
            eng.wait_ge(v_ready, 2 * (q + 1))
            if q >= 2:
                eng.wait_ge(taps_psum, q - 1)
            for l in range(NL):
                rows = slice(NM * l, NM * (l + 1))
                if e is nc.scalar:
                    e.copy(vbd[rows, u, :, l, :], v[rows, u, :, :]).then_inc(done, 1)
                else:
                    e.tensor_scalar(vbd[:, u, :, l, :], v[:, u, :, :], cols[:, 11 + l:12 + l], None,
                                    ALU.mult).then_inc(done, 1)

        par = {}

        def k_par(k):
            return par["u"]

        def run_steps(eng, step, rstd0=None):
            if rstd0:
                for n in range(2):
                    rstd0(n)
            for k in range(4):
                par["u"] = k % 2
                step(k, k < 2, False)
            with eng.Fori(2, NL * B // 2 - 1) as i:
                for u in range(2):
                    par["u"] = u
                    step(2 * i + u, False, False)
            for k in range(NL * B - 2, NL * B + 2):
                par["u"] = k % 2
                step(k, False, True)

        def run_batches(eng, batch):
            batch(0, 0)
            batch(1, 1)
            with eng.Fori(1, B // 2 - 1) as i:
                for u in range(2):
                    batch(2 * i + u, u)
            batch(B - 2, 0)
            batch(B - 1, 1)

        def follows(n, ahead):
            return not isinstance(n, int) or n + ahead < B

        def run_tiles(eng, step):
            for k in range(6):
                step(k, k % 2)
            with eng.Fori(3, NT // 2) as i:
                for u in range(2):
                    step(2 * i + u, u)
            for k in range(NT, NT + 4):
                step(k, k % 2)

        def live(k, back):
            return not isinstance(k, int) or 0 <= k - back < NT

        def at_least(n, v):
            return not isinstance(n, int) or n >= v

        @block.sync
        def _(sp):
            sp.dma_start(raw[:, 1:5, :], d["modes"]).then_inc(modes_in, 16)
            for l in range(NL):
                sp.dma_start(raw[NM * l:NM * (l + 1), 0, :],
                             d["log_dt"][l:l + 1, :].partition_broadcast(NM)).then_inc(modes_in, 16)
            sp.dma_start(const[:, :], d["const"]).then_inc(const_in, 16)
            sp.dma_start(ident[:, :], d["ident"]).then_inc(const_in, 16)
            sp.dma_start(ln_w_rows[:, :, :], d["ln_w"].partition_broadcast(P)).then_inc(rows_in, 16)
            sp.dma_start(d_row, d["d_skip"]).then_inc(rows_in, 16)
            sp.dma_start(cols[:, :], d["cols"]).then_inc(rows_in, 16)
            sp.dma_start(x_in, d["x"]).then_inc(x_in_s, 16)
            sp.dma_start(w_glu[:, :, :], d["w_glu"]).then_inc(wts_in, 16)
            sp.dma_start(biases_raw, d["biases"].partition_broadcast(3)).then_inc(wts_in, 16)
            sp.dma_start(w8[:, :], d["w8"]).then_inc(wts_in, 16)
            sp.dma_start(w_attn[:, :, :], d["w_attn"]).then_inc(wts_in, 16)
            sp.dma_start(w_gate[:, :], d["w_gate"]).then_inc(wts_in, 16)
            sp.dma_start(w_sgu[:, :, :], d["w_sgu"]).then_inc(wts_in, 16)
            sp.dma_start(w_sd[:, :, :], d["w_sd"]).then_inc(wts_in, 16)
            sp.wait_ge(kgen_idle, 1)
            sp.dma_start(x_again, d["x"]).then_inc(x_again_in, 16)
            sp.wait_ge(pool_consts, 6)
            sp.dma_start(x_sorted.rearrange("(t p) h -> p t h", p=P),
                         zero_tile[:, :].unsqueeze(1).broadcast_to([P, NT, H])).then_inc(zeros_out, 16)
            sp.wait_ge(g0_ready, B)
            sp.dma_start(routed[:, :], d["w_routed"]).then_inc(routed_in, 16)
            sp.wait_ge(scattered, 16 * B * C)

            def load(i, u, past):
                if past:
                    sp.wait_ge(tile_turned, i - 1)
                sp.dma_start(xtok[:, u, :], x_sorted[ds(i * P, P), :]).then_inc(tiles_in[u], 16)
            for u in range(2):
                load(u, u, False)
            with sp.Fori(1, NT // 2) as i:
                for u in range(2):
                    load(2 * i + u, u, True)
            for b in range(B):
                sp.wait_ge(final_step, 3 * (b + 1))
                sp.dma_start(d["out"][:, b, :, :], x1[:, b, :, :]).then_inc(out_s, 16)
            sp.wait_ge(out_s, 16 * B)

        @block.gpsimd
        def _(pool):
            pool.iota(iota[:, 0:NSMALL], pattern=[[1, NSMALL]], base=0, channel_multiplier=0,
                      allow_small_or_imprecise_dtypes=True).then_inc(iota_ready, 1)
            pool.iota(iota[:, NSMALL:NPOW], pattern=[[1, NBIG]], base=0, channel_multiplier=0,
                      allow_small_or_imprecise_dtypes=True).then_inc(iota_ready, 1)
            for m, value in enumerate((-0.5, H / 4, H * EPS, H ** 0.5, -0.5 * H ** 0.5, 0.5)):
                pool.memset(pconst[:, m, :], value).then_inc(iota_ready, 1)
            pool.memset(vbd_re, 0.0).then_inc(iota_ready, 1)
            pool.memset(zero_tile[:, :], 0.0).then_inc(pool_consts, 1)
            pool.iota(iota_e[:, :], pattern=[[1, E]], base=0, channel_multiplier=0,
                      allow_small_or_imprecise_dtypes=True).then_inc(pool_consts, 1)
            pool.iota(iota_t[:, :], pattern=[[1, NT]], base=0, channel_multiplier=0,
                      allow_small_or_imprecise_dtypes=True).then_inc(pool_consts, 1)
            pool.memset(ones_e[:, :], 1.0).then_inc(pool_consts, 1)
            pool.memset(run_mask[:, :, 1:], 1.0).then_inc(pool_consts, 1)
            pool.memset(run_mask[:, :, 0:1], 0.0).then_inc(pool_consts, 1)
            pool.memset(ones3[:, :], 1.0).then_inc(iota_ready, 1)
            pool.wait_ge(iota_ready, 10)
            pool.wait_ge(decay_ready, 1)
            for half in range(2):
                cs = slice(half * H // 2, (half + 1) * H // 2)
                for j, (lo, n) in enumerate(((0, NSMALL), (NSMALL, NBIG))):
                    pool.tensor_tensor(decay[:, cs, lo:lo + n],
                                       small[:, 1 + j, cs].unsqueeze(2).broadcast_to([P, H // 2, n]),
                                       iota[:, lo:lo + n].unsqueeze(1).broadcast_to([P, H // 2, n]),
                                       ALU.mult).then_inc(pool_chain, 1)

            def turns_of(q):
                u = q % 2
                if q >= 2:
                    pool.wait_ge(part_ready, 2 * (q - 1))
                for j, (lo, n) in enumerate(((0, NSMALL), (NSMALL, NBIG))):
                    rate = small[:, 3 + j, QH * q:QH * (q + 1)]
                    pool.tensor_tensor(turns[:, u, :, lo:lo + n],
                                       rate.unsqueeze(2).broadcast_to([P, QH, n]),
                                       iota[:, lo:lo + n].unsqueeze(1).broadcast_to([P, QH, n]),
                                       ALU.mult).then_inc(turns_ready, 1)
            turns_of(0)
            turns_of(1)
            pool.wait_ge(rows_in, 48)
            for q in range(NQ):
                if q + 2 < NQ:
                    turns_of(q + 2)
                vbd_copies(pool, nc.gpsimd, q, v_im, vbd_im, vbd_im_ready)

            def rstd(stat, done, n, u):
                even, odd = stats[:, u, :, 1], stats[:, u, :, 4]
                even2, odd2 = stats[:, u, :, 2], stats[:, u, :, 5]
                r = [rs[:, u, m, :] for m in range(8)]
                w = RSTD * n
                pool.wait_ge(stat, C * (n + 1))
                pool.tensor_tensor(r[2], even, odd, ALU.add).then_inc(done, 1)
                pool.tensor_tensor(r[3], even, odd, ALU.subtract).then_inc(done, 1)
                pool.tensor_tensor(r[4], even2, odd2, ALU.add).then_inc(done, 1)
                pool.wait_ge(done, w + 3)
                pool.tensor_tensor(r[5], r[3], r[3], ALU.mult).then_inc(done, 1)
                pool.wait_ge(done, w + 4)
                pool.tensor_tensor(r[6], r[5], pconst[:, 1, :], ALU.mult).then_inc(done, 1)
                pool.wait_ge(done, w + 5)
                pool.tensor_tensor(r[7], r[6], r[4], ALU.add).then_inc(done, 1)
                pool.wait_ge(done, w + 6)
                pool.tensor_tensor(r[3], r[7], pconst[:, 2, :], ALU.add).then_inc(done, 1)
                pool.wait_ge(done, w + 7)
                pool.tensor_tensor(r[4], r[3], pconst[:, 0, :], ALU.pow).then_inc(done, 1)
                pool.wait_ge(done, w + 8)
                pool.tensor_tensor(r[5], r[4], r[2], ALU.mult).then_inc(done, 1)
                pool.tensor_tensor(r[0], r[4], pconst[:, 3, :], ALU.mult).then_inc(done, 1)
                pool.wait_ge(done, w + 9)
                pool.tensor_tensor(r[1], r[5], pconst[:, 4, :], ALU.mult).then_inc(done, 1)

            with pool.Fori(0, B // 2) as i:
                for u in range(2):
                    rstd(xstats, xrstd, 2 * i + u, u)

            def first_residual(n):
                pool.wait_ge(h_ready, B + (NL - 1) * B + n + 1)
                if at_least(n, 1):
                    pool.wait_ge(x1_step, 2 * n)
                else:
                    pool.wait_ge(x_again_in, 16)
                hb, gb, xb = (t[:, n, :, :] if isinstance(n, int) else t[:, ds(n), :, :].squeeze(1) for t in (h, g0, x1))
                sgc = sg.rearrange("p (c h) -> p c h", c=C)
                pool.tensor_tensor(sgc, hb, gb, ALU.mult).then_inc(x1_step, 1)
                pool.wait_ge(x1_step, 2 * n + 1)
                pool.tensor_tensor(xb, xb, sgc, ALU.add).then_inc(x1_step, 1)

            def step(k, first, last):
                if not last:
                    rstd(lstats, lrstd, k + 2, k_par(k))
                if not first:
                    n = k - 2
                    pool.wait_ge(glu_ready, n + 1)
                    hb = h[:, ds(n % B), :, :].squeeze(1) if not isinstance(n, int) else h[:, n % B, :, :]
                    pool.tensor_tensor(hb, hb, prod[:, k_par(k), :, :], ALU.add).then_inc(h_ready, 1)
                if last and k < NL * B:
                    first_residual(k - (NL * B - 2))
                if last and 0 <= k - (NL * B - 1) < 2:
                    rstd(nstats, nrstd, k - (NL * B - 1), (k - (NL * B - 1)) % 2)
            run_steps(pool, step, rstd0=lambda n: rstd(lstats, lrstd, n, n % 2))


            def scaled(n, u):
                pool.wait_ge(mx_tanh, n + 1)
                pool.tensor_tensor(sc[:, u, 1, :], sc[:, u, 0, :], pconst[:, 5, :], ALU.mult).then_inc(sc_ready, 1)
                pool.wait_ge(sc_ready, 2 * n + 1)
                pool.tensor_tensor(sc[:, u, 1, :], sc[:, u, 1, :], pconst[:, 5, :], ALU.add).then_inc(sc_ready, 1)
                pool.wait_ge(sc_ready, 2 * n + 2)
                pool.tensor_tensor(xs[:, ds(n), :, :].squeeze(1), xn1[:, u, :, :],
                                   sc[:, u, 1, :].unsqueeze(2).broadcast_to([P, C, H]), ALU.mult).then_inc(xs_ready, 1)
            scaled(0, 0)

            def second(n, u):
                if follows(n, 2):
                    first_residual(n + 2)
                    rstd(nstats, nrstd, n + 2, u)
                if follows(n, 1):
                    scaled(n + 1, 1 - u)
                pool.wait_ge(wkv_step, WKV * (n + 1))
                pool.tensor_tensor(ratio, num, den, ALU.mult).then_inc(ratio_ready, 1)
            run_batches(pool, second)
            pool.wait_ge(slot_ready, 1)
            pool.wait_ge(xs_ready, B)
            pool.wait_ge(zeros_out, 16)
            for b in range(B):
                for c in range(C):
                    j = b * C + c
                    pool.indirect_dma_start(x_sorted, bass.IndirectOffsetOnAxis(ap=slot[:, j:j + 1], axis=0),
                                            xs[:, b, c, :], None).then_inc(scattered, 16)
            for u in range(2):
                pool.wait_ge(stored[u], 16 * NT // 2)
            for b in range(B):
                if b >= 2:
                    pool.wait_ge(tot_ready, b - 1)
                for c in range(C):
                    j = b * C + c
                    pool.indirect_dma_start(gat[:, b % 2, c, :], None, y_sorted,
                                            bass.IndirectOffsetOnAxis(ap=slot[:, j:j + 1], axis=0))\
                        .then_inc(gathered[b % 2], 16)

        @block.scalar
        def _(act):
            act.wait_ge(rows_in, 48)
            act.activation(dcol[:, 0:1], cols[:, 5:6], ACT.Exp).then_inc(dcols, 1)
            act.activation(dcol[:, 2:3], cols[:, 6:7], ACT.Exp).then_inc(dcols, 1)
            act.wait_ge(dcols, 1)
            act.activation(dcol[:, 1:2], dcol[:, 0:1], ACT.Exp, scale=-1.0).then_inc(dcols, 1)
            act.wait_ge(decay_ready, 1)
            act.activation(small[:, 9, :], small[:, 3, :], ACT.Sin, scale=TWO_PI).then_inc(small_sin, 1)
            act.activation(small[:, 10, :], small[:, 3, :], ACT.Sin, scale=TWO_PI / 2).then_inc(small_sin, 1)
            for half in range(2):
                act.wait_ge(pool_chain, 2 * (half + 1))
                dh = decay[:, half * H // 2:(half + 1) * H // 2, :]
                act.activation(dh, dh, ACT.Exp, scale=-1.0).then_inc(decay_exp, 1)

            def evacuate_taps(q):
                u = q % 2
                bank = (zbank if u == 0 else glbank)[0:NSMALL, 0:2, :]\
                    .rearrange("p a (h l d j) -> p (l d) (a h) j", l=NL, d=C, j=C, h=QH // 2)
                act.wait_ge(taps_psum, q + 1)
                for j in range(C):
                    out = taps[NSMALL * j:NSMALL * (j + 1), :, :, QH * q:QH * (q + 1)]\
                        .rearrange("p l d h -> p (l d) h")
                    nc.scalar.copy(out, bank[:, :, :, j]).then_inc(taps_ready, 1)

            act.wait_ge(rows_in, 48)
            for q in range(NQ):
                u = q % 2
                act.wait_ge(part_ready, 2 * (q + 1))
                if q >= 2:
                    act.wait_ge(pow_ready, 2 * (q - 1))
                act.activation(sines[:, u, :, :], part[:, u, :, :], ACT.Sin, scale=TWO_PI).then_inc(sines_ready, 1)
                act.activation(cosines[:, u, :, :], apart[:, u, :, :], ACT.Sin, scale=-TWO_PI,
                               bias=cols[:, 8:9]).then_inc(sines_ready, 1)
                if q >= 1:
                    vbd_copies(act, nc.scalar, q - 1, v_re, vbd_re, vbd_re_ready)
                if q >= 2:
                    evacuate_taps(q - 2)
            vbd_copies(act, nc.scalar, NQ - 1, v_re, vbd_re, vbd_re_ready)
            evacuate_taps(NQ - 2)
            evacuate_taps(NQ - 1)
            def take_spectra(l):
                act.wait_ge(spec_psum, l + 1)
                nc.scalar.copy(spectra[:, l, :, :, :].rearrange("p d k h -> p k d h"),
                               zbank[:, :, :].rearrange("p k (d h) -> p k d h", d=C)).then_inc(spec_ready, 1)
                act.wait_ge(resp_psum, l + 1)
                act.activation(ln_bias_response[:, l, :], ybank[1][:, :], ACT.Identity,
                               scale=cols[:, l:l + 1]).then_inc(resp_ready, 1)

            def normalize(out, src, u, done):
                for c in range(C):
                    act.activation(out[:, c, :], src[:, c, :], ACT.Identity, scale=rs[:, u, 0, c:c + 1],
                                   bias=rs[:, u, 1, c:c + 1]).then_inc(done[c == C - 1], 1)

            def x_norm_of(n, u):
                act.wait_ge(xrstd, RSTD * (n + 1))
                normalize(h[:, ds(n), :, :].squeeze(1), x_in[:, ds(n), :, :].squeeze(1), u, (x_norm, h_ready))

            def x_part(n, u, more):
                if more:
                    x_norm_of(n + 1, 1 - u)
                act.wait_ge(q8_turned, n + 1)
                nc.scalar.copy(q8T[:, u, :], ybank[0][:, :]).then_inc(q8T_ready, 1)
                act.wait_ge(ffn_psum, n + 1)
                act.activation(th8[:, u, :, :], xbank[:, :].rearrange("p (c h) -> p c h", c=C),
                               ACT.Tanh).then_inc(ffn_tanh, 1)
            act.wait_ge(kgen_idle, 1)
            x_norm_of(0, 0)
            take_spectra(0)
            for n in range(NL - 1):
                x_part(n, n % 2, True)
                take_spectra(n + 1)
            x_part(NL - 1, 1, True)
            with act.Fori(NL // 2, B // 2 - 1) as i:
                for u in range(2):
                    x_part(2 * i + u, u, True)
            x_part(B - 2, 0, True)
            x_part(B - 1, 1, False)

            def make_zn(n, u):
                act.wait_ge(lrstd, RSTD * (n + 1))
                if not isinstance(n, int) or n >= 2:
                    act.wait_ge(z_ready, n - 1)
                hb = h[:, ds(n % B), :, :].squeeze(1) if not isinstance(n, int) else h[:, n % B, :, :]
                normalize(zn[:, u, :, :], hb, u, (zn_ready, zn_ready))

            make_zn(0, 0)

            def step(k, first, last):
                u = k_par(k)
                if not last or k + 1 < NL * B:
                    make_zn(k + 1, 1 - u)
                if not (isinstance(k, int) and (k < 1 or k > NL * B)):
                    n = k - 1
                    act.wait_ge(y_psum, n + 1)
                    if not (isinstance(n, int) and n < 2):
                        act.wait_ge(glu_psum, n - 1)
                    act.activation(y[:, 1 - u, :], ybank[1 - u][:, :], ACT.Gelu_apprx_tanh).then_inc(y_ready, 1)
                if not first:
                    n = k - 2
                    act.wait_ge(glu_psum, n + 1)
                    if not (isinstance(n, int) and n < 2):
                        act.wait_ge(glu_ready, n - 1)
                    act.activation(th[:, u, :, :],
                                   glbank[:, :, :].rearrange("p a (c o) -> p (a c) o", c=2)[:, :, H:2 * H],
                                   ACT.Tanh, scale=0.5).then_inc(glu_tanh, 1)
            run_steps(act, step)

            def norm1(n, u):
                act.wait_ge(nrstd, RSTD * (n + 1))
                if at_least(n, 2):
                    act.wait_ge(xs_ready, n - 1)
                normalize(xn1[:, u, :, :], x1[:, ds(n), :, :].squeeze(1), u, (xn1_ready, xn1_ready))

            def take_turned(n, u):
                act.wait_ge(xn1_turned, n + 1)
                nc.scalar.copy(xT[:, u, :], ybank[0][:, :]).then_inc(xT_ready, 1)

            def best_tanh(n, u):
                act.wait_ge(logit_step, 2 * (n + 1))
                act.activation(sc[:, u, 0, :], mx[:, ds(n), :].squeeze(1), ACT.Tanh, scale=0.5).then_inc(mx_tanh, 1)

            def take_outputs(n):
                act.wait_ge(down_psum, n + 1)
                nc.scalar.copy(fo[:, ds(n), :, :].squeeze(1), xbank[:, :].rearrange("p (c h) -> p c h", c=C))\
                    .then_inc(fo_ready, 1)
                act.wait_ge(attn_psum, n + 1)
                nc.scalar.copy(sa[:, ds(n), :, :].squeeze(1), ybank[1][:, :].rearrange("p (c h) -> p c h", c=C))\
                    .then_inc(sa_ready, 1)
            norm1(0, 0)
            take_turned(0, 0)
            norm1(1, 1)
            best_tanh(0, 0)
            take_turned(1, 1)

            def second(n, u):
                act.wait_ge(kmin_ready, n + 1)
                if at_least(n, 1):
                    act.wait_ge(wkv_step, WKV * n)
                act.activation(ek, kmin, ACT.Exp).then_inc(ek_ready, 1)
                if at_least(n, 1):
                    act.wait_ge(rw_ready, n)
                act.activation(tr, zbank[:, 2, :], ACT.Tanh, scale=0.5).then_inc(tr_ready, 1)

                def gate_tanh(f):
                    act.wait_ge(gu_psum, 2 * n + f + 1)
                    if f or at_least(n, 1):
                        act.wait_ge(ffn_step, 2 * (2 * n + f))
                    act.activation(tg, glbank[:, 0, :], ACT.Tanh, scale=0.5).then_inc(tg_ready, 1)
                gate_tanh(0)
                if at_least(n, 1):
                    take_outputs(n - 1)
                if follows(n, 1):
                    best_tanh(n + 1, 1 - u)
                if follows(n, 2):
                    norm1(n + 2, u)
                gate_tanh(1)
                if follows(n, 2):
                    take_turned(n + 2, u)
            run_batches(act, second)
            take_outputs(B - 1)

            def step(k, u):
                if live(k, 1):
                    n = k - 1
                    act.wait_ge(gur_psum, n + 1)
                    if at_least(n, 2):
                        act.wait_ge(hr_ready, n - 1)
                    act.activation(sil[:, 1 - u, :], glbank[:, 1 - u, 0:F], ACT.Silu).then_inc(sil_ready, 1)
                if live(k, 3):
                    n = k - 3
                    act.wait_ge(y_r_psum, n + 1)
                    if at_least(n, 2):
                        act.wait_ge(stored[1 - u], 16 * (n // 2))
                    nc.scalar.copy(ytok[:, 1 - u, :], (xbank[:, 0:P] if u else zbank[:, 2, 0:P])).then_inc(ytok_ready, 1)
                if live(k, 4):
                    n = k - 4
                    act.wait_ge(ytok_ready, n + 1)
                    act.dma_start(y_sorted[ds(n * P, P), :], ytok[:, u, :]).then_inc(stored[u], 16)
            run_tiles(act, step)
            for b in range(B):
                act.wait_ge(tot_ready, b + 1)
                act.activation(tot[:, b % 2, :, :], tot[:, b % 2, :, :], ACT.Silu).then_inc(tot_silu, 1)

        @block.tensor
        def _(pe):
            pe.wait_ge(const_in, 32)
            for q in range(NQ):
                u = q % 2
                bank = (zbank if u == 0 else glbank)[0:NSMALL, 0:2, :]\
                    .rearrange("p a (h n) -> p (a h) n", n=NL * NBIG)
                pe.wait_ge(pow_ready, 2 * (q + 1))
                pe.wait_ge(vbd_re_ready, NL * (q + 1))
                pe.wait_ge(vbd_im_ready, NL * (q + 1))
                if q >= 2:
                    pe.wait_ge(taps_ready, C * (q - 1))
                for c in range(QH):
                    pe.matmul(bank[:, c, :], pow_re[:, u, c, 0:NSMALL], vbd_re[:, u, c, :, :],
                              start=True, stop=False)
                    mm = pe.matmul(bank[:, c, :], pow_im[:, u, c, 0:NSMALL], vbd_im[:, u, c, :, :],
                                   start=False, stop=True)
                mm.then_inc(taps_psum, 1)
            def spectra_of(l):
                pe.wait_ge(tapsw_ready, l + 1)
                if l >= 1:
                    pe.wait_ge(spec_ready, l)
                for k in range(NK):
                    pe.matmul(zbank[:, k, :], ker[:, k, :], taps_w[:, l, :, :], start=True, stop=False)
                    mm = pe.matmul(zbank[:, k, H:T], ker2[:, k, :], taps_w[:, l, 0:C - 1, :],
                                   start=False, stop=True)
                mm.then_inc(spec_psum, 1)
                if l >= 1:
                    pe.wait_ge(resp_ready, l)
                for c in range(C):
                    mm = pe.matmul(ybank[1][:, c * P:T], taps[:, l, c, :], tri[:, 0:T - c * P],
                                   start=(c == 0), stop=(c == C - 1))
                mm.then_inc(resp_psum, 1)

            spectra_of(0)
            pe.wait_ge(wts_in, 7 * 16)
            pe.wait_ge(small_w, 3)

            def x_part(n, u, past):
                pe.wait_ge(q8_ready, 6 * (n + 1))
                if past:
                    pe.wait_ge(q8T_ready, n)
                for c in range(C):
                    mm = pe.transpose(ybank[0][:, c * P:(c + 1) * P], q8r[:, u, c * P:(c + 1) * P], ident[:, :])
                mm.then_inc(q8_turned, 1)
                pe.wait_ge(q8T_ready, n + 1)
                if past:
                    pe.wait_ge(g0_ready, n)
                pe.matmul(xbank[:, :], ones3[:, :], b_ffn.unsqueeze(1).broadcast_to([3, C, H]), start=True, stop=False)
                for c in range(C):
                    mm = pe.matmul(xbank[:, c * H:(c + 1) * H], q8T[:, u, c * P:(c + 1) * P], w8[:, :],
                                   start=False, stop=(c == C - 1))
                mm.then_inc(ffn_psum, 1)
            for n in range(NL - 1):
                x_part(n, n % 2, n > 0)
                spectra_of(n + 1)
            x_part(NL - 1, 1, True)
            with pe.Fori(NL // 2, B // 2) as i:
                for u in range(2):
                    x_part(2 * i + u, u, True)

            def step(k, first, last):
                u = k_par(k)
                if not (isinstance(k, int) and k >= NL * B):
                    pe.wait_ge(zn_ready, C * (k + 1))
                    if not (isinstance(k, int) and k < 1):
                        pe.wait_ge(conv_step, CONV * k - 3)
                    for m in range(NK):
                        mm = pe.matmul(zbank[:, m, :], fwd[m], zn[:, u, :, :], start=True, stop=True)
                    mm.then_inc(z_ready, 1)
                if not (isinstance(k, int) and (k < 1 or k > NL * B)):
                    n = k - 1
                    pe.wait_ge(conv_step, CONV * (n + 1))
                    if not (isinstance(n, int) and n < 2):
                        pe.wait_ge(y_ready, n - 1)
                    resp = ln_bias_response[:, ds(n // B), :].squeeze(1) if not isinstance(n, int) \
                        else ln_bias_response[:, n // B, :]
                    pe.matmul(ybank[1 - u][:, :], ident[:, :], resp, start=True, stop=False)
                    for c in range(C):
                        for m in range(NK):
                            mm = pe.matmul(ybank[1 - u][:, c * P:(c + 1) * P], acc[:, 1 - u, m, c * H:(c + 1) * H],
                                           inv[:, m, :], start=False, stop=(c == C - 1 and m == NK - 1))
                    mm.then_inc(y_psum, 1)
                if not first:
                    n = k - 2
                    pe.wait_ge(y_ready, n + 1)
                    if not (isinstance(n, int) and n < 1):
                        pe.wait_ge(glu_ready, n)
                    dyn = not isinstance(n, int)
                    wg = w_glu[:, ds(n // B), :].squeeze(1) if dyn else w_glu[:, n // B, :]
                    bg = b_glu[:, ds(n // B), :].broadcast_to([3, 2, 2 * H]) if dyn \
                        else b_glu[:, n // B:n // B + 1, :].broadcast_to([3, 2, 2 * H])
                    for a in range(2):
                        pe.matmul(glbank[:, a, :], ones3[:, :], bg, start=True, stop=False)
                        for c in range(2):
                            mm = pe.matmul(glbank[:, a, c * 2 * H:(c + 1) * 2 * H],
                                           y[:, u, (2 * a + c) * P:(2 * a + c + 1) * P], wg,
                                           start=False, stop=(c == 1))
                    mm.then_inc(glu_psum, 1)
            run_steps(pe, step)

            def turn(n, u):
                pe.wait_ge(xn1_ready, C * (n + 1))
                if at_least(n, 1):
                    pe.wait_ge(logit_step, 2 * n - 1)
                for c in range(C):
                    mm = pe.transpose(ybank[0][:, c * P:(c + 1) * P], xn1[:, u, c, :], ident[:, :])
                mm.then_inc(xn1_turned, 1)

            def logits(n, u):
                pe.wait_ge(xT_ready, n + 1)
                for c in range(C):
                    mm = pe.matmul(ybank[0][:, c * E:(c + 1) * E], xT[:, u, c * P:(c + 1) * P], w_gate[:, :],
                                   start=True, stop=True)
                mm.then_inc(logit_psum, 1)

            def kvr(n):
                pe.wait_ge(xm_step, 2 * (n + 1))
                if at_least(n, 1):
                    pe.wait_ge(wkv_step, WKV * (n - 1) + 1)
                    pe.wait_ge(tr_ready, n)
                for m in range(3):
                    mm = pe.matmul(zbank[:, m, :], w_attn[:, m, :], xm, start=True, stop=True)
                mm.then_inc(kvr_psum, 1)

            def outputs(n, u):
                pe.wait_ge(ffn_step, 2 * (2 * n + 2))
                if at_least(n, 1):
                    pe.wait_ge(fo_ready, n)
                for c in range(C):
                    for f in range(2):
                        mm = pe.matmul(xbank[:, c * H:(c + 1) * H], hs[:, u, f, c * P:(c + 1) * P], w_sd[:, f, :],
                                       start=(f == 0), stop=(f == 1))
                mm.then_inc(down_psum, 1)
                pe.wait_ge(rw_ready, n + 1)
                if at_least(n, 1):
                    pe.wait_ge(sa_ready, n)
                for c in range(C):
                    mm = pe.matmul(ybank[1][:, c * H:(c + 1) * H], rw[:, u, c * P:(c + 1) * P], w_attn[:, 3, :],
                                   start=True, stop=True)
                mm.then_inc(attn_psum, 1)
            turn(0, 0)
            pe.wait_ge(w_half, 2)
            logits(0, 0)
            kvr(0)
            turn(1, 1)

            def second(n, u):
                def gate_up(f):
                    if f or at_least(n, 1):
                        pe.wait_ge(ffn_step, 2 * (2 * n + f))
                    for m in range(2):
                        mm = pe.matmul(glbank[:, m, :], w_sgu[:, m, f * P:(f + 1) * P], xT[:, u, :],
                                       start=True, stop=True)
                    mm.then_inc(gu_psum, 1)
                gate_up(0)
                if follows(n, 1):
                    logits(n + 1, 1 - u)
                if at_least(n, 1):
                    outputs(n - 1, 1 - u)
                gate_up(1)
                if follows(n, 1):
                    kvr(n + 1)
                if follows(n, 2):
                    turn(n + 2, u)
            run_batches(pe, second)
            outputs(B - 1, 1)

            pe.wait_ge(oh_ready, 3)
            pe.wait_ge(xT_ready, B)
            pe.matmul(ybank[0][:, 0:B * C * E], strict16[:, :], oh16[:, :], start=True, stop=True)
            pe.matmul(ybank[0][:, B * C * E:2 * B * C * E], ones16[:, :], oh16[:, :],
                      start=True, stop=True).then_inc(rank_psum, 1)

            pe.wait_ge(slot_ready, 2)
            pe.wait_ge(routed_in, 16)
            pe.wait_ge(fo_ready, B)
            pe.wait_ge(sa_ready, B)

            def step(k, u):
                if live(k, 0):
                    pe.wait_ge(tiles_in[u], 16 * (k // 2 + 1))
                    if at_least(k, 2):
                        pe.wait_ge(tile_copied, k - 1)
                    pe.transpose(zbank[:, u, 0:P], xtok[:, u, :], ident[:, :]).then_inc(tile_turned, 1)
                if live(k, 1):
                    n = k - 1
                    e = pe.value_load(tile_e[0:1, ds(n)], min_val=0, max_val=E - 1)
                    pe.wait_ge(tile_copied, n + 1)
                    if at_least(n, 2):
                        pe.wait_ge(hr_ready, n - 1)
                    pe.matmul(glbank[:, 1 - u, :], xt_r[:, 1 - u, :], routed[:, ds(e * (2 * F), 2 * F)],
                              start=True, stop=True).then_inc(gur_psum, 1)
                if live(k, 2):
                    n = k - 2
                    pe.wait_ge(hr_ready, n + 1)
                    if at_least(n, 2):
                        pe.wait_ge(hT_ready, n - 1)
                    for f in range(2):
                        mm = pe.transpose(ybank[u][:, f * P:(f + 1) * P], h_r[:, u, f * P:(f + 1) * P], ident[:, :])
                    mm.then_inc(hr_turned, 1)
                if live(k, 3):
                    n = k - 3
                    e = pe.value_load(tile_e[0:1, ds(n)], min_val=0, max_val=E - 1)
                    pe.wait_ge(hT_ready, n + 1)
                    if at_least(n, 2):
                        pe.wait_ge(ytok_ready, n - 1)
                    out = xbank[:, 0:P] if u else zbank[:, 2, 0:P]
                    for f in range(2):
                        mm = pe.matmul(out, hT_r[:, 1 - u, f * P:(f + 1) * P],
                                       routed[:, ds(e * (2 * H) + E * 2 * F + f * H, H)], start=(f == 0), stop=(f == 1))
                    mm.then_inc(y_r_psum, 1)
            run_tiles(pe, step)

        @block.vector
        def _(dve):
            links = [0]

            def link(ins):
                links[0] += 1
                ins.then_inc(dve_chain, 1)
                dve.wait_ge(dve_chain, links[0])

            def tt(o, a, b, op):
                link(dve.tensor_tensor(o, a, b, op))

            def ts(o, a, s1, s2, op0, op1=None):
                link(dve.tensor_scalar(o, a, s1, s2, op0) if op1 is None
                     else dve.tensor_scalar(o, a, s1, s2, op0, op1))

            def stt(o, a, s, b, op0, op1):
                link(dve.scalar_tensor_tensor(out=o, in0=a, scalar=s, in1=b, op0=op0, op1=op1))

            S = [small[:, i, :] for i in range(22)]
            dt, alpha, ea, em1, s1, s2 = S[5], S[6], S[7], S[8], S[9], S[10]
            beta, c_re, c_im = raw[:, 2, :], raw[:, 3, :], raw[:, 4, :]

            def exact_exp(x, lo, n):
                k, rem, p, s = [small[:, lo + n * m:lo + n * (m + 1), :] for m in range(4)]
                ts(rem, x, -87.0, 88.0, ALU.max, ALU.min)
                ts(k, rem, float(np.log2(np.e)), ROUND, ALU.mult, ALU.add)
                ts(k, k, -ROUND, None, ALU.add)
                stt(rem, k, -LN2_HI, rem, ALU.mult, ALU.add)
                stt(rem, k, -LN2_LO, rem, ALU.mult, ALU.add)
                ts(s.bitcast(I32), k, 127.0, 2.0 ** 23, ALU.add, ALU.mult)
                ts(p, rem, 1.0 / 5040, None, ALU.mult)
                for c in (1.0 / 720, 1.0 / 120, 1.0 / 24, 1.0 / 6, 0.5, 1.0):
                    stt(p, p, c, rem, ALU.add, ALU.mult)
                return p, s
            dve.wait_ge(modes_in, 80)
            p, s = exact_exp(raw[:, 0:2, :], 11, 2)
            stt(small[:, 5:7, :], p, 1.0, s, ALU.add, ALU.mult)
            tt(S[1], alpha, dt, ALU.mult)
            tt(S[11], beta, dt, ALU.mult)
            ts(S[11], S[11], float(1 / (2 * np.pi)), None, ALU.mult)
            ts(S[12], S[11], ROUND, -ROUND, ALU.add, ALU.add)
            tt(S[3], S[11], S[12], ALU.subtract)
            ts(S[11], S[3], float(NSMALL), None, ALU.mult)
            ts(S[12], S[11], ROUND, -ROUND, ALU.add, ALU.add)
            tt(S[4], S[11], S[12], ALU.subtract)
            dve.tensor_scalar(S[2], S[1], float(NSMALL), None, ALU.mult).then_inc(decay_ready, 1)
            ts(S[11], S[1], -1.0, None, ALU.mult)
            p, s = exact_exp(small[:, 11:12, :], 12, 1)
            p, s = p[:, 0, :], s[:, 0, :]
            stt(ea, p, 1.0, s, ALU.add, ALU.mult)
            ts(S[11], s, -1.0, None, ALU.add)
            tt(p, p, s, ALU.mult)
            tt(em1, p, S[11], ALU.add)
            dve.wait_ge(small_sin, 2)
            tt(S[14], s2, s2, ALU.mult)
            ts(S[15], S[14], -2.0, 1.0, ALU.mult, ALU.add)
            tt(S[13], em1, S[15], ALU.mult)
            stt(S[13], S[14], -2.0, S[13], ALU.mult, ALU.add)
            tt(S[14], ea, s1, ALU.mult)
            tt(S[15], alpha, alpha, ALU.mult)
            tt(S[16], beta, beta, ALU.mult)
            tt(S[15], S[15], S[16], ALU.add)
            link(dve.reciprocal(S[15], S[15]))
            tt(S[16], S[14], beta, ALU.mult)
            tt(S[17], S[13], alpha, ALU.mult)
            tt(S[16], S[16], S[17], ALU.subtract)
            tt(S[16], S[16], S[15], ALU.mult)
            tt(S[17], S[13], beta, ALU.mult)
            tt(S[18], S[14], alpha, ALU.mult)
            tt(S[17], S[17], S[18], ALU.add)
            tt(S[17], S[17], S[15], ALU.mult)
            tt(S[18], c_re, S[16], ALU.mult)
            tt(S[19], c_im, S[17], ALU.mult)
            tt(S[18], S[18], S[19], ALU.add)
            tt(S[19], c_im, S[16], ALU.mult)
            tt(S[20], c_re, S[17], ALU.mult)
            tt(S[19], S[19], S[20], ALU.subtract)
            cr, ci, ncr, nci = S[13], S[14], S[15], S[16]
            ts(cr, S[18], 2.0, None, ALU.mult)
            ts(ncr, S[18], -2.0, None, ALU.mult)
            ts(ci, S[19], 2.0, None, ALU.mult)
            ts(nci, S[19], -2.0, None, ALU.mult)

            def reduce_turns(q):
                u = q % 2
                dve.wait_ge(turns_ready, 2 * (q + 1))
                if q >= 2:
                    dve.wait_ge(sines_ready, 2 * (q - 1))
                ts(apart[:, u, :, :], turns[:, u, :, :], ROUND, -ROUND, ALU.add, ALU.add)
                dve.tensor_tensor(part[:, u, :, :], turns[:, u, :, :], apart[:, u, :, :], ALU.subtract).then_inc(part_ready, 1)
                dve.wait_ge(part_ready, 2 * q + 1)
                dve.tensor_scalar(apart[:, u, :, :].bitcast(I32), part[:, u, :, :].bitcast(I32), 0x7FFFFFFF, None,
                                  ALU.bitwise_and).then_inc(part_ready, 1)
            reduce_turns(0)
            dve.wait_ge(decay_exp, 2)
            for q in range(NQ):
                u = q % 2
                if q + 1 < NQ:
                    reduce_turns(q + 1)
                dve.wait_ge(sines_ready, 2 * (q + 1))
                if q >= 2:
                    dve.wait_ge(taps_psum, q - 1)
                dq = decay[:, QH * q:QH * (q + 1), :]
                dve.tensor_tensor(pow_re[:, u, :, :], dq, cosines[:, u, :, :], ALU.mult).then_inc(pow_ready, 1)
                dve.tensor_tensor(pow_im[:, u, :, :], dq, sines[:, u, :, :], ALU.mult).then_inc(pow_ready, 1)
                dve.wait_ge(pow_ready, 2 * (q + 1))

                def coef(x):
                    return x[:, QH * q:QH * (q + 1)].unsqueeze(2).broadcast_to([P, QH, NBIG])
                big_re, big_im = pow_re[:, u, :, NSMALL:NPOW], pow_im[:, u, :, NSMALL:NPOW]
                tt(vt[:, 0, :, :], big_re, coef(cr), ALU.mult)
                tt(vt[:, 1, :, :], big_im, coef(ci), ALU.mult)
                tt(vt[:, 2, :, :], big_re, coef(nci), ALU.mult)
                tt(vt[:, 3, :, :], big_im, coef(ncr), ALU.mult)
                if q >= 2:
                    dve.wait_ge(vbd_re_ready, NL * (q - 1))
                    dve.wait_ge(vbd_im_ready, NL * (q - 1))
                dve.tensor_tensor(v_re[:, u, :, :], vt[:, 0, :, :], vt[:, 1, :, :], ALU.subtract).then_inc(v_ready, 1)
                dve.tensor_tensor(v_im[:, u, :, :], vt[:, 2, :, :], vt[:, 3, :, :], ALU.add).then_inc(v_ready, 1)
            dve.wait_ge(rows_in, 48)
            dve.wait_ge(wts_in, 7 * 16)
            bg = biases_raw[:, 0:NL * 2 * H].rearrange("p (l o) -> p l o", l=NL)
            ts(bg[:, :, 0:H], bg[:, :, 0:H], 0.5, None, ALU.mult)
            ts(biases_raw[:, NL * 2 * H:], biases_raw[:, NL * 2 * H:], 0.5, None, ALU.mult)
            dve.tensor_scalar(w_glu[:, :, 0:H], w_glu[:, :, 0:H], 0.5, None, ALU.mult).then_inc(small_w, 1)
            ts(w8[:, :], w8[:, :], cols[:, 10:11], cols[:, 9:10], ALU.mult, ALU.mult)
            dve.tensor_scalar(w8[:, :], w8[:, :], 0.5, None, ALU.mult).then_inc(small_w, 1)
            link(dve.reciprocal(idle[:, 2:3], cols[:, 9:10]))
            w16 = [bsp16[:, i, 0:NBIAS] for i in range(3)]
            link(dve.tensor_copy(w16[0], biases_raw))
            tt(bsp[:, 0, :], biases_raw, w16[0], ALU.subtract)
            link(dve.tensor_copy(w16[1], bsp[:, 0, :]))
            tt(bsp[:, 1, :], bsp[:, 0, :], w16[1], ALU.subtract)
            link(dve.tensor_copy(w16[2], bsp[:, 1, :]))
            ts(bsp[:, 0, :], w16[0], ident[0:3, 0:1], None, ALU.mult)
            stt(bsp[:, 1, :], w16[1], ident[0:3, 1:2], bsp[:, 0, :], ALU.mult, ALU.add)
            dve.scalar_tensor_tensor(out=biases[:, :], in0=w16[2], scalar=ident[0:3, 2:3], in1=bsp[:, 1, :],
                                     op0=ALU.mult, op1=ALU.add).then_inc(small_w, 1)
            dve.wait_ge(taps_ready, C * NQ)
            tt(taps[0:1, :, 0, :], taps[0:1, :, 0, :], d_row.rearrange("p (l h) -> p l h", l=NL), ALU.add)
            dve.wait_ge(small_w, 3)
            for l in range(NL):
                dve.tensor_tensor(taps_w[:, l, :, :], taps[:, l, :, :],
                                  ln_w_rows[:, l, :].unsqueeze(1).broadcast_to([P, C, H]),
                                  ALU.mult).then_inc(tapsw_ready, 1)
            dve.memset(idle[:, 0:1], 0.0).then_inc(kgen_idle, 1)

            def norm_stats(src, u, done):
                for c in range(C):
                    dve.bn_stats(stats[:, u, c, :], src[:, c, :]).then_inc(done, 1)

            def quantize(n, u, past):
                w = 6 * n
                if past:
                    dve.wait_ge(q8_ready, w)
                dve.wait_ge(x_norm, (C - 1) * (n + 1))
                dve.wait_ge(h_ready, n + 1)
                xn = h[:, ds(n), :, :].squeeze(1).rearrange("p c h -> p (c h)")
                dve.tensor_scalar(q8, xn, idle[:, 2:3], FMAX8, ALU.mult, ALU.min).then_inc(q8_ready, 1)
                dve.wait_ge(q8_ready, w + 1)
                dve.tensor_scalar(q8, q8, -FMAX8, None, ALU.max).then_inc(q8_ready, 1)
                dve.wait_ge(q8_ready, w + 2)
                dve.tensor_scalar(q8s.bitcast(I32), q8.bitcast(I32), 0x7F800000, None,
                                  ALU.bitwise_and).then_inc(q8_ready, 1)
                dve.wait_ge(q8_ready, w + 3)
                dve.tensor_scalar(q8s, q8s, 2.0 ** -6, 1.5 * 2.0 ** 20, ALU.max, ALU.mult).then_inc(q8_ready, 1)
                dve.wait_ge(q8_ready, w + 4)
                dve.tensor_tensor(q8, q8, q8s, ALU.add).then_inc(q8_ready, 1)
                dve.wait_ge(q8_ready, w + 5)
                dve.tensor_tensor(q8r[:, u, :], q8, q8s, ALU.subtract).then_inc(q8_ready, 1)

            def gate0(n, u):
                dve.wait_ge(ffn_tanh, n + 1)
                dve.scalar_tensor_tensor(out=g0[:, ds(n), :, :].squeeze(1), in0=th8[:, u, :, :], scalar=1.0,
                                         in1=xbank[:, :].rearrange("p (c h) -> p c h", c=C),
                                         op0=ALU.add, op1=ALU.mult).then_inc(g0_ready, 1)
            def x_part(n, u, more, past):
                quantize(n, u, past)
                if more:
                    norm_stats(x_in[:, ds(n + 2), :, :].squeeze(1), u, xstats)
                if past:
                    gate0(n - 1, 1 - u)
            dve.wait_ge(x_in_s, 16)
            for u in range(2):
                norm_stats(x_in[:, u, :, :], u, xstats)
            x_part(0, 0, True, False)
            x_part(1, 1, True, True)
            with dve.Fori(1, B // 2 - 1) as i:
                for u in range(2):
                    x_part(2 * i + u, u, True, True)
            x_part(B - 2, 0, False, True)
            x_part(B - 1, 1, False, True)
            gate0(B - 1, 1)

            def layer_stats(n, u):
                if not isinstance(n, int) or n >= 2:
                    dve.wait_ge(zn_ready, C * (n - 1))
                dve.wait_ge(h_ready, n + 1)
                hb = h[:, ds(n % B), :, :].squeeze(1) if not isinstance(n, int) else h[:, n % B, :, :]
                norm_stats(hb, u, lstats)

            layer_stats(0, 0)
            layer_stats(1, 1)

            def step(k, first, last):
                u = k_par(k)
                dyn = not isinstance(k, int)
                if dyn or k < NL * B:
                    w = CONV * k
                    dve.wait_ge(z_ready, k + 1)
                    if dyn or k >= 2:
                        dve.wait_ge(y_psum, k - 1)
                    if dyn or k >= 1:
                        dve.wait_ge(conv_step, w)
                    for dist in range(C):
                        n = C - dist
                        sp_d = spectra[:, ds(k // B), dist, :, :].squeeze(1) if dyn else spectra[:, k // B, dist, :, :]
                        dst = acc[:, u, :, :] if dist == 0 else tmps[dist]
                        dve.tensor_tensor(dst.rearrange("p k (c h) -> p k c h", c=n),
                                          zbank[:, :, 0:n * H].rearrange("p k (c h) -> p k c h", c=n),
                                          sp_d.unsqueeze(2).broadcast_to([P, NK, n, H]),
                                          ALU.mult).then_inc(conv_step, 1)
                    for dist in range(1, C):
                        dve.wait_ge(conv_step, w + C + dist - 1)
                        a = acc[:, u, :, dist * H:]
                        dve.tensor_tensor(a, a, tmps[dist], ALU.add).then_inc(conv_step, 1)
                if not first:
                    n = k - 2
                    dve.wait_ge(glu_tanh, n + 1)
                    if not (isinstance(n, int) and n < 2):
                        dve.wait_ge(h_ready, B + n - 1)
                    dve.scalar_tensor_tensor(
                        out=prod[:, u, :, :], in0=th[:, u, :, :], scalar=1.0,
                        in1=glbank[:, :, :].rearrange("p a (c o) -> p (a c) o", c=2)[:, :, 0:H],
                        op0=ALU.add, op1=ALU.mult).then_inc(glu_ready, 1)
                if not last:
                    layer_stats(k + 2, u)
                elif 0 <= k - (NL * B - 1) < 2:
                    n = k - (NL * B - 1)
                    dve.wait_ge(x1_step, 2 * (n + 1))
                    norm_stats(x1[:, n, :, :], n % 2, nstats)
            run_steps(dve, step)

            dve.tensor_scalar(w_attn[:, 3, :], w_attn[:, 3, :], 0.5, None, ALU.mult).then_inc(w_half, 1)
            dve.tensor_scalar(w_sd[:, :, :], w_sd[:, :, :], 0.5, None, ALU.mult).then_inc(w_half, 1)
            ts(dcol[:, 3:4], cols[:, 4:5], -1.0, 1.0, ALU.mult, ALU.add)
            dve.wait_ge(dcols, 3)
            link(dve.memset(s_num[:, 0:1], 0.0))
            link(dve.memset(s_den[:, 0:1], 0.0))

            def mix(n, u):
                dve.wait_ge(xT_ready, n + 1)
                dve.tensor_scalar(xm, xT[:, u, :], cols[:, 4:5], None, ALU.mult).then_inc(xm_step, 1)
                dve.wait_ge(xm_step, 2 * n + 1)
                dve.scalar_tensor_tensor(out=xm[:, 1:T], in0=xT[:, u, 0:T - 1], scalar=dcol[:, 3:4],
                                         in1=xm[:, 1:T], op0=ALU.mult, op1=ALU.add).then_inc(xm_step, 1)

            def best_logits(n):
                dve.wait_ge(logit_psum, n + 1)
                l8n = l8[:, ds(n), :, :].squeeze(1)
                dve.tensor_copy(l8n, ybank[0][:, 0:C * E].rearrange("p (c e) -> p c e", c=C)).then_inc(logit_step, 1)
                dve.wait_ge(logit_step, 2 * n + 1)
                dve.tensor_reduce(mx[:, ds(n), :].squeeze(1), l8n, AX, ALU.max).then_inc(logit_step, 1)
            mix(0, 0)
            best_logits(0)

            def second(n, u):
                dve.wait_ge(kvr_psum, n + 1)
                if at_least(n, 1):
                    dve.wait_ge(ek_ready, n)
                dve.tensor_scalar(kmin, zbank[:, 0, :], 60.0, None, ALU.min).then_inc(kmin_ready, 1)
                if follows(n, 1):
                    mix(n + 1, 1 - u)
                if follows(n, 2):
                    dve.wait_ge(x1_step, 2 * (n + 3))
                    norm_stats(x1[:, ds(n + 2), :, :].squeeze(1), u, nstats)
                if follows(n, 1):
                    best_logits(n + 1)
                w = WKV * n
                if at_least(n, 1):
                    dve.wait_ge(wkv_step, w)
                dve.wait_ge(ek_ready, n + 1)
                dve.tensor_tensor(kv, ek, zbank[:, 1, :], ALU.mult).then_inc(wkv_step, 1)
                step_decay = dcol[:, 1:2].broadcast_to([P, T])
                dve.tensor_tensor_scan(s_den[:, 1:T + 1], step_decay, ek, 0.0, ALU.mult, ALU.add).then_inc(wkv_step, 1)
                dve.wait_ge(wkv_step, w + 1)
                dve.tensor_tensor_scan(s_num[:, 1:T + 1], step_decay, kv, 0.0, ALU.mult, ALU.add).then_inc(wkv_step, 1)

                def shared(f):
                    dve.wait_ge(tg_ready, 2 * n + f + 1)
                    dve.scalar_tensor_tensor(out=sl, in0=tg, scalar=1.0, in1=glbank[:, 0, :], op0=ALU.add,
                                             op1=ALU.mult).then_inc(ffn_step, 1)
                    dve.wait_ge(ffn_step, 2 * (2 * n + f) + 1)
                    dve.tensor_tensor(hs[:, u, f, :], sl, glbank[:, 1, :], ALU.mult).then_inc(ffn_step, 1)
                shared(0)
                if at_least(n, 1):
                    dve.wait_ge(ratio_ready, n)
                dve.wait_ge(wkv_step, w + 2)
                dve.scalar_tensor_tensor(out=den, in0=ek, scalar=dcol[:, 2:3], in1=s_den[:, 0:T], op0=ALU.mult,
                                         op1=ALU.add).then_inc(wkv_step, 1)
                dve.wait_ge(wkv_step, w + 3)
                dve.scalar_tensor_tensor(out=num, in0=kv, scalar=dcol[:, 2:3], in1=s_num[:, 0:T], op0=ALU.mult,
                                         op1=ALU.add).then_inc(wkv_step, 1)
                dve.wait_ge(wkv_step, w + 4)
                dve.tensor_scalar(den, den, 1e-9, None, ALU.add).then_inc(wkv_step, 1)
                dve.wait_ge(wkv_step, w + 6)
                dve.reciprocal(den, den).then_inc(wkv_step, 1)
                shared(1)
                dve.wait_ge(ratio_ready, n + 1)
                dve.wait_ge(tr_ready, n + 1)
                dve.scalar_tensor_tensor(out=rw[:, u, :], in0=tr, scalar=1.0, in1=ratio, op0=ALU.add,
                                         op1=ALU.mult).then_inc(rw_ready, 1)
            run_batches(dve, second)

            NJ = B * C

            def je(x):
                return x.rearrange("p (j e) -> p j e", e=E)

            def ej(x):
                return x.rearrange("p (e j) -> p e j", e=E)
            l8j = je(l8_flat)
            mxj = mx[:, :, :].rearrange("p b c -> p (b c)").unsqueeze(2).broadcast_to([P, NJ, E])
            dve.wait_ge(logit_step, 2 * B)
            dve.wait_ge(pool_consts, 6)
            tt(je(rt[:, 0, :]), l8j, mxj, ALU.is_ge)
            stt(je(rt[:, 1, :]), je(rt[:, 0, :]), -float(E), iota_e[:, :].unsqueeze(1).broadcast_to([P, NJ, E]),
                ALU.mult, ALU.add)
            link(dve.tensor_reduce(emin[:, :], je(rt[:, 1, :]), AX, ALU.min))
            oh = rt[:, 0, :]
            tt(je(oh), je(rt[:, 1, :]), emin[:, :].unsqueeze(2).broadcast_to([P, NJ, E]), ALU.is_equal)
            dve.tensor_copy(oh16[:, :], oh).then_inc(oh_ready, 1)
            dve.tensor_copy(strict16[:, :], strict).then_inc(oh_ready, 1)
            dve.memset(ones16[:, :], 1.0).then_inc(oh_ready, 1)
            dve.wait_ge(rank_psum, 1)
            total, until = rt[:, 1, :], rt[:, 2, :]
            link(dve.tensor_copy(ej(total), je(ybank[0][:, NJ * E:2 * NJ * E]).rearrange("p j e -> p e j")))
            link(dve.tensor_tensor_scan(until, run_mask[:, :, :].rearrange("p e j -> p (e j)"), total, 0.0,
                                        ALU.mult, ALU.add))
            tiles, ends, start = etab[:, 0, :], etab[:, 1, :], etab[:, 2, :]
            ts(tiles, ej(until)[:, :, NJ - 1], 1.0 / P, 127.0 / P - 0.498, ALU.mult, ALU.add)
            ts(tiles, tiles, ROUND, -ROUND, ALU.add, ALU.add)
            link(dve.tensor_tensor_scan(ends, ones_e[:, :], tiles, 0.0, ALU.mult, ALU.add))
            tt(start, ends, tiles, ALU.subtract)
            ts(start, start, float(P), None, ALU.mult)
            before = rt[:, 3, :]
            tt(before, until, total, ALU.subtract)
            tt(ej(before), ej(before), start.unsqueeze(2).broadcast_to([P, E, NJ]), ALU.add)
            tt(je(total), ej(before).rearrange("p e j -> p j e"), je(ybank[0][:, 0:NJ * E]), ALU.add)
            tt(je(total), je(total), je(oh), ALU.mult)
            link(dve.tensor_reduce(slot_f[:, :], je(total), AX, ALU.add))
            dve.tensor_copy(slot[:, :], slot_f[:, :]).then_inc(slot_ready, 1)
            for lo, hi in ((0, NT // 2), (NT // 2, NT)):
                tf = tile_f[:, 0:hi - lo, :]
                tt(tf, iota_t[:, lo:hi].unsqueeze(2).broadcast_to([P, hi - lo, E]),
                   ends.unsqueeze(1).broadcast_to([P, hi - lo, E]), ALU.is_ge)
                link(dve.tensor_reduce(tile_n[:, lo:hi], tf, AX, ALU.add))
            ts(tile_n[:, :], tile_n[:, :], float(E - 1), None, ALU.min)
            dve.tensor_copy(tile_e[:, :], tile_n[:, :]).then_inc(slot_ready, 1)

            def step(k, u):
                if live(k, 0):
                    dve.wait_ge(tile_turned, k + 1)
                    if at_least(k, 2):
                        dve.wait_ge(gur_psum, k - 1)
                    dve.tensor_copy(xt_r[:, u, :], zbank[:, u, 0:P]).then_inc(tile_copied, 1)
                if live(k, 1):
                    n = k - 1
                    dve.wait_ge(sil_ready, n + 1)
                    if at_least(n, 2):
                        dve.wait_ge(hr_turned, n - 1)
                    dve.tensor_tensor(h_r[:, 1 - u, :], sil[:, 1 - u, :], glbank[:, 1 - u, F:2 * F],
                                      ALU.mult).then_inc(hr_ready, 1)
                if live(k, 2):
                    n = k - 2
                    dve.wait_ge(hr_turned, n + 1)
                    if at_least(n, 2):
                        dve.wait_ge(y_r_psum, n - 1)
                    dve.tensor_copy(hT_r[:, u, :], ybank[u][:, 0:2 * P]).then_inc(hT_ready, 1)
            run_tiles(dve, step)

            for b in range(B):
                dve.wait_ge(gathered[b % 2], 16 * C * (b // 2 + 1))
                dve.tensor_tensor(tot[:, b % 2, :, :], gat[:, b % 2, :, :], fo[:, b, :, :], ALU.add).then_inc(tot_ready, 1)
                dve.wait_ge(tot_silu, b + 1)
                t = tot[:, b % 2, :, :]
                dve.tensor_tensor(t, t, sa[:, b, :, :], ALU.mult).then_inc(final_step, 1)
                dve.wait_ge(final_step, 3 * b + 1)
                dve.tensor_tensor(x1[:, b, :, :], x1[:, b, :, :], t, ALU.add).then_inc(final_step, 2)



def constants():
    t = np.arange(P)[:, None]
    w = 2 * np.pi * (np.arange(P)[None, :] + 0.5) / (2 * P)

    def comps(a, b, kinds):
        return [kinds[0](a, b), kinds[1](a, b), kinds[2](a, b)]
    out = []
    a, b = np.cos(w * t), -np.sin(w * t)
    out += [a + b, a, b]
    out += [a, b - a, a + b]
    a, b = np.cos(w * (t - P)), -np.sin(w * (t - P))
    out += [a, b - a, a + b]
    c, s = np.cos(w * t).T / P, np.sin(w * t).T / P
    out += [c - s, -s, -c]
    tri = np.ones((P, T))
    tri[:, :P] = np.arange(P)[None, :] >= t
    return np.concatenate(out + [tri, (np.arange(P)[None, :] > t)], axis=1).astype(np.float32)


def laid_out(x):
    f = np.ascontiguousarray

    def modes(name):
        return x[name].transpose(0, 2, 1).reshape(NL * NM, H)
    col = lambda a: np.broadcast_to(a.reshape(-1, 1), (P, 1))
    half_pi = np.full((P, 1), np.pi / 2, np.float32)
    zero = np.zeros((P, 1), np.float32)
    return {
        "modes": f(np.stack([modes("L0_attn_A_re_log"), modes("L0_attn_A_im"), modes("L0_attn_C_re"),
                             modes("L0_attn_C_im")], axis=1)),
        "log_dt": f(x["L0_attn_log_dt"]),
        "const": constants(),
        "ident": np.eye(P, dtype=np.float32),
        "ln_w": f(x["L0_attn_ln_w"]),
        "d_skip": f(x["L0_attn_D_skip"].reshape(1, NL * H)),
        "cols": f(np.concatenate([x["L0_attn_ln_b"].T, x["L1_attn_time_mix"].reshape(P, 1),
                                  x["L1_attn_time_decay"], x["L1_attn_time_first"], zero, half_pi,
                                  col(x["L0_ffn_input_scale"]), col(x["L0_ffn_weight_scale"])]
                                 + [np.kron(np.eye(NL), np.ones((NM, 1))).astype(np.float32), zero], axis=1)),
        "x": f(x["L0_attn_x"].reshape(B, C, P, H).transpose(2, 0, 1, 3)),
        "w_glu": f(x["L0_attn_W_out"].transpose(2, 0, 1)),
        "biases": f(np.concatenate([x["L0_attn_b_out"].reshape(-1), x["L0_ffn_bias"].reshape(-1)])),
        "w8": f(x["L0_ffn_weight_fp8"].T),
        "w_attn": f(np.stack([x[f"L1_attn_W{c}"].T for c in "kvro"], axis=1)),
        "w_gate": f(x["L1_ffn_gate_w"].T),
        "w_sgu": f(np.stack([x["L1_ffn_shared_gate"].T, x["L1_ffn_shared_up"].T], axis=1)),
        "w_sd": f(x["L1_ffn_shared_down"].T.reshape(2, P, H).transpose(1, 0, 2)),
        "w_routed": f(np.concatenate([
            np.stack([x["L1_ffn_r_gate"], x["L1_ffn_r_up"]], 1).transpose(3, 0, 1, 2).reshape(P, -1),
            x["L1_ffn_r_down"].transpose(0, 2, 1).reshape(E, 2, P, H).transpose(2, 0, 1, 3).reshape(P, -1)],
            axis=1)),
    }


def kernel(**inputs):
    import concourse.bacc as bacc
    from concourse.bass_utils import run_bass_kernel_spmd

    nc = bacc.Bacc("TRN2", target_bir_lowering=False, num_devices=1)
    arrays = laid_out({k: np.asarray(v) for k, v in inputs.items()})
    d = {k: nc.dram_tensor(f"in_{k}", a.shape, F32, kind="ExternalInput").ap() for k, a in arrays.items()}
    d["out"] = nc.dram_tensor("out", (P, B, C, H), F32, kind="ExternalOutput").ap()
    build(nc, d)
    r = run_bass_kernel_spmd(nc, [{f"in_{k}": a for k, a in arrays.items()}], core_ids=[0])
    return np.ascontiguousarray(r.results[0]["out"].transpose(1, 2, 0, 3)).reshape(B, T, H)
```

```python
from contextlib import ExitStack

import numpy as np

import concourse.bass as bass
from concourse import mybir

P = 128
ARENA = 28944
B, T, H = 8, 512, 128
C = T // P
NL, NM = 4, 32
NSMALL, NBIG = 32, 16
NPOW = NSMALL + NBIG
QH = 16
NQ = H // QH
NK = 3
E, F = 8, 256
NT = 40
REGION = B * T + P
XROW = H + 1
FMAX8 = 448.0
EPS = 1e-5
TWO_PI = 6.283185
LN2_HI = 0.693145751953125
LN2_LO = float(np.log(2) - 0.693145751953125)
ROUND = 12582912.0
CW = 4 * NK * P + T + P

ALU = mybir.AluOpType
ACT = mybir.ActivationFunctionType
AX = mybir.AxisListType.X
F32R = mybir.dt.float32r
F32, BF16, I32, U32 = mybir.dt.float32, mybir.dt.bfloat16, mybir.dt.int32, mybir.dt.uint32


def ds(i, n=1):
    return bass.ds(i, n)


def build(nc, d):
    with ExitStack() as ctx:
        def sb(name, shape, dt=F32):
            return ctx.enter_context(nc.sbuf_tensor(name, shape, dt))

        def pb(name, shape):
            return ctx.enter_context(nc.psum_tensor(name, shape, F32))

        def sem(name):
            return ctx.enter_context(nc.semaphore(name))

        const = sb("const", [P, CW])
        ident = sb("ident", [P, P])
        spectra = sb("spectra", [P, NL, C, NK, H])
        resp_high = sb("resp_high", [P, NL, T], F32R)
        resp_low = sb("resp_low", [P, NL, T], F32R)
        ident_r = sb("ident_r", [P, P], F32R)
        w_glu = sb("w_glu", [P, NL, 2 * H])
        biases = sb("biases", [3, NL * 2 * H + H], BF16)
        b_glu = biases[:, 0:NL * 2 * H].rearrange("p (l o) -> p l o", l=NL)
        b_ffn = biases[:, NL * 2 * H:]
        ones3 = sb("ones3", [3, P], BF16)
        w8 = sb("w8", [P, H])
        w_attn = sb("w_attn", [P, 4, H])
        w_gate = sb("w_gate", [P, E])
        w_sgu = sb("w_sgu", [P, 2, F])
        w_sd = sb("w_sd", [P, 2, H])
        routed = sb("routed", [P, E * (2 * F + 2 * H)])
        cols = sb("cols", [P, 16])
        arena = sb("arena", [P, ARENA])

        fwd = [const[:, k * P:(k + 1) * P] for k in range(3)]
        ker = const[:, 3 * P:6 * P].rearrange("p (k f) -> p k f", k=NK)
        ker2 = const[:, 6 * P:9 * P].rearrange("p (k f) -> p k f", k=NK)
        inv = const[:, 9 * P:12 * P].rearrange("p (k t) -> p k t", k=NK)
        tri = const[:, 12 * P:12 * P + T]
        strict = const[:, 12 * P + T:12 * P + T + P]

        class Carve:
            def __init__(self, at):
                self.at = at

            def __call__(self, *shape):
                n = int(np.prod(shape))
                v = arena[:, self.at:self.at + n]
                self.at += n
                assert self.at <= ARENA
                if len(shape) == 1:
                    return v
                names = [chr(97 + i) for i in range(len(shape))]
                return v.rearrange(f"p ({' '.join(names)}) -> p {' '.join(names)}",
                                   **dict(zip(names, shape)))

        cut = Carve(0)
        decay = cut(H, NPOW)
        turns = cut(2, QH, NPOW)
        part = cut(2, QH, NPOW)
        apart = cut(2, QH, NPOW)
        sines = cut(2, QH, NPOW)
        cosines = cut(2, QH, NPOW)
        pow_re = cut(2, QH, NPOW)
        pow_im = cut(2, QH, NPOW)
        vt = cut(4, QH, NBIG)
        v_re = cut(2, QH, NBIG)
        v_im = cut(2, QH, NBIG)
        vbd_re = cut(2, QH, NL, NBIG)
        vbd_im = cut(2, QH, NL, NBIG)
        iota = cut(NPOW)
        spectra_flat = spectra[:, :, :, :, :].rearrange("p a b c d -> p (a b c d)")
        small = spectra_flat[:, 0:22 * H].rearrange("p (a h) -> p a h", h=H)
        raw = spectra_flat[:, 22 * H:27 * H].rearrange("p (a h) -> p a h", h=H)
        d_row = spectra_flat[0:1, 27 * H:31 * H]
        kgen_end = max(cut.at, ARENA - 2 * NL * C * H)
        cut = Carve(kgen_end)
        taps = cut(NL, C, H)
        taps_w = cut(NL, C, H)
        ln_w_rows = sb("ln_w_rows", [P, NL, H])
        NBIAS = NL * 2 * H + H
        biases_raw = routed[0:3, B * T:B * T + NBIAS]
        angles = arena[0:3, H * NPOW:H * NPOW + 4 * NBIAS]
        bsp = angles[:, 0:2 * NBIAS].rearrange("p (u n) -> p u n", u=2)
        bsp16 = angles[:, 2 * NBIAS:4 * NBIAS].bitcast(BF16).rearrange("p (u n) -> p u n", u=4)
        assert 4 * NBIAS <= 3 * 2 * QH * NPOW

        cut = Carve(0)
        x_in = routed[:, 0:B * T].rearrange("p (b c h) -> p b c h", b=B, c=C)
        x_again = cut(B, C, H)
        h = cut(B, C, H)
        g0 = cut(B, C, H)
        zn = cut(2, C, H)
        acc = cut(2, NK, C * H)
        tmp = cut(NK * H * 6)
        y = cut(2, T)
        th = cut(2, C, H)
        prod = cut(2, C, H)
        q8_at = cut.at
        q8 = cut(T)
        q8s = cut(T)
        q8r = cut(2, T)
        q8T = cut(2, T)
        th8 = th
        idle = sb("idle", [P, 4])
        assert cut.at <= kgen_end
        tmps, at = [None], 0
        for dist in range(1, C):
            n = (C - dist) * H
            tmps.append(tmp[:, at:at + NK * n].rearrange("p (k n) -> p k n", k=NK))
            at += NK * n
        stats = sb("stats", [P, 2, C, 6])
        rs = sb("rs", [P, 2, 8, C])
        pconst = sb("pconst", [P, 7, C])

        x1 = x_again
        sa = g0
        fo = h
        cut = Carve(q8_at)
        sg = cut(T)
        xn1 = cut(2, C, H)
        xT = cut(2, T)
        xm = cut(T)
        xs = cut(2, C, XROW)
        moe_at = cut.at
        cut = Carve(3 * B * T)
        kmin = cut(T)
        ek = cut(T)
        kv = cut(T)
        s_num = cut(T + 1)
        s_den = cut(T + 1)
        num = cut(T)
        den = cut(T)
        ratio = cut(T)
        rw = cut(2, T)
        tr = cut(T)
        tg = cut(T)
        sl = cut(T)
        hs = cut(2, 2, T)
        assert cut.at <= q8_at
        tile_tmp = spectra_flat[:, 0:2 * NT * E].rearrange("p (a t e) -> p a t e", a=2, e=E)
        cut = Carve(moe_at)
        sil = cut(2, F)
        h_r = cut(2, F)
        xt_r = cut(2, P)
        hT_r = cut(2, 2 * P)
        xtok = cut(4, XROW)
        ytok = cut(4, P)
        gat = Carve(3 * B * T)(B, C, H)
        assert 4 * B * T <= moe_at
        lt = sb("lt", [P, C, E])
        pick = sb("pick", [P, C, E])
        oh16 = sb("oh16", [P, C * E], BF16)
        cum16 = sb("cum16", [P, E], BF16)
        count = sb("count", [P, E])
        place = sb("place", [P, C, E])
        region = sb("region", [P, E])
        id_f = sb("id_f", [P, B * C])
        ids = sb("ids", [P, 8], U32)
        shift = sb("shift", [P, 8])
        own_rows = sb("own_rows", [P, NT])
        blank = sb("blank", [P, XROW])
        strict16 = sb("strict16", [P, P], BF16)
        ones16 = sb("ones16", [P, P], BF16)
        etab = sb("etab", [P, 4, E])
        mx = sb("mx", [P, 2, C])
        emin = sb("emin", [P, C])
        sc = sb("sc", [P, 2, 2, C])
        slot_f = sb("slot_f", [P, C])
        slot = sb("slot", [P, 2, C], U32)
        tile_n = sb("tile_n", [P, NT])
        tile_s = sb("tile_s", [P, NT])
        tile_e = sb("tile_e", [P, NT], I32)
        tile_row = sb("tile_row", [P, NT], I32)
        blank_row = sb("blank_row", [P, E], I32)
        iota_e = sb("iota_e", [P, E])
        iota_t = sb("iota_t", [P, NT])
        ones_e = sb("ones_e", [P, E])
        dcol = sb("dcol", [P, 4])

        zbank = pb("zbank", [P, NK, T])
        glbank = pb("glbank", [P, 2, T])
        ybank = [pb("ybank0", [P, T]), pb("ybank1", [P, T])]
        xbank = pb("xbank", [P, T])

        x_sorted = nc.dram_tensor("x_sorted", [E * REGION + P, XROW], F32).ap()
        y_routed = nc.dram_tensor("y_routed", [B * T + NT * P, H], F32).ap()

        modes_in = sem("modes_in")
        const_in = sem("const_in")
        rows_in = sem("rows_in")
        wts_in = sem("wts_in")
        x_in_s = sem("x_in_s")
        iota_ready = sem("iota_ready")
        dve_chain = sem("dve_chain")
        pool_chain = sem("pool_chain")
        decay_ready = sem("decay_ready")
        decay_exp = sem("decay_exp")
        small_sin = sem("small_sin")
        turns_ready = sem("turns_ready")
        part_ready = sem("part_ready")
        sines_ready = sem("sines_ready")
        pow_ready = sem("pow_ready")
        pow_im_ready = sem("pow_im_ready")
        v_ready = sem("v_ready")
        vbd_re_ready = sem("vbd_re_ready")
        vbd_im_ready = sem("vbd_im_ready")
        taps_psum = sem("taps_psum")
        taps_ready = sem("taps_ready")
        tapsw_ready = sem("tapsw_ready")
        spec_psum = sem("spec_psum")
        spec_ready = sem("spec_ready")
        resp_psum = sem("resp_psum")
        resp_ready = sem("resp_ready")
        resp_split = sem("resp_split")
        ident_ready = sem("ident_ready")
        kgen_idle = sem("kgen_idle")
        xstats = sem("xstats")
        xrstd = sem("xrstd")
        x_norm = sem("x_norm")
        q8_ready = sem("q8_ready")
        q8_turned = sem("q8_turned")
        q8T_ready = sem("q8T_ready")
        ffn_psum = sem("ffn_psum")
        ffn_tanh = sem("ffn_tanh")
        g0_ready = sem("g0_ready")
        lstats = sem("lstats")
        lrstd = sem("lrstd")
        zn_ready = sem("zn_ready")
        z_ready = sem("z_ready")
        conv_step = sem("conv_step")
        far_step = sem("far_step")
        y_psum = sem("y_psum")
        y_ready = sem("y_ready")
        glu_psum = sem("glu_psum")
        glu_tanh = sem("glu_tanh")
        glu_ready = sem("glu_ready")
        h_ready = sem("h_ready")
        blanks_out = sem("blanks_out")
        routed_in = sem("routed_in")
        x_again_in = sem("x_again_in")
        out_s = sem("out_s")
        small_w = sem("small_w")
        x1_step = sem("x1_step")
        nstats = sem("nstats")
        nrstd = sem("nrstd")
        xn1_ready = sem("xn1_ready")
        xn1_turned = sem("xn1_turned")
        xT_ready = sem("xT_ready")
        xm_step = sem("xm_step")
        kvr_psum = sem("kvr_psum")
        kmin_ready = sem("kmin_ready")
        ek_ready = sem("ek_ready")
        tr_ready = sem("tr_ready")
        logit_psum = sem("logit_psum")
        place_step = sem("place_step")
        mx_tanh = sem("mx_tanh")
        sc_ready = sem("sc_ready")
        xs_ready = sem("xs_ready")
        gu_psum = sem("gu_psum")
        tg_ready = sem("tg_ready")
        ffn_step = sem("ffn_step")
        wkv_step = sem("wkv_step")
        ratio_ready = sem("ratio_ready")
        rw_ready = sem("rw_ready")
        attn_psum = sem("attn_psum")
        sa_ready = sem("sa_ready")
        down_psum = sem("down_psum")
        fo_ready = sem("fo_ready")
        w_half = sem("w_half")
        masks_ready = sem("masks_ready")
        rank_psum = sem("rank_psum")
        tables_ready = sem("tables_ready")
        pool_consts = sem("pool_consts")
        scattered = [sem(f"scattered_{u}") for u in range(2)]
        tiles_in = [sem(f"tiles_in_{u}") for u in range(4)]
        ids_ready = sem("ids_ready")
        tile_turned = sem("tile_turned")
        tile_copied = sem("tile_copied")
        gur_psum = sem("gur_psum")
        sil_ready = sem("sil_ready")
        hr_ready = sem("hr_ready")
        hr_turned = sem("hr_turned")
        hT_ready = sem("hT_ready")
        y_r_psum = sem("y_r_psum")
        ytok_ready = sem("ytok_ready")
        stored = [sem(f"stored_{u}") for u in range(4)]
        routed_back = [sem(f"routed_back_{b}") for b in range(B)]
        tot_ready = sem("tot_ready")
        tot_silu = sem("tot_silu")
        gated = sem("gated")
        final_step = sem("final_step")
        dcols = sem("dcols")

        RSTD = 11
        WKV = 7
        PLACE = 12
        CONV = 5

        block = ctx.enter_context(nc.Block())

        PIECES = [(l, k) for l in range(1, NL) for k in range(NK + 1)]
        NEARLY = 2

        def pieces_at(n):
            i = NEARLY + 2 * n
            return PIECES[i:i + 1], PIECES[i + 1:i + 2]

        def before_vbd(eng, q):
            eng.wait_ge(v_ready, 2 * (q + 1))
            if q >= 2:
                eng.wait_ge(taps_psum, q - 1)

        par = {}

        def k_par(k):
            return par["u"]

        def run_steps(eng, step):
            for k in range(4):
                par["u"] = k % 2
                step(k)
            with eng.Fori(2, NL * B // 2 - 2) as i:
                for u in range(2):
                    par["u"] = u
                    step(2 * i + u)
            for k in range(NL * B - 4, NL * B + 2):
                par["u"] = k % 2
                step(k)

        def behind(k, back):
            return not isinstance(k, int) or 0 <= k - back < NL * B

        def ahead(k, more):
            return not isinstance(k, int) or k + more < NL * B

        def of(n, t):
            return t[:, n // B] if isinstance(n, int) else t[:, ds(n // B)].squeeze(1)

        def run_batches(eng, batch):
            batch(0, 0)
            batch(1, 1)
            with eng.Fori(1, B // 2 - 1) as i:
                for u in range(2):
                    batch(2 * i + u, u)
            batch(B - 2, 0)
            batch(B - 1, 1)

        def follows(n, ahead):
            return not isinstance(n, int) or n + ahead < B

        def run_tiles(eng, step):
            def at(k, u, quarters):
                step(k, u, lambda back: quarters + (u - back) // 4)
            for k in range(8):
                at(k, k, 0)
            with eng.Fori(0, (NT - 8) // 16) as i:
                for u in range(16):
                    at(16 * i + 8 + u, u, 4 * i + 2)
            for k in range(NT, NT + 4):
                at(k, k - NT, NT // 4)

        def live(k, back):
            return not isinstance(k, int) or 0 <= k - back < NT

        def at_least(n, v):
            return not isinstance(n, int) or n >= v

        @block.sync
        def _(sp):
            sp.dma_start(raw[:, 1:5, :], d["modes"]).then_inc(modes_in, 16)
            for l in range(NL):
                sp.dma_start(raw[NM * l:NM * (l + 1), 0, :],
                             d["log_dt"][l:l + 1, :].partition_broadcast(NM)).then_inc(modes_in, 16)
            sp.dma_start(const[:, :], d["const"]).then_inc(const_in, 16)
            sp.dma_start(ident[:, :], d["ident"]).then_inc(const_in, 16)
            sp.dma_start(ln_w_rows[:, :, :], d["ln_w"].partition_broadcast(P)).then_inc(rows_in, 16)
            sp.dma_start(d_row, d["d_skip"]).then_inc(rows_in, 16)
            sp.dma_start(cols[:, :], d["cols"]).then_inc(rows_in, 16)
            sp.dma_start(x_in, d["x"]).then_inc(x_in_s, 16)
            sp.dma_start(w_glu[:, :, :], d["w_glu"]).then_inc(wts_in, 16)
            sp.dma_start(biases_raw, d["biases"].partition_broadcast(3)).then_inc(wts_in, 16)
            sp.dma_start(w8[:, :], d["w8"]).then_inc(wts_in, 16)
            sp.dma_start(w_attn[:, :, :], d["w_attn"]).then_inc(wts_in, 16)
            sp.dma_start(w_gate[:, :], d["w_gate"]).then_inc(wts_in, 16)
            sp.dma_start(w_sgu[:, :, :], d["w_sgu"]).then_inc(wts_in, 16)
            sp.dma_start(w_sd[:, :, :], d["w_sd"]).then_inc(wts_in, 16)
            sp.wait_ge(kgen_idle, 1)
            sp.dma_start(x_again, d["x"]).then_inc(x_again_in, 16)
            sp.wait_ge(pool_consts, 8)
            sp.dma_start(x_sorted[E * REGION:, :], blank[:, :]).then_inc(blanks_out, 16)
            sp.wait_ge(g0_ready, B)
            sp.dma_start(routed[:, :], d["w_routed"]).then_inc(routed_in, 16)
            sp.wait_ge(tables_ready, 3)
            for e in range(0, E, 2):
                row = sp.value_load(blank_row[0:1, e:e + 1], min_val=0, max_val=E * REGION - P)
                sp.dma_start(x_sorted[ds(row, P), :], blank[:, :]).then_inc(blanks_out, 16)
            sp.wait_ge(blanks_out, 16 * (E + 1))
            for u in range(2):
                sp.wait_ge(scattered[u], 16 * C * B // 2)

            for k in range(NT):
                row = sp.value_load(tile_row[0:1, k:k + 1], min_val=0, max_val=E * REGION)
                if k >= 4:
                    sp.wait_ge(tile_turned, k - 3)
                    sp.wait_ge(ids_ready, 2 * (k - 3))
                sp.dma_start(xtok[:, k % 4, :], x_sorted[ds(row, P), :]).then_inc(tiles_in[k % 4], 16)
            for u in range(4):
                sp.wait_ge(stored[u], 16 * NT // 4)
            for b in range(B):
                sp.dma_start(gat[:, b, :, :], y_routed[b * T:(b + 1) * T, :].rearrange("(c p) h -> p c h", p=P))\
                    .then_inc(routed_back[b], 16)
            for b in range(B):
                sp.wait_ge(final_step, b + 1)
                sp.dma_start(d["out"][:, b, :, :], x1[:, b, :, :]).then_inc(out_s, 16)
            sp.wait_ge(out_s, 16 * B)

        @block.gpsimd
        def _(pool):
            pool.iota(iota[:, 0:NSMALL], pattern=[[1, NSMALL]], base=0, channel_multiplier=0,
                      allow_small_or_imprecise_dtypes=True).then_inc(iota_ready, 1)
            pool.iota(iota[:, NSMALL:NPOW], pattern=[[1, NBIG]], base=0, channel_multiplier=0,
                      allow_small_or_imprecise_dtypes=True).then_inc(iota_ready, 1)
            for m, value in enumerate((-0.5, H / 4, H * EPS, H ** 0.5, -0.5 * H ** 0.5, 0.5, 1.0)):
                pool.memset(pconst[:, m, :], value).then_inc(iota_ready, 1)
            pool.memset(vbd_re, 0.0).then_inc(iota_ready, 1)
            pool.memset(blank[:, 0:H], 0.0).then_inc(pool_consts, 1)
            pool.iota(blank[:, H:XROW], pattern=[[1, 1]], base=B * T, channel_multiplier=1,
                      allow_small_or_imprecise_dtypes=True).then_inc(pool_consts, 1)
            pool.iota(id_f[:, :], pattern=[[P, B * C]], base=0, channel_multiplier=1,
                      allow_small_or_imprecise_dtypes=True).then_inc(pool_consts, 1)
            pool.iota(region[:, :], pattern=[[REGION, E]], base=0, channel_multiplier=0,
                      allow_small_or_imprecise_dtypes=True).then_inc(pool_consts, 1)
            pool.iota(iota_e[:, :], pattern=[[1, E]], base=0, channel_multiplier=0,
                      allow_small_or_imprecise_dtypes=True).then_inc(pool_consts, 1)
            pool.iota(iota_t[:, :], pattern=[[1, NT]], base=0, channel_multiplier=0,
                      allow_small_or_imprecise_dtypes=True).then_inc(pool_consts, 1)
            pool.memset(ones_e[:, :], 1.0).then_inc(pool_consts, 1)
            pool.iota(own_rows[:, :], pattern=[[P, NT]], base=0, channel_multiplier=0,
                      allow_small_or_imprecise_dtypes=True).then_inc(pool_consts, 1)
            pool.memset(ones3[:, :], 1.0).then_inc(iota_ready, 1)
            pool.wait_ge(iota_ready, 11)
            def turns_of(q):
                u = q % 2
                if q >= 2:
                    pool.wait_ge(part_ready, 2 * (q - 1))
                for j, (lo, n) in enumerate(((0, NSMALL), (NSMALL, NBIG))):
                    rate = small[:, 3 + j, QH * q:QH * (q + 1)]
                    pool.tensor_tensor(turns[:, u, :, lo:lo + n],
                                       rate.unsqueeze(2).broadcast_to([P, QH, n]),
                                       iota[:, lo:lo + n].unsqueeze(1).broadcast_to([P, QH, n]),
                                       ALU.mult).then_inc(turns_ready, 1)
            pool.wait_ge(decay_ready, 1)
            turns_of(0)
            for half in range(2):
                cs = slice(half * H // 2, (half + 1) * H // 2)
                for j, (lo, n) in enumerate(((0, NSMALL), (NSMALL, NBIG))):
                    pool.tensor_tensor(decay[:, cs, lo:lo + n],
                                       small[:, 1 + j, cs].unsqueeze(2).broadcast_to([P, H // 2, n]),
                                       iota[:, lo:lo + n].unsqueeze(1).broadcast_to([P, H // 2, n]),
                                       ALU.mult).then_inc(pool_chain, 1)
            turns_of(1)
            pool.wait_ge(rows_in, 48)
            def imaginary_powers(q):
                u = q % 2
                pool.wait_ge(sines_ready, 2 * (q + 1))
                pool.wait_ge(decay_exp, 2)
                if q >= 2:
                    pool.wait_ge(taps_psum, q - 1)
                    pool.wait_ge(v_ready, 2 * (q - 1))
                pool.tensor_tensor(pow_im[:, u, :, :], decay[:, QH * q:QH * (q + 1), :], sines[:, u, :, :],
                                   ALU.mult).then_inc(pow_im_ready, 1)
            imaginary_powers(0)
            for q in range(NQ):
                if q + 2 < NQ:
                    turns_of(q + 2)
                before_vbd(pool, q)
                shape = [P, QH, NL, NBIG]
                pool.tensor_tensor(vbd_im[:, q % 2, :, :, :], v_im[:, q % 2, :, :].unsqueeze(2).broadcast_to(shape),
                                   cols[:, 11:11 + NL].unsqueeze(1).unsqueeze(3).broadcast_to(shape),
                                   ALU.mult).then_inc(vbd_im_ready, 1)
                if q + 1 < NQ:
                    imaginary_powers(q + 1)

            def rstd(stat, done, n, u):
                even, odd = stats[:, u, :, 1], stats[:, u, :, 4]
                even2, odd2 = stats[:, u, :, 2], stats[:, u, :, 5]
                r = [rs[:, u, m, :] for m in range(8)]
                w = RSTD * n
                pool.wait_ge(stat, C * (n + 1))
                pool.tensor_tensor(r[2], even, odd, ALU.add).then_inc(done, 1)
                pool.tensor_tensor(r[3], even, odd, ALU.subtract).then_inc(done, 1)
                pool.tensor_tensor(r[4], even2, odd2, ALU.add).then_inc(done, 1)
                pool.wait_ge(done, w + 3)
                pool.tensor_tensor(r[5], r[3], r[3], ALU.mult).then_inc(done, 1)
                pool.wait_ge(done, w + 4)
                pool.tensor_tensor(r[6], r[5], pconst[:, 1, :], ALU.mult).then_inc(done, 1)
                pool.wait_ge(done, w + 5)
                pool.tensor_tensor(r[7], r[6], r[4], ALU.add).then_inc(done, 1)
                pool.wait_ge(done, w + 6)
                pool.tensor_tensor(r[3], r[7], pconst[:, 2, :], ALU.add).then_inc(done, 1)
                pool.wait_ge(done, w + 7)
                pool.tensor_tensor(r[4], r[3], pconst[:, 0, :], ALU.pow).then_inc(done, 1)
                pool.wait_ge(done, w + 8)
                pool.tensor_tensor(r[5], r[4], r[2], ALU.mult).then_inc(done, 1)
                pool.tensor_tensor(r[0], r[4], pconst[:, 3, :], ALU.mult).then_inc(done, 1)
                pool.wait_ge(done, w + 9)
                pool.tensor_tensor(r[1], r[5], pconst[:, 4, :], ALU.mult).then_inc(done, 1)

            with pool.Fori(0, B // 2) as i:
                for u in range(2):
                    rstd(xstats, xrstd, 2 * i + u, u)

            def first_residual(n):
                pool.wait_ge(h_ready, B + (NL - 1) * B + n + 1)
                if at_least(n, 1):
                    pool.wait_ge(x1_step, 2 * n)
                else:
                    pool.wait_ge(x_again_in, 16)
                hb, gb, xb = (t[:, n, :, :] if isinstance(n, int) else t[:, ds(n), :, :].squeeze(1) for t in (h, g0, x1))
                sgc = sg.rearrange("p (c h) -> p c h", c=C)
                pool.tensor_tensor(sgc, hb, gb, ALU.mult).then_inc(x1_step, 1)
                pool.wait_ge(x1_step, 2 * n + 1)
                pool.tensor_tensor(xb, xb, sgc, ALU.add).then_inc(x1_step, 1)

            def step(k):
                u = k_par(k)
                if ahead(k, 0):
                    pool.wait_ge(conv_step, CONV * k + 2)
                    two = tmps[2][:, :, H:2 * H]
                    pool.tensor_tensor(two, two, tmps[3], ALU.add).then_inc(far_step, 1)
                    pool.wait_ge(conv_step, CONV * k + 3)
                    pool.wait_ge(far_step, 2 * k + 1)
                    one = tmps[1][:, :, H:3 * H]
                    pool.tensor_tensor(one, one, tmps[2], ALU.add).then_inc(far_step, 1)
                if ahead(k, 2):
                    pool.wait_ge(zn_ready, C * (k + 1))
                    rstd(lstats, lrstd, k + 2, u)
                elif k + 2 - NL * B < 2:
                    pool.wait_ge(zn_ready, C * (k + 1))
                    rstd(nstats, nrstd, k + 2 - NL * B, u)
                if behind(k, 2):
                    n = k - 2
                    pool.wait_ge(glu_ready, n + 1)
                    hb = h[:, ds(n % B), :, :].squeeze(1) if not isinstance(n, int) else h[:, n % B, :, :]
                    pool.tensor_tensor(hb, hb, prod[:, u, :, :], ALU.add).then_inc(h_ready, 1)
                if not ahead(k, 4) and ahead(k, 2):
                    first_residual(k - (NL * B - 4))
            for n in range(2):
                rstd(lstats, lrstd, n, n)
            run_steps(pool, step)
            first_residual(2)

            def scaled(n, u):
                pool.wait_ge(mx_tanh, n + 1)
                pool.tensor_tensor(sc[:, u, 1, :], sc[:, u, 0, :], pconst[:, 5, :], ALU.mult).then_inc(sc_ready, 1)
                pool.wait_ge(sc_ready, 2 * n + 1)
                pool.tensor_tensor(sc[:, u, 1, :], sc[:, u, 1, :], pconst[:, 5, :], ALU.add).then_inc(sc_ready, 1)
                pool.wait_ge(sc_ready, 2 * n + 2)
                if at_least(n, 2):
                    pool.wait_ge(scattered[u], 16 * C * (n // 2))
                    pool.wait_ge(xs_ready, 2 * (n - 1))
                pool.tensor_tensor(xs[:, u, :, 0:H], xn1[:, u, :, :],
                                   sc[:, u, 1, :].unsqueeze(2).broadcast_to([P, C, H]), ALU.mult).then_inc(xs_ready, 1)
                pool.tensor_tensor(xs[:, u, :, H], id_f[:, ds(n * C, C)], pconst[:, 6, :], ALU.mult).then_inc(xs_ready, 1)

            def scatter(n, u):
                pool.wait_ge(place_step, PLACE * (n + 1))
                pool.wait_ge(xs_ready, 2 * (n + 1))
                for c in range(C):
                    pool.indirect_dma_start(x_sorted, bass.IndirectOffsetOnAxis(ap=slot[:, u, c:c + 1], axis=0),
                                            xs[:, u, c, :], None).then_inc(scattered[u], 16)
            scaled(0, 0)

            for n in range(B):
                u = n % 2
                if n + 2 < B:
                    rstd(nstats, nrstd, n + 2, u)
                scatter(n, u)
                if n + 1 < B:
                    scaled(n + 1, 1 - u)
                pool.wait_ge(wkv_step, WKV * (n + 1))
                pool.tensor_tensor(ratio, num, den, ALU.mult).then_inc(ratio_ready, 1)
                if n + 3 < B:
                    first_residual(n + 3)

            for n in range(NT):
                pool.wait_ge(ytok_ready, n + 1)
                pool.wait_ge(ids_ready, 2 * (n + 1))
                pool.indirect_dma_start(y_routed, bass.IndirectOffsetOnAxis(ap=ids[:, n % 8:n % 8 + 1], axis=0),
                                        ytok[:, n % 4, :], None).then_inc(stored[n % 4], 16)
            for b in range(B):
                pool.wait_ge(gated, b + 1)
                pool.tensor_tensor(x1[:, b, :, :], x1[:, b, :, :], gat[:, b, :, :], ALU.add).then_inc(final_step, 1)

        @block.scalar
        def _(act):
            act.wait_ge(rows_in, 48)
            act.activation(dcol[:, 0:1], cols[:, 5:6], ACT.Exp).then_inc(dcols, 1)
            act.activation(dcol[:, 2:3], cols[:, 6:7], ACT.Exp).then_inc(dcols, 1)
            act.wait_ge(dcols, 1)
            act.activation(dcol[:, 1:2], dcol[:, 0:1], ACT.Exp, scale=-1.0).then_inc(dcols, 1)
            act.wait_ge(decay_ready, 1)
            act.activation(small[:, 9, :], small[:, 3, :], ACT.Sin, scale=TWO_PI).then_inc(small_sin, 1)
            act.activation(small[:, 10, :], small[:, 3, :], ACT.Sin, scale=TWO_PI / 2).then_inc(small_sin, 1)

            def sines_of(q):
                u = q % 2
                act.wait_ge(part_ready, 2 * (q + 1))
                if q >= 2:
                    act.wait_ge(pow_ready, q - 1)
                    act.wait_ge(pow_im_ready, q - 1)
                act.activation(sines[:, u, :, :], part[:, u, :, :], ACT.Sin, scale=TWO_PI).then_inc(sines_ready, 1)
                act.activation(cosines[:, u, :, :], apart[:, u, :, :], ACT.Sin, scale=-TWO_PI,
                               bias=cols[:, 8:9]).then_inc(sines_ready, 1)
            sines_of(0)
            for half in range(2):
                act.wait_ge(pool_chain, 2 * (half + 1))
                dh = decay[:, half * H // 2:(half + 1) * H // 2, :]
                act.activation(dh, dh, ACT.Exp, scale=-1.0).then_inc(decay_exp, 1)

            def evacuate_taps(q):
                u = q % 2
                bank = (zbank if u == 0 else glbank)[0:NSMALL, 0:2, :]\
                    .rearrange("p a (h l d j) -> p (l d) (a h) j", l=NL, d=C, j=C, h=QH // 2)
                act.wait_ge(taps_psum, q + 1)
                for j in range(C):
                    out = taps[NSMALL * j:NSMALL * (j + 1), :, :, QH * q:QH * (q + 1)]\
                        .rearrange("p l d h -> p (l d) h")
                    nc.scalar.copy(out, bank[:, :, :, j]).then_inc(taps_ready, 1)

            def real_blocks(q):
                before_vbd(act, q)
                for l in range(NL):
                    rows = slice(NM * l, NM * (l + 1))
                    nc.scalar.copy(vbd_re[rows, q % 2, :, l, :], v_re[rows, q % 2, :, :]).then_inc(vbd_re_ready, 1)

            for q in range(NQ):
                if q >= 1:
                    sines_of(q)
                    real_blocks(q - 1)
                if q >= 2:
                    evacuate_taps(q - 2)
            real_blocks(NQ - 1)
            evacuate_taps(NQ - 2)
            evacuate_taps(NQ - 1)

            def take_piece(l, k):
                if k < NK:
                    act.wait_ge(spec_psum, NK * l + k + 1)
                    nc.scalar.copy(spectra[:, l, :, k, :], zbank[:, k, :].rearrange("p (d h) -> p d h", d=C))\
                        .then_inc(spec_ready, 1)
                else:
                    act.wait_ge(resp_psum, l + 1)
                    act.activation(resp_high[:, l, :], ybank[1][:, :], ACT.Identity,
                                   scale=cols[:, l:l + 1]).then_inc(resp_ready, 1)

            def normalize(out, src, u, done):
                for c in range(C):
                    act.activation(out[:, c, :], src[:, c, :], ACT.Identity, scale=rs[:, u, 0, c:c + 1],
                                   bias=rs[:, u, 1, c:c + 1]).then_inc(done[c == C - 1], 1)

            def x_norm_of(n, u):
                act.wait_ge(xrstd, RSTD * (n + 1))
                normalize(h[:, ds(n), :, :].squeeze(1), x_in[:, ds(n), :, :].squeeze(1), u, (x_norm, h_ready))

            def make_zn(n, u):
                act.wait_ge(lrstd, RSTD * (n + 1))
                if not isinstance(n, int) or n >= 2:
                    act.wait_ge(z_ready, n - 1)
                hb = h[:, ds(n % B), :, :].squeeze(1) if not isinstance(n, int) else h[:, n % B, :, :]
                normalize(zn[:, u, :, :], hb, u, (zn_ready, zn_ready))

            def x_part(n, u, more, pieces=((), ())):
                if more:
                    x_norm_of(n + 1, 1 - u)
                else:
                    make_zn(0, 0)
                act.wait_ge(q8_turned, n + 1)
                nc.scalar.copy(q8T[:, u, :], ybank[0][:, :]).then_inc(q8T_ready, 1)
                for piece in pieces[0]:
                    take_piece(*piece)
                act.wait_ge(ffn_psum, n + 1)
                act.activation(th8[:, u, :, :], xbank[:, :].rearrange("p (c h) -> p c h", c=C),
                               ACT.Tanh).then_inc(ffn_tanh, 1)
                for piece in pieces[1]:
                    take_piece(*piece)
            act.wait_ge(kgen_idle, 1)
            x_norm_of(0, 0)
            for k in range(NK + 1):
                take_piece(0, k)
            for piece in PIECES[:NEARLY]:
                take_piece(*piece)
            for n in range(B):
                x_part(n, n % 2, n + 1 < B, pieces_at(n))


            def norm1(n, u):
                act.wait_ge(nrstd, RSTD * (n + 1))
                if at_least(n, 2):
                    act.wait_ge(xs_ready, 2 * (n - 1))
                normalize(xn1[:, u, :, :], x1[:, ds(n), :, :].squeeze(1), u, (xn1_ready, xn1_ready))

            def take_turned(n, u):
                act.wait_ge(xn1_turned, n + 1)
                nc.scalar.copy(xT[:, u, :], ybank[0][:, :]).then_inc(xT_ready, 1)

            def step(k):
                u = k_par(k)
                if ahead(k, 1):
                    make_zn(k + 1, 1 - u)
                elif k + 1 - NL * B < 2:
                    norm1(k + 1 - NL * B, 1 - u)
                if behind(k, 1):
                    n = k - 1
                    act.wait_ge(y_psum, n + 1)
                    if not (isinstance(n, int) and n < 2):
                        act.wait_ge(glu_psum, n - 1)
                    act.activation(y[:, 1 - u, :], ybank[1 - u][:, :], ACT.Gelu_apprx_tanh).then_inc(y_ready, 1)
                if behind(k, 2):
                    n = k - 2
                    act.wait_ge(glu_psum, n + 1)
                    if not (isinstance(n, int) and n < 2):
                        act.wait_ge(glu_ready, n - 1)
                    act.activation(th[:, u, :, :],
                                   glbank[:, :, :].rearrange("p a (c o) -> p (a c) o", c=2)[:, :, H:2 * H],
                                   ACT.Tanh, scale=0.5).then_inc(glu_tanh, 1)
                if isinstance(k, int) and k == NL * B:
                    take_turned(0, 0)
            run_steps(act, step)

            def best_tanh(n, u):
                act.wait_ge(place_step, PLACE * n + 2)
                act.activation(sc[:, u, 0, :], mx[:, u, :], ACT.Tanh, scale=0.5).then_inc(mx_tanh, 1)

            def take_outputs(n):
                act.wait_ge(down_psum, n + 1)
                nc.scalar.copy(fo[:, ds(n), :, :].squeeze(1), xbank[:, :].rearrange("p (c h) -> p c h", c=C))\
                    .then_inc(fo_ready, 1)
                act.wait_ge(attn_psum, n + 1)
                nc.scalar.copy(sa[:, ds(n), :, :].squeeze(1), ybank[1][:, :].rearrange("p (c h) -> p c h", c=C))\
                    .then_inc(sa_ready, 1)
            best_tanh(0, 0)
            take_turned(1, 1)

            def second(n, u):
                act.wait_ge(kmin_ready, n + 1)
                if at_least(n, 1):
                    act.wait_ge(wkv_step, WKV * n)
                act.activation(ek, kmin, ACT.Exp).then_inc(ek_ready, 1)
                if at_least(n, 1):
                    act.wait_ge(rw_ready, n)
                act.activation(tr, zbank[:, 2, :], ACT.Tanh, scale=0.5).then_inc(tr_ready, 1)

                def gate_tanh(f):
                    act.wait_ge(gu_psum, 2 * n + f + 1)
                    if f or at_least(n, 1):
                        act.wait_ge(ffn_step, 2 * (2 * n + f))
                    act.activation(tg, glbank[:, 0, :], ACT.Tanh, scale=0.5).then_inc(tg_ready, 1)
                gate_tanh(0)
                if at_least(n, 1):
                    take_outputs(n - 1)
                if follows(n, 1):
                    best_tanh(n + 1, 1 - u)
                if follows(n, 2):
                    norm1(n + 2, u)
                gate_tanh(1)
                if not follows(n, 1):
                    act.wait_ge(tables_ready, 3)
                    for e in range(1, E, 2):
                        row = act.value_load(blank_row[0:1, e:e + 1], min_val=0, max_val=E * REGION - P)
                        act.dma_start(x_sorted[ds(row, P), :], blank[:, :]).then_inc(blanks_out, 16)
                if follows(n, 2):
                    take_turned(n + 2, u)
            run_batches(act, second)
            take_outputs(B - 1)

            def step(k, u, quarter):
                if live(k, 1):
                    n = k - 1
                    act.wait_ge(gur_psum, n + 1)
                    if at_least(n, 2):
                        act.wait_ge(hr_ready, n - 1)
                    act.activation(sil[:, (u - 1) % 2, :], glbank[:, (u - 1) % 2, 0:F], ACT.Silu).then_inc(sil_ready, 1)
                if live(k, 4):
                    n = k - 4
                    act.wait_ge(y_r_psum, n + 1)
                    if at_least(n, 4):
                        act.wait_ge(stored[u % 4], 16 * quarter(4))
                    nc.scalar.copy(ytok[:, u % 4, :], (xbank[:, 0:P] if u % 2 else zbank[:, 2, 0:P])).then_inc(ytok_ready, 1)
            run_tiles(act, step)
            for b in range(B):
                act.wait_ge(tot_ready, b + 1)
                act.activation(gat[:, b, :, :], gat[:, b, :, :], ACT.Silu).then_inc(tot_silu, 1)

        @block.tensor
        def _(pe):
            pe.wait_ge(const_in, 32)
            for q in range(NQ):
                u = q % 2
                bank = (zbank if u == 0 else glbank)[0:NSMALL, 0:2, :]\
                    .rearrange("p a (h n) -> p (a h) n", n=NL * NBIG)
                pe.wait_ge(pow_ready, q + 1)
                pe.wait_ge(pow_im_ready, q + 1)
                pe.wait_ge(vbd_re_ready, NL * (q + 1))
                pe.wait_ge(vbd_im_ready, q + 1)
                if q >= 2:
                    pe.wait_ge(taps_ready, C * (q - 1))
                for c in range(QH):
                    pe.matmul(bank[:, c, :], pow_re[:, u, c, 0:NSMALL], vbd_re[:, u, c, :, :],
                              start=True, stop=False)
                    mm = pe.matmul(bank[:, c, :], pow_im[:, u, c, 0:NSMALL], vbd_im[:, u, c, :, :],
                                   start=False, stop=True)
                mm.then_inc(taps_psum, 1)
            def piece_of(l, k):
                pe.wait_ge(tapsw_ready, l + 1)
                if k < NK:
                    if l >= 1:
                        pe.wait_ge(spec_ready, NK * (l - 1) + k + 1)
                    pe.matmul(zbank[:, k, :], ker[:, k, :], taps_w[:, l, :, :], start=True, stop=False)
                    pe.matmul(zbank[:, k, H:T], ker2[:, k, :], taps_w[:, l, 0:C - 1, :],
                              start=False, stop=True).then_inc(spec_psum, 1)
                else:
                    if l >= 1:
                        pe.wait_ge(resp_split, l)
                    for c in range(C):
                        mm = pe.matmul(ybank[1][:, c * P:T], taps[:, l, c, :], tri[:, 0:T - c * P],
                                       start=(c == 0), stop=(c == C - 1))
                    mm.then_inc(resp_psum, 1)

            for k in range(NK + 1):
                piece_of(0, k)
            for piece in PIECES[:NEARLY]:
                piece_of(*piece)
            pe.wait_ge(wts_in, 7 * 16)
            pe.wait_ge(small_w, 3)

            def x_part(n, u, past, pieces=((), ())):
                pe.wait_ge(q8_ready, 6 * (n + 1))
                if past:
                    pe.wait_ge(q8T_ready, n)
                for c in range(C):
                    mm = pe.transpose(ybank[0][:, c * P:(c + 1) * P], q8r[:, u, c * P:(c + 1) * P], ident[:, :])
                mm.then_inc(q8_turned, 1)
                for piece in pieces[0]:
                    piece_of(*piece)
                pe.wait_ge(q8T_ready, n + 1)
                if past:
                    pe.wait_ge(g0_ready, n)
                pe.matmul(xbank[:, :], ones3[:, :], b_ffn.unsqueeze(1).broadcast_to([3, C, H]), start=True, stop=False)
                for c in range(C):
                    mm = pe.matmul(xbank[:, c * H:(c + 1) * H], q8T[:, u, c * P:(c + 1) * P], w8[:, :],
                                   start=False, stop=(c == C - 1))
                mm.then_inc(ffn_psum, 1)
                for piece in pieces[1]:
                    piece_of(*piece)
            for n in range(B):
                x_part(n, n % 2, n > 0, pieces_at(n))

            def turn(n, u):
                pe.wait_ge(xn1_ready, C * (n + 1))
                if at_least(n, 1):
                    pe.wait_ge(place_step, PLACE * n - 4)
                for c in range(C):
                    mm = pe.transpose(ybank[0][:, c * P:(c + 1) * P], xn1[:, u, c, :], ident[:, :])
                mm.then_inc(xn1_turned, 1)

            def kvr(n):
                pe.wait_ge(xm_step, 2 * (n + 1))
                if at_least(n, 1):
                    pe.wait_ge(wkv_step, WKV * (n - 1) + 1)
                    pe.wait_ge(tr_ready, n)
                for m in range(3):
                    mm = pe.matmul(zbank[:, m, :], w_attn[:, m, :], xm, start=True, stop=True)
                mm.then_inc(kvr_psum, 1)

            def logits(n, u):
                pe.wait_ge(xT_ready, n + 1)
                for c in range(C):
                    mm = pe.matmul(ybank[0][:, c * E:(c + 1) * E], xT[:, u, c * P:(c + 1) * P], w_gate[:, :],
                                   start=True, stop=True)
                mm.then_inc(logit_psum, 1)

            def ranks(n):
                pe.wait_ge(place_step, PLACE * n + 6)
                rank = ybank[0][:, C * E:2 * C * E]
                pe.matmul(rank, strict16[:, :], oh16[:, :], start=True, stop=False)
                for c in range(1, C):
                    pe.matmul(rank[:, c * E:], ones16[:, :], oh16[:, 0:(C - c) * E], start=False, stop=False)
                pe.matmul(rank, ones16[:, :], cum16[:, :].unsqueeze(1).broadcast_to([P, C, E]),
                          start=False, stop=True).then_inc(rank_psum, 1)
            pe.wait_ge(ident_ready, 1)
            pe.wait_ge(resp_split, NL)

            def step(k):
                u = k_par(k)
                if ahead(k, 0):
                    pe.wait_ge(zn_ready, C * (k + 1))
                    if not (isinstance(k, int) and k < 1):
                        pe.wait_ge(conv_step, CONV * k - 1)
                    for m in range(NK):
                        mm = pe.matmul(zbank[:, m, :], fwd[m], zn[:, u, :, :], start=True, stop=True)
                    mm.then_inc(z_ready, 1)
                if behind(k, 1):
                    n = k - 1
                    pe.wait_ge(conv_step, CONV * (n + 1))
                    if behind(n, 2):
                        pe.wait_ge(y_ready, n - 1)
                    pe.matmul(ybank[1 - u][:, :], ident_r[:, :], of(n, resp_high), start=True, stop=False)
                    pe.matmul(ybank[1 - u][:, :], ident_r[:, :], of(n, resp_low), start=False, stop=False)
                    for c in range(C):
                        for m in range(NK):
                            mm = pe.matmul(ybank[1 - u][:, c * P:(c + 1) * P], acc[:, 1 - u, m, c * H:(c + 1) * H],
                                           inv[:, m, :], start=False, stop=(c == C - 1 and m == NK - 1))
                    mm.then_inc(y_psum, 1)
                if behind(k, 2):
                    n = k - 2
                    if isinstance(k, int) and k == NL * B + 1:
                        logits(0, 0)
                    pe.wait_ge(y_ready, n + 1)
                    if not (isinstance(n, int) and n < 1):
                        pe.wait_ge(glu_ready, n)
                    dyn = not isinstance(n, int)
                    wg = w_glu[:, ds(n // B), :].squeeze(1) if dyn else w_glu[:, n // B, :]
                    bg = b_glu[:, ds(n // B), :].broadcast_to([3, 2, 2 * H]) if dyn \
                        else b_glu[:, n // B:n // B + 1, :].broadcast_to([3, 2, 2 * H])
                    for a in range(2):
                        pe.matmul(glbank[:, a, :], ones3[:, :], bg, start=True, stop=False)
                        for c in range(2):
                            mm = pe.matmul(glbank[:, a, c * 2 * H:(c + 1) * 2 * H],
                                           y[:, u, (2 * a + c) * P:(2 * a + c + 1) * P], wg,
                                           start=False, stop=(c == 1))
                    mm.then_inc(glu_psum, 1)
                if isinstance(k, int) and k == NL * B + 1:
                    kvr(0)
                    pe.wait_ge(masks_ready, 3)
                    ranks(0)
                if isinstance(k, int) and k == NL * B:
                    pe.wait_ge(y_ready, k - 1)
                    turn(0, 0)
            run_steps(pe, step)

            def outputs(n, u):
                pe.wait_ge(ffn_step, 2 * (2 * n + 2))
                if at_least(n, 1):
                    pe.wait_ge(fo_ready, n)
                for c in range(C):
                    for f in range(2):
                        mm = pe.matmul(xbank[:, c * H:(c + 1) * H], hs[:, u, f, c * P:(c + 1) * P], w_sd[:, f, :],
                                       start=(f == 0), stop=(f == 1))
                mm.then_inc(down_psum, 1)
                pe.wait_ge(rw_ready, n + 1)
                if at_least(n, 1):
                    pe.wait_ge(sa_ready, n)
                for c in range(C):
                    mm = pe.matmul(ybank[1][:, c * H:(c + 1) * H], rw[:, u, c * P:(c + 1) * P], w_attn[:, 3, :],
                                   start=True, stop=True)
                mm.then_inc(attn_psum, 1)
            pe.wait_ge(w_half, 2)
            pe.wait_ge(glu_ready, NL * B)
            turn(1, 1)

            def second(n, u):
                def gate_up(f):
                    if f or at_least(n, 1):
                        pe.wait_ge(ffn_step, 2 * (2 * n + f))
                    for m in range(2):
                        mm = pe.matmul(glbank[:, m, :], w_sgu[:, m, f * P:(f + 1) * P], xT[:, u, :],
                                       start=True, stop=True)
                    mm.then_inc(gu_psum, 1)
                gate_up(0)
                if follows(n, 1):
                    logits(n + 1, 1 - u)
                else:
                    pe.wait_ge(place_step, PLACE * B)
                    pe.matmul(ybank[0][:, 0:E], ones16[:, :], cum16[:, :], start=True, stop=True).then_inc(rank_psum, 1)
                if at_least(n, 1):
                    outputs(n - 1, 1 - u)
                if follows(n, 1):
                    ranks(n + 1)
                gate_up(1)
                if follows(n, 1):
                    kvr(n + 1)
                if follows(n, 2):
                    turn(n + 2, u)
            run_batches(pe, second)
            outputs(B - 1, 1)

            pe.wait_ge(tables_ready, 3)
            pe.wait_ge(routed_in, 16)
            pe.wait_ge(fo_ready, B)
            pe.wait_ge(sa_ready, B)

            loaded = {}

            def step(k, u, quarter):
                def expert(back):
                    if u - back not in loaded:
                        loaded[u - back] = pe.value_load(tile_e[0:1, ds(k - back)], min_val=0, max_val=E - 1)
                    return loaded[u - back]
                if u == 0:
                    loaded.clear()
                e_up = expert(1) if live(k, 1) else None
                e_down = expert(4) if live(k, 4) else None
                if live(k, 0):
                    pe.wait_ge(tiles_in[u % 4], 16 * (quarter(0) + 1))
                    if at_least(k, 2):
                        pe.wait_ge(tile_copied, k - 1)
                    pe.transpose(zbank[:, u % 2, 0:P], xtok[:, u % 4, 0:H], ident[:, :]).then_inc(tile_turned, 1)
                if live(k, 4):
                    n, e = k - 4, e_down
                    pe.wait_ge(hT_ready, n + 1)
                    if at_least(n, 2):
                        pe.wait_ge(ytok_ready, n - 1)
                    out = xbank[:, 0:P] if u % 2 else zbank[:, 2, 0:P]
                    for f in range(2):
                        mm = pe.matmul(out, hT_r[:, u % 2, f * P:(f + 1) * P],
                                       routed[:, ds(e * (2 * H) + E * 2 * F + f * H, H)], start=(f == 0), stop=(f == 1))
                    mm.then_inc(y_r_psum, 1)
                if live(k, 3):
                    n, v = k - 3, (u - 3) % 2
                    pe.wait_ge(hr_ready, n + 1)
                    if at_least(n, 2):
                        pe.wait_ge(hT_ready, n - 1)
                    for f in range(2):
                        mm = pe.transpose(ybank[v][:, f * P:(f + 1) * P], h_r[:, v, f * P:(f + 1) * P], ident[:, :])
                    mm.then_inc(hr_turned, 1)
                if live(k, 1):
                    n, v, e = k - 1, (u - 1) % 2, e_up
                    pe.wait_ge(tile_copied, n + 1)
                    if at_least(n, 2):
                        pe.wait_ge(hr_ready, n - 1)
                    pe.matmul(glbank[:, v, :], xt_r[:, v, :], routed[:, ds(e * (2 * F), 2 * F)],
                              start=True, stop=True).then_inc(gur_psum, 1)
            run_tiles(pe, step)

        @block.vector
        def _(dve):
            links = [0]

            def link(ins):
                links[0] += 1
                ins.then_inc(dve_chain, 1)
                dve.wait_ge(dve_chain, links[0])

            def tt(o, a, b, op):
                link(dve.tensor_tensor(o, a, b, op))

            def ts(o, a, s1, s2, op0, op1=None):
                link(dve.tensor_scalar(o, a, s1, s2, op0) if op1 is None
                     else dve.tensor_scalar(o, a, s1, s2, op0, op1))

            def stt(o, a, s, b, op0, op1):
                link(dve.scalar_tensor_tensor(out=o, in0=a, scalar=s, in1=b, op0=op0, op1=op1))

            S = [small[:, i, :] for i in range(22)]
            dt, alpha, ea, em1, s1, s2 = S[5], S[6], S[7], S[8], S[9], S[10]
            beta, c_re, c_im = raw[:, 2, :], raw[:, 3, :], raw[:, 4, :]

            def exact_exp(x, lo, n):
                k, rem, p, s = [small[:, lo + n * m:lo + n * (m + 1), :] for m in range(4)]
                ts(rem, x, -87.0, 88.0, ALU.max, ALU.min)
                ts(k, rem, float(np.log2(np.e)), ROUND, ALU.mult, ALU.add)
                ts(k, k, -ROUND, None, ALU.add)
                stt(rem, k, -LN2_HI, rem, ALU.mult, ALU.add)
                stt(rem, k, -LN2_LO, rem, ALU.mult, ALU.add)
                ts(s.bitcast(I32), k, 127.0, 2.0 ** 23, ALU.add, ALU.mult)
                ts(p, rem, 1.0 / 5040, None, ALU.mult)
                for c in (1.0 / 720, 1.0 / 120, 1.0 / 24, 1.0 / 6, 0.5, 1.0):
                    stt(p, p, c, rem, ALU.add, ALU.mult)
                return p, s
            dve.wait_ge(modes_in, 80)
            p, s = exact_exp(raw[:, 0:2, :], 11, 2)
            stt(small[:, 5:7, :], p, 1.0, s, ALU.add, ALU.mult)
            tt(S[1], alpha, dt, ALU.mult)
            tt(S[11], beta, dt, ALU.mult)
            ts(S[11], S[11], float(1 / (2 * np.pi)), None, ALU.mult)
            ts(S[12], S[11], ROUND, -ROUND, ALU.add, ALU.add)
            tt(S[3], S[11], S[12], ALU.subtract)
            ts(S[11], S[3], float(NSMALL), None, ALU.mult)
            ts(S[12], S[11], ROUND, -ROUND, ALU.add, ALU.add)
            tt(S[4], S[11], S[12], ALU.subtract)
            dve.tensor_scalar(S[2], S[1], float(NSMALL), None, ALU.mult).then_inc(decay_ready, 1)
            ts(S[11], S[1], -1.0, None, ALU.mult)
            p, s = exact_exp(small[:, 11:12, :], 12, 1)
            p, s = p[:, 0, :], s[:, 0, :]
            stt(ea, p, 1.0, s, ALU.add, ALU.mult)
            ts(S[11], s, -1.0, None, ALU.add)
            tt(p, p, s, ALU.mult)
            tt(em1, p, S[11], ALU.add)
            def reduce_turns(q):
                u = q % 2
                dve.wait_ge(turns_ready, 2 * (q + 1))
                if q >= 2:
                    dve.wait_ge(sines_ready, 2 * (q - 1))
                ts(apart[:, u, :, :], turns[:, u, :, :], ROUND, -ROUND, ALU.add, ALU.add)
                dve.tensor_tensor(part[:, u, :, :], turns[:, u, :, :], apart[:, u, :, :],
                                  ALU.subtract).then_inc(part_ready, 1)
                dve.wait_ge(part_ready, 2 * q + 1)
                dve.tensor_scalar(apart[:, u, :, :].bitcast(I32), part[:, u, :, :].bitcast(I32), 0x7FFFFFFF, None,
                                  ALU.bitwise_and).then_inc(part_ready, 1)
            reduce_turns(0)
            dve.wait_ge(small_sin, 2)
            tt(S[14], s2, s2, ALU.mult)
            ts(S[15], S[14], -2.0, 1.0, ALU.mult, ALU.add)
            tt(S[13], em1, S[15], ALU.mult)
            stt(S[13], S[14], -2.0, S[13], ALU.mult, ALU.add)
            tt(S[14], ea, s1, ALU.mult)
            tt(S[15], alpha, alpha, ALU.mult)
            tt(S[16], beta, beta, ALU.mult)
            tt(S[15], S[15], S[16], ALU.add)
            link(dve.reciprocal(S[15], S[15]))
            tt(S[16], S[14], beta, ALU.mult)
            tt(S[17], S[13], alpha, ALU.mult)
            tt(S[16], S[16], S[17], ALU.subtract)
            tt(S[16], S[16], S[15], ALU.mult)
            tt(S[17], S[13], beta, ALU.mult)
            tt(S[18], S[14], alpha, ALU.mult)
            tt(S[17], S[17], S[18], ALU.add)
            tt(S[17], S[17], S[15], ALU.mult)
            tt(S[18], c_re, S[16], ALU.mult)
            tt(S[19], c_im, S[17], ALU.mult)
            tt(S[18], S[18], S[19], ALU.add)
            tt(S[19], c_im, S[16], ALU.mult)
            tt(S[20], c_re, S[17], ALU.mult)
            tt(S[19], S[19], S[20], ALU.subtract)
            cr, ci, ncr, nci = S[13], S[14], S[15], S[16]
            ts(cr, S[18], 2.0, None, ALU.mult)
            ts(ncr, S[18], -2.0, None, ALU.mult)
            ts(ci, S[19], 2.0, None, ALU.mult)
            ts(nci, S[19], -2.0, None, ALU.mult)

            dve.wait_ge(decay_exp, 2)
            for q in range(NQ):
                u = q % 2
                dve.wait_ge(sines_ready, 2 * (q + 1))
                if q >= 2:
                    dve.wait_ge(taps_psum, q - 1)
                dq = decay[:, QH * q:QH * (q + 1), :]
                dve.tensor_tensor(pow_re[:, u, :, :], dq, cosines[:, u, :, :], ALU.mult).then_inc(pow_ready, 1)
                dve.wait_ge(pow_ready, q + 1)

                def coef(x):
                    return x[:, QH * q:QH * (q + 1)].unsqueeze(2).broadcast_to([P, QH, NBIG])
                big_re, big_im = pow_re[:, u, :, NSMALL:NPOW], pow_im[:, u, :, NSMALL:NPOW]
                tt(vt[:, 0, :, :], big_re, coef(cr), ALU.mult)
                tt(vt[:, 2, :, :], big_re, coef(nci), ALU.mult)
                if q + 1 < NQ:
                    reduce_turns(q + 1)
                dve.wait_ge(pow_im_ready, q + 1)
                tt(vt[:, 1, :, :], big_im, coef(ci), ALU.mult)
                tt(vt[:, 3, :, :], big_im, coef(ncr), ALU.mult)
                if q >= 2:
                    dve.wait_ge(vbd_re_ready, NL * (q - 1))
                    dve.wait_ge(vbd_im_ready, q - 1)
                dve.tensor_tensor(v_re[:, u, :, :], vt[:, 0, :, :], vt[:, 1, :, :], ALU.subtract).then_inc(v_ready, 1)
                dve.tensor_tensor(v_im[:, u, :, :], vt[:, 2, :, :], vt[:, 3, :, :], ALU.add).then_inc(v_ready, 1)
            dve.wait_ge(rows_in, 48)
            dve.wait_ge(wts_in, 7 * 16)
            bg = biases_raw[:, 0:NL * 2 * H].rearrange("p (l o) -> p l o", l=NL)
            ts(bg[:, :, 0:H], bg[:, :, 0:H], 0.5, None, ALU.mult)
            ts(biases_raw[:, NL * 2 * H:], biases_raw[:, NL * 2 * H:], 0.5, None, ALU.mult)
            dve.tensor_scalar(w_glu[:, :, 0:H], w_glu[:, :, 0:H], 0.5, None, ALU.mult).then_inc(small_w, 1)
            ts(w8[:, :], w8[:, :], cols[:, 10:11], cols[:, 9:10], ALU.mult, ALU.mult)
            dve.tensor_scalar(w8[:, :], w8[:, :], 0.5, None, ALU.mult).then_inc(small_w, 1)
            link(dve.reciprocal(idle[:, 2:3], cols[:, 9:10]))
            def norm_stats(src, u, done):
                for c in range(C):
                    dve.bn_stats(stats[:, u, c, :], src[:, c, :]).then_inc(done, 1)

            dve.wait_ge(x_in_s, 16)
            for u in range(2):
                norm_stats(x_in[:, u, :, :], u, xstats)
            w16 = [bsp16[:, i, 0:NBIAS] for i in range(3)]
            link(dve.tensor_copy(w16[0], biases_raw))
            tt(bsp[:, 0, :], biases_raw, w16[0], ALU.subtract)
            link(dve.tensor_copy(w16[1], bsp[:, 0, :]))
            tt(bsp[:, 1, :], bsp[:, 0, :], w16[1], ALU.subtract)
            dve.wait_ge(taps_ready, C * NQ)
            tt(taps[0:1, :, 0, :], taps[0:1, :, 0, :], d_row.rearrange("p (l h) -> p l h", l=NL), ALU.add)
            for l in range(NL):
                dve.tensor_tensor(taps_w[:, l, :, :], taps[:, l, :, :],
                                  ln_w_rows[:, l, :].unsqueeze(1).broadcast_to([P, C, H]),
                                  ALU.mult).then_inc(tapsw_ready, 1)
            dve.memset(idle[:, 0:1], 0.0).then_inc(kgen_idle, 1)
            dve.tensor_copy(ident_r[:, :], ident[:, :]).then_inc(ident_ready, 1)
            link(dve.tensor_copy(w16[2], bsp[:, 1, :]))
            ts(bsp[:, 0, :], w16[0], ident[0:3, 0:1], None, ALU.mult)
            stt(bsp[:, 1, :], w16[1], ident[0:3, 1:2], bsp[:, 0, :], ALU.mult, ALU.add)
            dve.scalar_tensor_tensor(out=biases[:, :], in0=w16[2], scalar=ident[0:3, 2:3], in1=bsp[:, 1, :],
                                     op0=ALU.mult, op1=ALU.add).then_inc(small_w, 1)
            dve.wait_ge(small_w, 3)

            def quantize(n, u, past):
                w = 6 * n
                if past:
                    dve.wait_ge(q8_ready, w)
                dve.wait_ge(x_norm, (C - 1) * (n + 1))
                dve.wait_ge(h_ready, n + 1)
                xn = h[:, ds(n), :, :].squeeze(1).rearrange("p c h -> p (c h)")
                dve.tensor_scalar(q8, xn, idle[:, 2:3], FMAX8, ALU.mult, ALU.min).then_inc(q8_ready, 1)
                dve.wait_ge(q8_ready, w + 1)
                dve.tensor_scalar(q8, q8, -FMAX8, None, ALU.max).then_inc(q8_ready, 1)
                dve.wait_ge(q8_ready, w + 2)
                dve.tensor_scalar(q8s.bitcast(I32), q8.bitcast(I32), 0x7F800000, None,
                                  ALU.bitwise_and).then_inc(q8_ready, 1)
                dve.wait_ge(q8_ready, w + 3)
                dve.tensor_scalar(q8s, q8s, 2.0 ** -6, 1.5 * 2.0 ** 20, ALU.max, ALU.mult).then_inc(q8_ready, 1)
                dve.wait_ge(q8_ready, w + 4)
                dve.tensor_tensor(q8, q8, q8s, ALU.add).then_inc(q8_ready, 1)
                dve.wait_ge(q8_ready, w + 5)
                dve.tensor_tensor(q8r[:, u, :], q8, q8s, ALU.subtract).then_inc(q8_ready, 1)

            def gate0(n, u):
                dve.wait_ge(ffn_tanh, n + 1)
                dve.scalar_tensor_tensor(out=g0[:, ds(n), :, :].squeeze(1), in0=th8[:, u, :, :], scalar=1.0,
                                         in1=xbank[:, :].rearrange("p (c h) -> p c h", c=C),
                                         op0=ALU.add, op1=ALU.mult).then_inc(g0_ready, 1)
            def layer_stats(n, u):
                if not isinstance(n, int) or n >= 2:
                    dve.wait_ge(lrstd, RSTD * (n - 1))
                dve.wait_ge(h_ready, n + 1)
                hb = h[:, ds(n % B), :, :].squeeze(1) if not isinstance(n, int) else h[:, n % B, :, :]
                norm_stats(hb, u, lstats)

            def split_response(l):
                dve.wait_ge(resp_ready, l + 1)
                dve.scalar_tensor_tensor(out=resp_low[:, l, :], in0=ybank[1][:, :], scalar=cols[:, l:l + 1],
                                         in1=resp_high[:, l, :].bitcast(F32), op0=ALU.mult,
                                         op1=ALU.subtract).then_inc(resp_split, 1)

            def x_part(n, u, more, past):
                quantize(n, u, past)
                if more:
                    norm_stats(x_in[:, ds(n + 2), :, :].squeeze(1), u, xstats)
                else:
                    layer_stats(n - (B - 2), u)
                if past:
                    gate0(n - 1, 1 - u)
            for n in range(B):
                x_part(n, n % 2, n + 2 < B, n > 0)
                if n % 2 == 0:
                    split_response(n // 2)
            gate0(B - 1, 1)


            dve.tensor_scalar(w_attn[:, 3, :], w_attn[:, 3, :], 0.5, None, ALU.mult).then_inc(w_half, 1)
            dve.tensor_scalar(w_sd[:, :, :], w_sd[:, :, :], 0.5, None, ALU.mult).then_inc(w_half, 1)
            ts(dcol[:, 3:4], cols[:, 4:5], -1.0, 1.0, ALU.mult, ALU.add)
            dve.wait_ge(dcols, 3)

            def mix(n, u):
                dve.wait_ge(xT_ready, n + 1)
                dve.tensor_scalar(xm, xT[:, u, :], cols[:, 4:5], None, ALU.mult).then_inc(xm_step, 1)
                dve.wait_ge(xm_step, 2 * n + 1)
                dve.scalar_tensor_tensor(out=xm[:, 1:T], in0=xT[:, u, 0:T - 1], scalar=dcol[:, 3:4],
                                         in1=xm[:, 1:T], op0=ALU.mult, op1=ALU.add).then_inc(xm_step, 1)

            def place_tokens(n, u):
                w = PLACE * n
                cE = [P, C, E]
                l8 = ybank[0][:, 0:C * E].rearrange("p (c e) -> p c e", c=C)
                rank = ybank[0][:, C * E:2 * C * E].rearrange("p (c e) -> p c e", c=C)
                oh = oh16[:, :].rearrange("p (c e) -> p c e", c=C)
                dve.wait_ge(logit_psum, n + 1)
                dve.tensor_copy(lt[:, :, :], l8).then_inc(place_step, 1)
                yield
                dve.wait_ge(place_step, w + 1)
                dve.tensor_reduce(mx[:, u, :], lt[:, :, :], AX, ALU.max).then_inc(place_step, 1)
                yield
                dve.wait_ge(place_step, w + 2)
                dve.tensor_tensor(pick[:, :, :], lt[:, :, :], mx[:, u, :].unsqueeze(2).broadcast_to(cE),
                                  ALU.is_ge).then_inc(place_step, 1)
                yield
                dve.wait_ge(place_step, w + 3)
                dve.scalar_tensor_tensor(out=pick[:, :, :], in0=pick[:, :, :], scalar=-float(E),
                                         in1=iota_e[:, :].unsqueeze(1).broadcast_to(cE),
                                         op0=ALU.mult, op1=ALU.add).then_inc(place_step, 1)
                yield
                dve.wait_ge(place_step, w + 4)
                dve.tensor_reduce(emin[:, :], pick[:, :, :], AX, ALU.min).then_inc(place_step, 1)
                yield
                dve.wait_ge(place_step, w + 5)
                dve.tensor_tensor(oh, pick[:, :, :], emin[:, :].unsqueeze(2).broadcast_to(cE),
                                  ALU.is_equal).then_inc(place_step, 1)
                yield
                dve.wait_ge(place_step, w + 6)
                dve.tensor_reduce(count[:, :], oh.rearrange("p c e -> p e c"), AX, ALU.add).then_inc(place_step, 1)
                yield
                dve.wait_ge(rank_psum, n + 1)
                dve.wait_ge(place_step, w + 7)
                dve.tensor_tensor(place[:, :, :], rank, region[:, :].unsqueeze(1).broadcast_to(cE),
                                  ALU.add).then_inc(place_step, 1)
                yield
                dve.tensor_tensor(cum16[:, :], cum16[:, :], count[:, :], ALU.add).then_inc(place_step, 1)
                yield
                dve.wait_ge(place_step, w + 8)
                dve.tensor_tensor(place[:, :, :], place[:, :, :], oh, ALU.mult).then_inc(place_step, 1)
                yield
                dve.wait_ge(place_step, w + 10)
                dve.tensor_reduce(slot_f[:, :], place[:, :, :], AX, ALU.add).then_inc(place_step, 1)
                yield
                dve.wait_ge(place_step, w + 11)
                if at_least(n, 2):
                    dve.wait_ge(scattered[u], 16 * C * (n // 2))
                dve.tensor_copy(slot[:, u, :], slot_f[:, :]).then_inc(place_step, 1)
                yield
            dve.memset(cum16[:, :], 0.0).then_inc(masks_ready, 1)
            dve.tensor_copy(strict16[:, :], strict).then_inc(masks_ready, 1)
            dve.memset(ones16[:, :], 1.0).then_inc(masks_ready, 1)
            dve.wait_ge(pool_consts, 8)
            dve.wait_ge(masks_ready, 3)
            layer_stats(2, 0)

            def step(k):
                u = k_par(k)
                if ahead(k, 0):
                    w = CONV * k
                    dve.wait_ge(z_ready, k + 1)
                    if behind(k, 2):
                        dve.wait_ge(y_psum, k - 1)
                    if behind(k, 1):
                        dve.wait_ge(conv_step, w)
                    for dist in range(C - 1, -1, -1):
                        n = C - dist
                        sp_d = of(k, spectra)[:, dist, :, :]
                        dst = acc[:, u, :, :] if dist == 0 else tmps[dist]
                        dve.tensor_tensor(dst.rearrange("p k (c h) -> p k c h", c=n),
                                          zbank[:, :, 0:n * H].rearrange("p k (c h) -> p k c h", c=n),
                                          sp_d.unsqueeze(2).broadcast_to([P, NK, n, H]),
                                          ALU.mult).then_inc(conv_step, 1)
                    dve.wait_ge(conv_step, w + C)
                    dve.wait_ge(far_step, 2 * (k + 1))
                    a = acc[:, u, :, H:]
                    dve.tensor_tensor(a, a, tmps[1], ALU.add).then_inc(conv_step, 1)
                if behind(k, 2):
                    n = k - 2
                    if isinstance(k, int) and k == NL * B + 1:
                        mix(0, 0)
                        routing = place_tokens(0, 0)
                        for _ in range(7):
                            next(routing)
                    dve.wait_ge(glu_tanh, n + 1)
                    if behind(n, 2):
                        dve.wait_ge(h_ready, B + n - 1)
                    dve.scalar_tensor_tensor(
                        out=prod[:, u, :, :], in0=th[:, u, :, :], scalar=1.0,
                        in1=glbank[:, :, :].rearrange("p a (c o) -> p (a c) o", c=2)[:, :, 0:H],
                        op0=ALU.add, op1=ALU.mult).then_inc(glu_ready, 1)
                    if isinstance(k, int) and k == NL * B + 1:
                        for _ in routing:
                            pass
                if ahead(k, 3):
                    layer_stats(k + 3, 1 - u)
                elif k + 3 - NL * B < 2:
                    n = k + 3 - NL * B
                    dve.wait_ge(x1_step, 2 * (n + 1))
                    norm_stats(x1[:, n, :, :], n % 2, nstats)
            run_steps(dve, step)

            link(dve.memset(s_num[:, 0:1], 0.0))
            link(dve.memset(s_den[:, 0:1], 0.0))


            def tile_tables():
                def put(ins):
                    links[0] += 1
                    ins.then_inc(dve_chain, 1)
                    return links[0]
                tiles, ends, blank_f, total = [etab[:, i, :] for i in range(4)]
                past, their = tile_tmp[:, 0, :, :], tile_tmp[:, 1, :, :]
                tE = [P, NT, E]
                tn, tsl = tile_n[:, :], tile_s[:, :]
                dve.wait_ge(rank_psum, B + 1)
                v = put(dve.tensor_copy(total, ybank[0][:, 0:E]))
                yield
                dve.wait_ge(dve_chain, v)
                v = put(dve.tensor_scalar(tiles, total, 1.0 / P, 127.0 / P - 0.498, ALU.mult, ALU.add))
                put(dve.tensor_tensor(blank_f, total, region[:, :], ALU.add))
                yield
                dve.wait_ge(dve_chain, v)
                v = put(dve.tensor_scalar(tiles, tiles, ROUND, -ROUND, ALU.add, ALU.add))
                yield
                dve.wait_ge(dve_chain, v)
                dve.tensor_copy(blank_row[:, :], blank_f).then_inc(tables_ready, 1)
                v = put(dve.tensor_tensor_scan(ends, ones_e[:, :], tiles, 0.0, ALU.mult, ALU.add))
                yield
                dve.wait_ge(dve_chain, v)
                v = put(dve.tensor_tensor(past, iota_t[:, :].unsqueeze(2).broadcast_to(tE),
                                          ends.unsqueeze(1).broadcast_to(tE), ALU.is_ge))
                yield
                dve.wait_ge(dve_chain, v)
                put(dve.tensor_reduce(tn, past, AX, ALU.add))
                v = put(dve.tensor_tensor(their, past, tiles.unsqueeze(1).broadcast_to(tE), ALU.mult))
                yield
                dve.wait_ge(dve_chain, v)
                v = put(dve.tensor_reduce(tsl, their, AX, ALU.add))
                yield
                dve.wait_ge(dve_chain, v)
                v = put(dve.tensor_tensor(tsl, iota_t[:, :], tsl, ALU.subtract))
                yield
                dve.wait_ge(dve_chain, v)
                v = put(dve.tensor_scalar(tsl, tsl, float(P), None, ALU.mult))
                yield
                dve.wait_ge(dve_chain, v)
                v = put(dve.scalar_tensor_tensor(out=tsl, in0=tn, scalar=float(REGION), in1=tsl,
                                                 op0=ALU.mult, op1=ALU.add))
                yield
                dve.wait_ge(dve_chain, v)
                v = put(dve.tensor_scalar(tsl, tsl, float(E * REGION), None, ALU.min))
                put(dve.tensor_scalar(tn, tn, float(E - 1), None, ALU.min))
                yield
                dve.wait_ge(dve_chain, v + 1)
                dve.tensor_copy(tile_row[:, :], tsl).then_inc(tables_ready, 1)
                dve.tensor_copy(tile_e[:, :], tn).then_inc(tables_ready, 1)

            def second(n, u):
                routing = place_tokens(n + 1, 1 - u) if follows(n, 1) else tile_tables()
                dve.wait_ge(kvr_psum, n + 1)
                if at_least(n, 1):
                    dve.wait_ge(ek_ready, n)
                dve.tensor_scalar(kmin, zbank[:, 0, :], 60.0, None, ALU.min).then_inc(kmin_ready, 1)
                if follows(n, 1):
                    mix(n + 1, 1 - u)
                next(routing, None)
                if follows(n, 2):
                    dve.wait_ge(x1_step, 2 * (n + 3))
                    norm_stats(x1[:, ds(n + 2), :, :].squeeze(1), u, nstats)
                next(routing, None)
                w = WKV * n
                if at_least(n, 1):
                    dve.wait_ge(wkv_step, w)
                dve.wait_ge(ek_ready, n + 1)
                dve.tensor_tensor(kv, ek, zbank[:, 1, :], ALU.mult).then_inc(wkv_step, 1)
                next(routing, None)
                step_decay = dcol[:, 1:2].broadcast_to([P, T])
                dve.tensor_tensor_scan(s_den[:, 1:T + 1], step_decay, ek, 0.0, ALU.mult, ALU.add).then_inc(wkv_step, 1)
                next(routing, None)
                dve.wait_ge(wkv_step, w + 1)
                dve.tensor_tensor_scan(s_num[:, 1:T + 1], step_decay, kv, 0.0, ALU.mult, ALU.add).then_inc(wkv_step, 1)
                next(routing, None)

                def shared(f):
                    dve.wait_ge(tg_ready, 2 * n + f + 1)
                    dve.scalar_tensor_tensor(out=sl, in0=tg, scalar=1.0, in1=glbank[:, 0, :], op0=ALU.add,
                                             op1=ALU.mult).then_inc(ffn_step, 1)
                    next(routing, None)
                    dve.wait_ge(ffn_step, 2 * (2 * n + f) + 1)
                    dve.tensor_tensor(hs[:, u, f, :], sl, glbank[:, 1, :], ALU.mult).then_inc(ffn_step, 1)
                shared(0)
                next(routing, None)
                if at_least(n, 1):
                    dve.wait_ge(ratio_ready, n)
                dve.wait_ge(wkv_step, w + 2)
                dve.scalar_tensor_tensor(out=den, in0=ek, scalar=dcol[:, 2:3], in1=s_den[:, 0:T], op0=ALU.mult,
                                         op1=ALU.add).then_inc(wkv_step, 1)
                dve.wait_ge(wkv_step, w + 3)
                dve.scalar_tensor_tensor(out=num, in0=kv, scalar=dcol[:, 2:3], in1=s_num[:, 0:T], op0=ALU.mult,
                                         op1=ALU.add).then_inc(wkv_step, 1)
                dve.wait_ge(wkv_step, w + 4)
                dve.tensor_scalar(den, den, 1e-9, None, ALU.add).then_inc(wkv_step, 1)
                next(routing, None)
                next(routing, None)
                if not follows(n, 1):
                    for _ in routing:
                        pass
                dve.wait_ge(wkv_step, w + 6)
                dve.reciprocal(den, den).then_inc(wkv_step, 1)
                next(routing, None)
                shared(1)
                for _ in routing:
                    pass
                dve.wait_ge(ratio_ready, n + 1)
                dve.wait_ge(tr_ready, n + 1)
                dve.scalar_tensor_tensor(out=rw[:, u, :], in0=tr, scalar=1.0, in1=ratio, op0=ALU.add,
                                         op1=ALU.mult).then_inc(rw_ready, 1)
            run_batches(dve, second)

            def step(k, u, quarter):
                if live(k, 0):
                    dve.wait_ge(tile_turned, k + 1)
                    if at_least(k, 2):
                        dve.wait_ge(gur_psum, k - 1)
                    dve.tensor_copy(xt_r[:, u % 2, :], zbank[:, u % 2, 0:P]).then_inc(tile_copied, 1)
                    if at_least(k, 8):
                        dve.wait_ge(stored[u % 4], 16 * quarter(4))
                    row = xtok[:, u % 4, H:XROW]
                    v = slice(u % 8, u % 8 + 1)
                    dve.scalar_tensor_tensor(out=shift[:, v], in0=row, scalar=float(B * T), in1=own_rows[:, ds(k)],
                                             op0=ALU.is_ge, op1=ALU.mult).then_inc(ids_ready, 1)
                    dve.wait_ge(ids_ready, 2 * k + 1)
                    dve.tensor_tensor(ids[:, v], row, shift[:, v], ALU.add).then_inc(ids_ready, 1)
                if live(k, 3):
                    n, v = k - 3, (u - 3) % 2
                    dve.wait_ge(hr_turned, n + 1)
                    if at_least(n, 2):
                        dve.wait_ge(y_r_psum, n - 1)
                    dve.tensor_copy(hT_r[:, v, :], ybank[v][:, 0:2 * P]).then_inc(hT_ready, 1)
                if live(k, 1):
                    n, v = k - 1, (u - 1) % 2
                    dve.wait_ge(sil_ready, n + 1)
                    if at_least(n, 2):
                        dve.wait_ge(hr_turned, n - 1)
                    dve.tensor_tensor(h_r[:, v, :], sil[:, v, :], glbank[:, v, F:2 * F],
                                      ALU.mult).then_inc(hr_ready, 1)
            run_tiles(dve, step)

            for b in range(B + 1):
                if b < B:
                    dve.wait_ge(routed_back[b], 16)
                    t = gat[:, b, :, :]
                    dve.tensor_tensor(t, t, fo[:, b, :, :], ALU.add).then_inc(tot_ready, 1)
                if b >= 1:
                    dve.wait_ge(tot_silu, b)
                    t = gat[:, b - 1, :, :]
                    dve.tensor_tensor(t, t, sa[:, b - 1, :, :], ALU.mult).then_inc(gated, 1)


def constants():
    t = np.arange(P)[:, None]
    w = 2 * np.pi * (np.arange(P)[None, :] + 0.5) / (2 * P)

    def comps(a, b, kinds):
        return [kinds[0](a, b), kinds[1](a, b), kinds[2](a, b)]
    out = []
    a, b = np.cos(w * t), -np.sin(w * t)
    out += [a + b, a, b]
    out += [a, b - a, a + b]
    a, b = np.cos(w * (t - P)), -np.sin(w * (t - P))
    out += [a, b - a, a + b]
    c, s = np.cos(w * t).T / P, np.sin(w * t).T / P
    out += [c - s, -s, -c]
    tri = np.ones((P, T))
    tri[:, :P] = np.arange(P)[None, :] >= t
    return np.concatenate(out + [tri, (np.arange(P)[None, :] > t)], axis=1).astype(np.float32)


def laid_out(x):
    f = np.ascontiguousarray

    def modes(name):
        return x[name].transpose(0, 2, 1).reshape(NL * NM, H)
    col = lambda a: np.broadcast_to(a.reshape(-1, 1), (P, 1))
    half_pi = np.full((P, 1), np.pi / 2, np.float32)
    zero = np.zeros((P, 1), np.float32)
    return {
        "modes": f(np.stack([modes("L0_attn_A_re_log"), modes("L0_attn_A_im"), modes("L0_attn_C_re"),
                             modes("L0_attn_C_im")], axis=1)),
        "log_dt": f(x["L0_attn_log_dt"]),
        "const": constants(),
        "ident": np.eye(P, dtype=np.float32),
        "ln_w": f(x["L0_attn_ln_w"]),
        "d_skip": f(x["L0_attn_D_skip"].reshape(1, NL * H)),
        "cols": f(np.concatenate([x["L0_attn_ln_b"].T, x["L1_attn_time_mix"].reshape(P, 1),
                                  x["L1_attn_time_decay"], x["L1_attn_time_first"], zero, half_pi,
                                  col(x["L0_ffn_input_scale"]), col(x["L0_ffn_weight_scale"])]
                                 + [np.kron(np.eye(NL), np.ones((NM, 1))).astype(np.float32), zero], axis=1)),
        "x": f(x["L0_attn_x"].reshape(B, C, P, H).transpose(2, 0, 1, 3)),
        "w_glu": f(x["L0_attn_W_out"].transpose(2, 0, 1)),
        "biases": f(np.concatenate([x["L0_attn_b_out"].reshape(-1), x["L0_ffn_bias"].reshape(-1)])),
        "w8": f(x["L0_ffn_weight_fp8"].T),
        "w_attn": f(np.stack([x[f"L1_attn_W{c}"].T for c in "kvro"], axis=1)),
        "w_gate": f(x["L1_ffn_gate_w"].T),
        "w_sgu": f(np.stack([x["L1_ffn_shared_gate"].T, x["L1_ffn_shared_up"].T], axis=1)),
        "w_sd": f(x["L1_ffn_shared_down"].T.reshape(2, P, H).transpose(1, 0, 2)),
        "w_routed": f(np.concatenate([
            np.stack([x["L1_ffn_r_gate"], x["L1_ffn_r_up"]], 1).transpose(3, 0, 1, 2).reshape(P, -1),
            x["L1_ffn_r_down"].transpose(0, 2, 1).reshape(E, 2, P, H).transpose(2, 0, 1, 3).reshape(P, -1)],
            axis=1)),
    }


def kernel(**inputs):
    import concourse.bacc as bacc
    from concourse.bass_utils import run_bass_kernel_spmd

    nc = bacc.Bacc("TRN2", target_bir_lowering=False, num_devices=1)
    arrays = laid_out({k: np.asarray(v) for k, v in inputs.items()})
    d = {k: nc.dram_tensor(f"in_{k}", a.shape, F32, kind="ExternalInput").ap() for k, a in arrays.items()}
    d["out"] = nc.dram_tensor("out", (P, B, C, H), F32, kind="ExternalOutput").ap()
    build(nc, d)
    r = run_bass_kernel_spmd(nc, [{f"in_{k}": a for k, a in arrays.items()}], core_ids=[0])
    return np.ascontiguousarray(r.results[0]["out"].transpose(1, 2, 0, 3)).reshape(B, T, H)
```
